# Optimizing a Trainium2 kernel written in Bass

```python
import numpy as np
import jax
import jax.numpy as jnp

def _softmax(x, axis=-1):
    return jax.nn.softmax(x, axis=axis)

def _gelu(x):
    return jax.nn.gelu(x, approximate=True)

def _silu(x):
    return jax.nn.silu(x)

def _sigmoid(x):
    return jax.nn.sigmoid(x)

def _layernorm(x, axis=-1, eps=1e-05):
    m = jnp.mean(x, axis=axis, keepdims=True)
    v = jnp.var(x, axis=axis, keepdims=True)
    return (x - m) / jnp.sqrt(v + eps)

def _scatter_add(tgt, idx, src, axis=0):
    return tgt.at[idx].add(src)

def _segment_sum(src, seg, n):
    return jax.ops.segment_sum(src, seg, n)
kernel_name = 'mk_gnn_preln_d2_gnn_r8_ed8859'

def setup_inputs(seed: int=0):
    np.random.seed(seed)
    _w = jnp.asarray

    def _rec_inputs():
        import jax
        import jax.numpy as jnp
        _gk = jax.random.key(seed)
        x = -0.000202 + 1 * jax.random.normal(jax.random.fold_in(_gk, 1), (12500, 64), jnp.float32)
        src = jax.random.randint(jax.random.fold_in(_gk, 2), (400000,), 0, 12500, jnp.int32)
        dst = jax.random.randint(jax.random.fold_in(_gk, 3), (400000,), 0, 12500, jnp.int32)
        _o = jnp.argsort(dst, stable=True)
        src = src[_o]
        dst = dst[_o]
        edge_attr_64 = 4.59472e-05 + 1.00006 * jax.random.normal(jax.random.fold_in(_gk, 12), (400000, 64), jnp.float32)
        edge_weight1 = jax.random.uniform(jax.random.fold_in(_gk, 14), (400000, 1), jnp.float32, 0.0, 0.999999)
        return (x, src, dst, edge_attr_64, edge_weight1)
    x, src, dst, edge_attr_64, edge_weight1 = _rec_inputs()

    def _L0_gnn_setup():
        import jax, jax.numpy as jnp
        import numpy as np
        N_NODES = 12500
        N_EDGES = 156250
        D = 64
        key = jax.random.key(seed)
        ks = jax.random.split(key, 8)
        x = jax.random.normal(ks[0], (N_NODES, D), dtype=jnp.float32)
        edge_index = jax.random.randint(ks[1], (2, N_EDGES), 0, N_NODES, dtype=jnp.int64)
        edge_attr = jax.random.normal(ks[2], (N_EDGES, D), dtype=jnp.float32)
        s = 1.0 / np.sqrt(D)
        Wl = jax.random.uniform(ks[3], (D, D), jnp.float32, -s, s)
        bl = jax.random.uniform(ks[4], (D,), jnp.float32, -s, s)
        Wn = jax.random.uniform(ks[5], (D, D), jnp.float32, -s, s)
        bn = jax.random.uniform(ks[6], (D,), jnp.float32, -s, s)
        return {'x': x, 'edge_index': edge_index, 'edge_attr': edge_attr, 'Wl': Wl, 'bl': bl, 'Wn': Wn, 'bn': bn}
    _L0_gnn_all = _L0_gnn_setup()
    _L0_gnn_in = {k: v for k, v in _L0_gnn_all.items() if k in ('Wl', 'bl', 'Wn', 'bn')}
    del _L0_gnn_all

    def _L1_gnn_setup():
        import jax, jax.numpy as jnp
        import numpy as np
        N = 12500
        E = 200000
        H = 4
        C = 16
        D = H * C
        EPS = 1e-05

        def _gat(x, src, dst, ea, W, a_s, a_d, a_e, We, b):
            n = x.shape[0]
            h = (x @ W.T).reshape(n, H, C)
            a_src = jnp.einsum('nhc,hc->nh', h, a_s)
            a_dst = jnp.einsum('nhc,hc->nh', h, a_d)
            ef = (ea @ We.T).reshape(-1, H, C)
            a_edge = jnp.einsum('ehc,hc->eh', ef, a_e)
            alpha = jax.nn.leaky_relu(a_src[src] + a_dst[dst] + a_edge, 0.2)
            amax = jax.ops.segment_max(alpha, dst, num_segments=n)
            ex = jnp.exp(alpha - amax[dst])
            den = jax.ops.segment_sum(ex, dst, num_segments=n)
            alpha = ex / den[dst]
            out = jax.ops.segment_sum(alpha[:, :, None] * h[src], dst, num_segments=n)
            return out.reshape(n, H * C) + b

        def _bn(x, g, b):
            m = x.mean(0)
            v = x.var(0)
            return (x - m) * jax.lax.rsqrt(v + EPS) * g + b
        key = jax.random.key(seed)
        ks = jax.random.split(key, 20)
        s = 0.1
        inp = {'x': jax.random.normal(ks[0], (N, D), dtype=jnp.float32), 'edge_index': jax.random.randint(ks[1], (2, E), 0, N), 'edge_attr': jax.random.uniform(ks[2], (E, 1), dtype=jnp.float32), 'batch': jnp.zeros((N,), dtype=jnp.int64), 'W1': jax.random.normal(ks[3], (H * C, D)) * s, 'as1': jax.random.normal(ks[4], (H, C)) * s, 'ad1': jax.random.normal(ks[5], (H, C)) * s, 'ae1': jax.random.normal(ks[6], (H, C)) * s, 'We1': jax.random.normal(ks[7], (H * C, 1)) * s, 'b1': jnp.zeros((H * C,), dtype=jnp.float32), 'W2': jax.random.normal(ks[8], (H * C, D)) * s, 'as2': jax.random.normal(ks[9], (H, C)) * s, 'ad2': jax.random.normal(ks[10], (H, C)) * s, 'ae2': jax.random.normal(ks[11], (H, C)) * s, 'We2': jax.random.normal(ks[12], (H * C, 1)) * s, 'b2': jnp.zeros((H * C,), dtype=jnp.float32), 'gamma': jnp.ones((D,), dtype=jnp.float32), 'beta': jnp.zeros((D,), dtype=jnp.float32)}
        return inp
    _L1_gnn_all = _L1_gnn_setup()
    _L1_gnn_in = {k: v for k, v in _L1_gnn_all.items() if k in ('W1', 'as1', 'ad1', 'ae1', 'We1', 'b1', 'W2', 'as2', 'ad2', 'ae2', 'We2', 'b2', 'gamma', 'beta')}
    del _L1_gnn_all
    return {'x': x, 'src': src, 'dst': dst, 'edge_attr_64': edge_attr_64, 'edge_weight1': edge_weight1, 'L0_gnn_Wl': _L0_gnn_in['Wl'], 'L0_gnn_bl': _L0_gnn_in['bl'], 'L0_gnn_Wn': _L0_gnn_in['Wn'], 'L0_gnn_bn': _L0_gnn_in['bn'], 'L1_gnn_W1': _L1_gnn_in['W1'], 'L1_gnn_as1': _L1_gnn_in['as1'], 'L1_gnn_ad1': _L1_gnn_in['ad1'], 'L1_gnn_ae1': _L1_gnn_in['ae1'], 'L1_gnn_We1': _L1_gnn_in['We1'], 'L1_gnn_b1': _L1_gnn_in['b1'], 'L1_gnn_W2': _L1_gnn_in['W2'], 'L1_gnn_as2': _L1_gnn_in['as2'], 'L1_gnn_ad2': _L1_gnn_in['ad2'], 'L1_gnn_ae2': _L1_gnn_in['ae2'], 'L1_gnn_We2': _L1_gnn_in['We2'], 'L1_gnn_b2': _L1_gnn_in['b2'], 'L1_gnn_gamma': _L1_gnn_in['gamma'], 'L1_gnn_beta': _L1_gnn_in['beta']}

def reference(x, src, dst, edge_attr_64, edge_weight1, L0_gnn_Wl, L0_gnn_bl, L0_gnn_Wn, L0_gnn_bn, L1_gnn_W1, L1_gnn_as1, L1_gnn_ad1, L1_gnn_ae1, L1_gnn_We1, L1_gnn_b1, L1_gnn_W2, L1_gnn_as2, L1_gnn_ad2, L1_gnn_ae2, L1_gnn_We2, L1_gnn_b2, L1_gnn_gamma, L1_gnn_beta):
    import jax
    import jax.numpy as jnp

    def _L0_gnn_ref(x, edge_index, edge_attr, Wl, bl, Wn, bn):
        import jax, jax.numpy as jnp
        import numpy as np
        N_NODES = 12500
        N_EDGES = 156250
        D = 64
        src = edge_index[0]
        dst = edge_index[1]
        e_proj = edge_attr @ Wl + bl
        msg = jax.nn.relu(x[src] + e_proj)
        agg = jax.ops.segment_sum(msg, dst, num_segments=x.shape[0])
        return (x + agg) @ Wn + bn

    def _L1_gnn_ref(x, edge_index, edge_attr, batch, W1, as1, ad1, ae1, We1, b1, W2, as2, ad2, ae2, We2, b2, gamma, beta):
        import jax, jax.numpy as jnp
        import numpy as np
        N = 12500
        E = 200000
        H = 4
        C = 16
        D = H * C
        EPS = 1e-05

        def _gat(x, src, dst, ea, W, a_s, a_d, a_e, We, b):
            n = x.shape[0]
            h = (x @ W.T).reshape(n, H, C)
            a_src = jnp.einsum('nhc,hc->nh', h, a_s)
            a_dst = jnp.einsum('nhc,hc->nh', h, a_d)
            ef = (ea @ We.T).reshape(-1, H, C)
            a_edge = jnp.einsum('ehc,hc->eh', ef, a_e)
            alpha = jax.nn.leaky_relu(a_src[src] + a_dst[dst] + a_edge, 0.2)
            amax = jax.ops.segment_max(alpha, dst, num_segments=n)
            ex = jnp.exp(alpha - amax[dst])
            den = jax.ops.segment_sum(ex, dst, num_segments=n)
            alpha = ex / den[dst]
            out = jax.ops.segment_sum(alpha[:, :, None] * h[src], dst, num_segments=n)
            return out.reshape(n, H * C) + b

        def _bn(x, g, b):
            m = x.mean(0)
            v = x.var(0)
            return (x - m) * jax.lax.rsqrt(v + EPS) * g + b
        n = x.shape[0]
        loops = jnp.arange(n)
        src = jnp.concatenate([edge_index[0], loops])
        dst = jnp.concatenate([edge_index[1], loops])
        ea = jnp.concatenate([edge_attr, jnp.broadcast_to(edge_attr.mean(0, keepdims=True), (n, edge_attr.shape[1]))])
        out = jax.nn.relu(_bn(_gat(x, src, dst, ea, W1, as1, ad1, ae1, We1, b1), gamma, beta))
        out = _bn(_gat(out, src, dst, ea, W2, as2, ad2, ae2, We2, b2), gamma, beta)
        return jax.nn.relu(out + x)
    edge_index = jnp.stack([src, dst])
    batch0 = jnp.zeros((12500,), jnp.int32)
    h = jnp.maximum(_layernorm(x, axis=-1), 0.0)
    x = x + _L0_gnn_ref(h, edge_index, edge_attr_64, L0_gnn_Wl, L0_gnn_bl, L0_gnn_Wn, L0_gnn_bn)
    h = jnp.maximum(_layernorm(x, axis=-1), 0.0)
    x = x + _L1_gnn_ref(h, edge_index, edge_weight1, batch0, L1_gnn_W1, L1_gnn_as1, L1_gnn_ad1, L1_gnn_ae1, L1_gnn_We1, L1_gnn_b1, L1_gnn_W2, L1_gnn_as2, L1_gnn_ad2, L1_gnn_ae2, L1_gnn_We2, L1_gnn_b2, L1_gnn_gamma, L1_gnn_beta)
    return x

_drawn_inputs = setup_inputs


def setup_inputs(seed=0):
    import zlib

    import numpy as np

    out = dict(_drawn_inputs(seed))
    spreads = {'L1_gnn_b1': (0.0, 0.8),
     'L1_gnn_b2': (0.0, 0.8),
     'L1_gnn_gamma': (1.0, 0.6),
     'L1_gnn_beta': (0.0, 0.78)}
    factors = {'edge_weight1': 8.0,
     'L0_gnn_bn': 7.301,
     'L1_gnn_as1': 8.0,
     'L1_gnn_ad1': 8.0,
     'L1_gnn_ae1': 8.0,
     'L1_gnn_We1': 8.0,
     'L1_gnn_as2': 5.613,
     'L1_gnn_ad2': 8.0,
     'L1_gnn_ae2': 8.0,
     'L1_gnn_We2': 8.0}
    for name, (base, spread) in spreads.items():
        noise = np.random.default_rng([zlib.crc32(name.encode()), seed]).standard_normal(out[name].shape)
        drawn = base * np.exp(spread * noise) if base else spread * noise
        out[name] = jnp.asarray(drawn.astype(out[name].dtype))
    for name, factor in factors.items():
        out[name] = (out[name] * factor).astype(out[name].dtype)
    return out
```

```python
import concourse.bass as bass
from concourse import mybir
from contextlib import ExitStack

P = 128
N = 12500
E = 400000
D = 64
H, C = 4, 16
CHUNK = E // P
G = 25
GROUPS = CHUNK // G
PAIRS = GROUPS // 2
NP, NJ = 125, 100
HC = C + 1
ACC = H * HC
ROW = ACC + H
PROJ = ROW + H
NB = 4
BATCHES = NJ // NB
SUPER, BLOCKS, BLOCK = 100, 80, 50
NEG = -1.0e30
SKIP = float(1 << 20)
LN_EPS = 1e-05
BN_EPS = 1e-05

F32 = mybir.dt.float32
I32 = mybir.dt.int32
U32 = mybir.dt.uint32
ALU = mybir.AluOpType
ACT = mybir.ActivationFunctionType
AX = mybir.AxisListType


def along(ap, axis, count):
    shape = list(ap.shape)
    return ap.unsqueeze(axis).broadcast_to(shape[:axis] + [count] + shape[axis:])


class Memory:

    def __init__(self, nc, ctx, ins):
        def sb(name, shape, dt=F32):
            return ctx.enter_context(nc.sbuf_tensor(name, shape, dt))

        def dram(name, shape, dt=F32):
            return nc.dram_tensor(name, shape, dt).ap()

        self.ins = ins
        self.relu_table = dram("relu_table", (N, D))
        self.edge_sums = dram("edge_sums", (E, D))
        self.att_table = dram("att_table", (N, ROW))
        self.adst_table = dram("adst_table", (N, H))
        self.adst_edges = dram("adst_edges", (E, H))
        self.edge_rows = dram("edge_rows", (E, ROW))
        self.counts = dram("counts", (N + 1, 1))

        self.ident = sb("ident", [P, P])
        self.ones = sb("ones", [P, P])
        self.head_mask = sb("head_mask", [D, H])
        self.w_edge = sb("w_edge", [D, D])
        self.w_node = sb("w_node", [D, D])
        self.w_att = [sb(f"w_att{i}", [D, D]) for i in range(2)]
        self.heads = [sb(f"heads{i}", [D, 4]) for i in range(2)]
        self.place = [sb(f"place{i}", [D, PROJ]) for i in range(2)]
        self.w_ext = [sb(f"w_ext{i}", [D, PROJ]) for i in range(2)]
        self.we_prod = [sb(f"we_prod{i}", [D, P]) for i in range(2)]
        self.c_edge = [sb(f"c_edge{i}", [P, H]) for i in range(2)]
        self.rows = sb("rows", [NP, 6, D])
        self.w_mean = sb("w_mean", [P, 1])

        self.keep = sb("keep", [P, CHUNK])
        self.ends = sb("ends", [P, 2], I32)
        self.cont = sb("cont", [ACC, P])
        self.through = sb("through", [ACC, P])
        self.chunk_end = sb("chunk_end", [P, 1])
        self.fix_from = sb("fix_from", [P, 1], U32)
        self.fix_to = sb("fix_to", [P, 1], U32)
        self.first_dst = sb("first_dst", [P, 1], U32)
        self.full = sb("full", [NP, NJ])
        self.last_row = sb("last_row", [NP, NJ], U32)
        self.start_row = sb("start_row", [NP, NJ], U32)
        self.node_id = sb("node_id", [NP, NJ], I32)
        self.stat = sb("stat", [P, 4, NJ])
        self.cols = sb("cols", [P, 8, D])
        self.chunk_tmp = sb("chunk_tmp", [P, 6, P])

        self.x_nodes = sb("x_nodes", [NP, NJ, D])
        self.h_nodes = sb("h_nodes", [NP, NJ, D])
        self.aside = sb("aside", [NP, NJ, H])
        self.aself = sb("aself", [NP, NJ, H])

        self.work = sb("work", [P, 16000])
        self.stream = sb("stream", [P, 2 * G * P])
        self.idx = sb("idx", [P, 2, G], U32)
        self.psum = ctx.enter_context(nc.psum_tensor("psum", [P, 4096], F32))

    def area(self, at, *shape, parts=P, dt=F32, of=None):
        size = 1
        for s in shape:
            size *= s
        v = (self.work if of is None else of)[0:parts, at:at + size]
        if dt is not F32:
            v = v.bitcast(dt)
        names = "abcd"[:len(shape)]
        if len(shape) > 1:
            v = v.rearrange("p (" + " ".join(names) + ") -> p " + " ".join(names),
                            **{n: s for n, s in zip(names, shape)})
        return v


def run(eng, body):
    with eng.Fori(0, PAIRS) as i:
        for k in range(2):
            body(k, 2 * i + k, i)
    body(0, 2 * PAIRS, PAIRS)


def layer_norm(nc, dve, x, y, sq, stat, std_wanted, std_ready, nth):
    total, mean, var, rstd = (stat[0:NP, i, :] for i in range(4))
    nc.vector.tensor_reduce(total, x, AX.X, ALU.add)
    dve.drain()
    nc.vector.tensor_scalar(mean, total, 1.0 / D, None, ALU.mult)
    dve.drain()
    nc.vector.tensor_tensor(y, x, along(mean, 2, D), ALU.subtract)
    dve.drain()
    nc.vector.tensor_tensor(sq, y, y, ALU.mult)
    dve.drain()
    nc.vector.tensor_reduce(total, sq, AX.X, ALU.add)
    dve.drain()
    nc.vector.tensor_scalar(var, total, 1.0 / D, LN_EPS, ALU.mult, ALU.add).then_inc(std_wanted, 1)
    dve.wait_ge(std_ready, nth)
    nc.vector.reciprocal(rstd, var)
    dve.drain()
    nc.vector.scalar_tensor_tensor(y, y, 0.0, along(rstd, 2, D), ALU.max, ALU.mult)
    dve.drain()


def standard_deviation(nc, act, stat, std_wanted, std_ready, nth):
    act.wait_ge(std_wanted, nth)
    nc.scalar.activation(stat[0:NP, 2, :], stat[0:NP, 2, :], ACT.Sqrt).then_inc(std_ready, 1)


def setup(nc, m, ctx):
    ins = m.ins

    def sem(name):
        return ctx.enter_context(nc.semaphore(name))

    weights_in = sem("weights_in")
    x_in = sem("x_in")
    dst_in = sem("dst_in")
    ew_in = sem("ew_in")
    supers_in = sem("supers_in")
    ids_ready = sem("ids_ready")
    zeros_ready = sem("zeros_ready")
    adst_cleared = sem("adst_cleared")
    std_wanted = sem("std_wanted")
    std_ready = sem("std_ready")
    table_ready = sem("table_ready")
    table_out = sem("table_out")
    supers_found = sem("supers_found")
    blocks_in = sem("blocks_in")
    blocks_found = sem("blocks_found")
    edges_in = sem("edges_in")
    counts_ready = sem("counts_ready")
    counts_out = sem("counts_out")
    starts_in = sem("starts_in")
    fix_in = sem("fix_in")
    parts_ready = sem("parts_ready")
    products_ready = sem("products_ready")
    ends_ready = sem("ends_ready")
    ends_spread = sem("ends_spread")

    dst_all = m.area(0, CHUNK, dt=I32)
    ew_all = m.area(CHUNK, CHUNK)
    zeros = m.area(NJ * SUPER, 500)
    supers = m.area(NJ * SUPER + 500, SUPER, parts=NP, dt=I32)
    level = m.area(0, NJ, SUPER, parts=NP)
    level_b = m.area(0, NJ, BLOCKS, parts=NP, dt=I32)
    level_c = m.area(0, NJ, BLOCK, parts=NP, dt=I32)
    sq = m.area(0, NJ, D, parts=NP, of=m.stream)
    index = m.area(0, NJ, parts=NP, dt=U32, of=m.chunk_tmp[:, :, :].rearrange("p a b -> p (a b)"))
    found = m.stat[0:NP, 0, :]
    block = m.stat[0:NP, 1, :]
    count = m.stat[0:NP, 2, :]
    start = m.stat[0:NP, 3, :]
    ends_f = m.cols[:, 0, 0:2]
    ends_b = m.chunk_tmp[:, 0:2, 0:ACC]
    fix = m.cols[:, 1, 0:4]
    wsum = m.cols[:, 2, 0:1]
    dst_v = ins["dst"].rearrange("(p f) -> p f", p=P)
    psum_ends = m.psum[0:ACC, 0:2 * P].rearrange("p (a b) -> p a b", a=2)
    psum_ext = m.psum[0:D, 512:512 + 2 * PROJ].rearrange("p (a b) -> p a b", a=2)
    psum_c = m.psum[:, 1024:1024 + 2 * H].rearrange("p (a b) -> p a b", a=2)
    psum_w = m.psum[:, 1536:1537]

    with nc.Block() as blk:

        @blk.sync
        def _(sp):
            sp.dma_start(m.x_nodes[:, :, :], ins["x"].rearrange("(p j) c -> p j c", p=NP)).then_inc(x_in, 16)
            sp.dma_start(dst_all, dst_v).then_inc(dst_in, 16)
            sp.dma_start(ew_all, ins["edge_weight1"].rearrange("(p f) o -> p (f o)", p=P)).then_inc(ew_in, 16)
            sp.dma_start(supers, ins["dst_supers"].rearrange("(o a) -> o a", o=1).broadcast_to([NP, SUPER])).then_inc(supers_in, 16)
            sp.wait_ge(zeros_ready, 1)
            sp.dma_start(m.adst_edges.rearrange("(p k f) h -> p k (f h)", p=P, k=25),
                         along(zeros, 1, 25)).then_inc(adst_cleared, 16)
            sp.wait_ge(table_ready, 1)
            sp.dma_start(m.relu_table.rearrange("(p j) c -> p j c", p=NP), sq).then_inc(table_out, 16)
            sp.wait_ge(counts_ready, 1)
            sp.dma_start(m.counts[1:N + 1, :].rearrange("(p j) o -> p (j o)", p=NP), count).then_inc(counts_out, 16)
            sp.dma_start(m.counts[0:1, :], zeros[0:1, 0:1]).then_inc(counts_out, 16)
            sp.wait_ge(counts_out, 32)
            sp.dma_start(start, m.counts[0:N, :].rearrange("(p j) o -> p (j o)", p=NP)).then_inc(starts_in, 16)
            sp.wait_ge(table_out, 16)
            sp.wait_ge(adst_cleared, 16)

        @blk.gpsimd
        def _(pool):
            nc.gpsimd.iota(m.node_id[:, :], pattern=[[1, NJ]], base=0, channel_multiplier=NJ).then_inc(ids_ready, 1)
            pool.wait_ge(supers_found, 1)
            for j in range(NJ):
                pool.indirect_dma_start(level_b[:, j, :], None, ins["dst_blocks"],
                                        bass.IndirectOffsetOnAxis(index[:, j:j + 1], 0)).then_inc(blocks_in, 16)
            pool.wait_ge(blocks_found, 1)
            for j in range(NJ):
                pool.indirect_dma_start(level_c[:, j, :], None, ins["dst"].rearrange("(a b) -> a b", b=BLOCK),
                                        bass.IndirectOffsetOnAxis(index[:, j:j + 1], 0)).then_inc(edges_in, 16)
            pool.wait_ge(counts_out, 32)
            pool.indirect_dma_start(fix[:, 0:1], None, m.counts,
                                    bass.IndirectOffsetOnAxis(m.first_dst[:, :], 0)).then_inc(fix_in, 16)

        @blk.scalar
        def _(act):
            def load(to, what):
                act.dma_start(to, what).then_inc(weights_in, 16)

            load(m.ident[:, :], ins["ident"])
            load(m.head_mask[:, :], ins["head_mask"])
            load(m.chunk_end[:, :], ins["chunk_ends"])
            load(m.w_edge[:, :], ins["L0_gnn_Wl"])
            load(m.w_node[:, :], ins["L0_gnn_Wn"])
            for i in range(2):
                load(m.w_att[i][:, :], ins[f"L1_gnn_W{i + 1}"])
                load(m.place[i][:, 0:ACC], ins["place"])
                for k, name in enumerate(("as", "ad", "ae")):
                    load(m.heads[i][:, k:k + 1], ins[f"L1_gnn_{name}{i + 1}"].rearrange("h (c o) -> (h c) o", o=1))
                load(m.heads[i][:, 3:4], ins[f"L1_gnn_We{i + 1}"])
            for k, name in enumerate(("L0_gnn_bl", "L0_gnn_bn", "L1_gnn_b1", "L1_gnn_b2", "L1_gnn_gamma", "L1_gnn_beta")):
                load(m.rows[:, k, :], ins[name].rearrange("(o a) -> o a", o=1).broadcast_to([NP, D]))
            standard_deviation(nc, act, m.stat, std_wanted, std_ready, 1)

        @blk.tensor
        def _(pe):
            pe.wait_ge(parts_ready, 1)
            for i in range(2):
                nc.tensor.matmul(psum_ext[:, i, :], m.w_att[i][:, :], m.place[i][:, :], start=True, stop=True)
                nc.tensor.matmul(psum_c[:, i, :], m.we_prod[i][:, :], m.head_mask[:, :], start=True, stop=True)
            nc.tensor.matmul(psum_w, m.ones[:, :], wsum, start=True, stop=True).then_inc(products_ready, 1)
            pe.wait_ge(ends_ready, 1)
            nc.tensor.matmul(psum_ends[:, 0, :], ends_b[:, 0, :], m.ident[:, :], start=True, stop=True)
            nc.tensor.matmul(psum_ends[:, 1, :], ends_b[:, 1, :], m.ident[:, :], start=True, stop=True).then_inc(ends_spread, 1)

        @blk.vector
        def _(dve):
            nc.vector.memset(zeros, 0.0).then_inc(zeros_ready, 1)
            nc.vector.memset(m.ones[:, :], 1.0)
            dve.wait_ge(dst_in, 16)
            nc.vector.memset(m.keep[:, 0:1], 0.0)
            nc.vector.tensor_tensor(m.keep[:, 1:CHUNK], dst_all[:, 1:CHUNK], dst_all[:, 0:CHUNK - 1], ALU.is_equal)
            for k, f in enumerate((0, CHUNK - 1)):
                nc.vector.tensor_copy(m.ends[:, k:k + 1], dst_all[:, f:f + 1])
                nc.vector.tensor_copy(ends_f[:, k:k + 1], dst_all[:, f:f + 1])
            dve.drain()
            for k in range(2):
                nc.vector.tensor_copy(ends_b[:, k, :], ends_f[:, k:k + 1].broadcast_to([P, ACC]))
            dve.drain()
            nc.vector.tensor_scalar(m.first_dst[:, :], ends_f[:, 0:1], 1.0, None, ALU.add).then_inc(ends_ready, 1)
            dve.wait_ge(ew_in, 16)
            nc.vector.tensor_reduce(wsum, ew_all, AX.X, ALU.add)
            dve.wait_ge(weights_in, 16 * (5 + 2 * 6 + 6))
            for i in range(2):
                for k in range(2):
                    nc.vector.tensor_scalar(m.place[i][:, ACC + k * H:ACC + (k + 1) * H], m.head_mask[:, :],
                                            m.heads[i][:, k:k + 1], None, ALU.mult)
                nc.vector.tensor_tensor(m.we_prod[i][:, :], m.heads[i][:, 2:3].broadcast_to([D, P]),
                                        m.heads[i][:, 3:4].broadcast_to([D, P]), ALU.mult)
            dve.drain()
            dve.sem_inc(parts_ready, 1)
            dve.wait_ge(products_ready, 1)
            for i in range(2):
                nc.vector.tensor_copy(m.w_ext[i][:, :], psum_ext[:, i, :])
                nc.vector.tensor_copy(m.c_edge[i][:, :], psum_c[:, i, :])
            nc.vector.tensor_scalar(m.w_mean[:, :], psum_w, 1.0 / E, None, ALU.mult)
            dve.wait_ge(ends_spread, 1)
            last = m.chunk_tmp[0:ACC, 2, :]
            nc.vector.tensor_copy(last, psum_ends[:, 1, :])
            nc.vector.memset(m.cont[:, 0:1], 0.0)
            dve.drain()
            nc.vector.tensor_tensor(m.cont[:, 1:P], psum_ends[:, 0, 1:P], last[:, 0:P - 1], ALU.is_equal)
            nc.vector.tensor_tensor(m.through[:, :], psum_ends[:, 0, :], last, ALU.is_equal)
            dve.drain()
            nc.vector.tensor_tensor(m.through[:, :], m.through[:, :], m.cont[:, :], ALU.mult)
            dve.wait_ge(x_in, 16)
            layer_norm(nc, dve, m.x_nodes[:, :, :], m.h_nodes[:, :, :], sq, m.stat, std_wanted, std_ready, 1)
            nc.vector.tensor_tensor(sq, m.h_nodes[:, :, :], along(m.rows[:, 0, :], 1, NJ), ALU.add).then_inc(table_ready, 1)
            dve.wait_ge(supers_in, 16)
            dve.wait_ge(ids_ready, 1)
            nc.vector.tensor_tensor(level, along(m.node_id[:, :], 2, SUPER), along(supers, 1, NJ), ALU.is_ge)
            dve.drain()
            nc.vector.tensor_reduce(found, level, AX.X, ALU.add)
            dve.drain()
            nc.vector.tensor_scalar(found, found, float(SUPER - 1), None, ALU.min)
            dve.drain()
            nc.vector.tensor_copy(index, found).then_inc(supers_found, 1)
            dve.wait_ge(blocks_in, 16 * NJ)
            nc.vector.tensor_tensor(level_b, along(m.node_id[:, :], 2, BLOCKS), level_b, ALU.is_ge)
            dve.drain()
            nc.vector.tensor_reduce(block, level_b, AX.X, ALU.add)
            dve.drain()
            nc.vector.scalar_tensor_tensor(block, found, float(BLOCKS), block, ALU.mult, ALU.add)
            dve.drain()
            nc.vector.tensor_scalar(block, block, float(SUPER * BLOCKS - 1), None, ALU.min)
            dve.drain()
            nc.vector.tensor_copy(index, block).then_inc(blocks_found, 1)
            dve.wait_ge(edges_in, 16 * NJ)
            nc.vector.tensor_tensor(level_c, along(m.node_id[:, :], 2, BLOCK), level_c, ALU.is_ge)
            dve.drain()
            nc.vector.tensor_reduce(count, level_c, AX.X, ALU.add)
            dve.drain()
            nc.vector.scalar_tensor_tensor(count, block, float(BLOCK), count, ALU.mult, ALU.add)
            dve.drain()
            dve.sem_inc(counts_ready, 1)
            nc.vector.tensor_scalar(found, count, -1.0, 0.0, ALU.add, ALU.max)
            dve.drain()
            nc.vector.tensor_copy(m.last_row[:, :], found)
            dve.wait_ge(starts_in, 16)
            nc.vector.tensor_tensor(m.full[:, :], count, start, ALU.is_gt)
            dve.drain()
            nc.vector.tensor_scalar(found, m.full[:, :], -SKIP, SKIP, ALU.mult, ALU.add)
            dve.drain()
            nc.vector.tensor_tensor(found, found, start, ALU.add)
            dve.drain()
            nc.vector.tensor_copy(m.start_row[:, :], found)
            dve.wait_ge(fix_in, 16)
            nc.vector.tensor_scalar(fix[:, 1:2], fix[:, 0:1], m.chunk_end[:, :], None, ALU.is_gt)
            dve.drain()
            nc.vector.tensor_scalar(fix[:, 2:3], fix[:, 0:1], m.chunk_end[:, :], -1.0, ALU.min, ALU.add)
            dve.drain()
            nc.vector.tensor_copy(m.fix_from[:, :], fix[:, 2:3])
            nc.vector.scalar_tensor_tensor(fix[:, 3:4], fix[:, 1:2], SKIP, fix[:, 2:3], ALU.mult, ALU.add)
            dve.drain()
            nc.vector.tensor_copy(m.fix_to[:, :], fix[:, 3:4])
            nc.vector.tensor_copy(m.first_dst[:, :], m.ends[:, 0:1])


def message_edges(nc, m, ctx):
    ins = m.ins

    def sem(name):
        return ctx.enter_context(nc.semaphore(name))

    idx_in = [sem(f"l0_idx_in{k}") for k in range(2)]
    attr_in = [sem(f"l0_attr_in{k}") for k in range(2)]
    gathered = [sem(f"l0_gathered{k}") for k in range(2)]
    projected = [sem(f"l0_projected{k}") for k in range(2)]
    added = [sem(f"l0_added{k}") for k in range(2)]
    terms_ready = sem("l0_terms_ready")
    scanned = sem("l0_scanned")
    rows_ready = sem("l0_rows_ready")
    stored = [sem(f"l0_stored{k}") for k in range(2)]
    turn = sem("l0_turn")

    W = G + 1
    attr = [m.area(k * G * P, G, P, parts=D, of=m.stream) for k in range(2)]
    rows_g = [m.area(k * G * D, G, D) for k in range(2)]
    at = 2 * G * D
    total = m.area(at, G, D)
    at += G * D
    keeps = m.area(at, D, W)
    at += D * W
    terms = m.area(at, D, W)
    at += D * W
    sums = [m.area(at + k * D * W, D, W) for k in range(2)]
    at += 2 * D * W
    rows_out = [m.area(at + k * G * D, G, D) for k in range(2)]
    proj = [m.psum[:, k * 2048:k * 2048 + G * D] for k in range(2)]
    src_v = ins["src"].bitcast(U32).rearrange("(p f) -> p f", p=P)
    out_v = m.edge_sums.rearrange("(p f) c -> p f c", p=P)

    with nc.Block() as blk:

        @blk.sync
        def _(sp):
            def body(k, g, n):
                sp.wait_ge(added[k], n + 1)
                sp.sem_inc(turn, 1)
                sp.dma_start(m.idx[:, k, :], src_v[:, bass.ds(g * G, G)]).then_inc(idx_in[k], 16)
                sp.dma_start(attr[k], ins["edge_attr"][:, bass.ds(g * G, G), :]).then_inc(attr_in[k], 16)

            run(sp, body)

        @blk.gpsimd
        def _(pool):
            def body(k, g, n):
                pool.wait_ge(idx_in[k], 16 * (n + 1))
                pool.sem_inc(turn, 1)
                for t in range(G):
                    pool.indirect_dma_start(rows_g[k][:, t, :], None, m.relu_table,
                                            bass.IndirectOffsetOnAxis(m.idx[:, k, t:t + 1], 0)).then_inc(gathered[k], 16)

            run(pool, body)

        @blk.tensor
        def _(pe):
            def body(k, g, n):
                pe.wait_ge(added[k], n + 1)
                pe.wait_ge(attr_in[k], 16 * (n + 1))
                for t in range(G):
                    last = nc.tensor.matmul(proj[k][:, t * D:(t + 1) * D], attr[k][:, t, :], m.w_edge[:, :],
                                            start=True, stop=True)
                last.then_inc(projected[k], 1)

            run(pe, body)

        @blk.scalar
        def _(act):
            def body(k, g, n):
                act.wait_ge(scanned, g + 1)
                nc.scalar.activation(keeps[:, :, 1:W], along(m.keep[:, bass.ds(g * G, G)], 1, D), ACT.Copy)
                act.wait_ge(added[k], n + 2)
                nc.scalar.activation(terms[:, :, 1:W], total.rearrange("p g c -> p c g"), ACT.Relu).then_inc(terms_ready, 1)
                act.wait_ge(scanned, g + 2)
                nc.scalar.activation(rows_out[k], sums[k][:, :, 1:W].rearrange("p c g -> p g c"), ACT.Copy).then_inc(rows_ready, 1)
                act.wait_ge(rows_ready, g + 1)
                act.dma_start(out_v[:, bass.ds(g * G, G), :], rows_out[k]).then_inc(stored[k], 16)

            with act.Fori(0, PAIRS) as i:
                for k in range(2):
                    body(k, 2 * i + k, i)
                for k in range(2):
                    act.wait_ge(stored[k], 16 * (i + 1))
            body(0, 2 * PAIRS, PAIRS)
            act.wait_ge(stored[0], 16 * (PAIRS + 1))

        @blk.vector
        def _(dve):
            nc.vector.memset(keeps[:, :, 0:1], 0.0)
            nc.vector.memset(sums[1][:, :, G:W], 0.0)
            dve.drain()
            for k in range(2):
                dve.sem_inc(added[k], 1)
            dve.sem_inc(scanned, 1)

            def body(k, g, n):
                dve.wait_ge(gathered[k], 16 * G * (n + 1))
                dve.wait_ge(projected[k], n + 1)
                nc.vector.tensor_tensor(total.rearrange("p g c -> p (g c)"), rows_g[k].rearrange("p g c -> p (g c)"),
                                        proj[k], ALU.add).then_inc(added[k], 1)
                dve.drain()
                nc.vector.tensor_copy(terms[:, :, 0:1], sums[1 - k][:, :, G:W])
                dve.drain()
                dve.wait_ge(terms_ready, g + 1)
                nc.vector.tensor_tensor_scan(sums[k].rearrange("p c g -> p (c g)"), keeps.rearrange("p c g -> p (c g)"),
                                             terms.rearrange("p c g -> p (c g)"), 0.0, ALU.mult, ALU.add).then_inc(scanned, 1)

            run(dve, body)


class Projection:

    def __init__(self, nc, m, sem, name, weight, cols):
        at = 2 * NJ * ROW
        self.nc, self.m, self.weight, self.cols = nc, m, weight, cols
        self.rows = [m.area(at + k * NB * D, NB, D, parts=NP) for k in range(2)]
        at += 2 * NB * D
        self.flipped = [m.area(at + k * NB * NP, NB, NP, parts=D) for k in range(2)]
        self.flipped_ps = [m.psum[0:D, k * 512:k * 512 + NB * NP].rearrange("p (a b) -> p a b", a=NB) for k in range(2)]
        self.product = [m.psum[0:NP, 1024 + k * 512:1024 + k * 512 + NB * cols].rearrange("p (a b) -> p a b", a=NB)
                        for k in range(2)]
        self.rows_ready = sem(f"{name}_rows_ready")
        self.flipped_ready = sem(f"{name}_flipped_ready")
        self.flipped_out = sem(f"{name}_flipped_out")
        self.product_ready = sem(f"{name}_product_ready")
        self.turn = sem(f"{name}_turn")

    def vector(self, dve, bring, take):
        bring(0, 0).then_inc(self.rows_ready, 1)

        def step(k, b):
            bring(1 - k, b + 1).then_inc(self.rows_ready, 1)
            dve.wait_ge(self.product_ready, b + 1)
            take(k, b)

        with dve.Fori(0, BATCHES // 2) as i:
            for k in range(2):
                step(k, 2 * i + k)
        dve.wait_ge(self.product_ready, BATCHES)
        take(0, BATCHES - 1)
        dve.drain()

    def tensor(self, pe):
        def flip(k, b):
            pe.wait_ge(self.rows_ready, b + 1)
            pe.sem_inc(self.turn, 1)
            for q in range(NB):
                last = self.nc.tensor.transpose(self.flipped_ps[k][:, q, :], self.rows[k][:, q, :], self.m.ident[0:NP, 0:NP])
            last.then_inc(self.flipped_ready, 1)

        def multiply(k, b):
            pe.wait_ge(self.flipped_out, b + 1)
            for q in range(NB):
                last = self.nc.tensor.matmul(self.product[k][:, q, :], self.flipped[k][:, q, :], self.weight,
                                             start=True, stop=True)
            last.then_inc(self.product_ready, 1)

        flip(0, 0)
        with pe.Fori(0, BATCHES // 2) as i:
            for k in range(2):
                flip(1 - k, 2 * i + k + 1)
                multiply(k, 2 * i + k)
        multiply(0, BATCHES - 1)

    def scalar(self, act):
        def step(k, b):
            act.wait_ge(self.flipped_ready, b + 1)
            self.nc.scalar.activation(self.flipped[k], self.flipped_ps[k], ACT.Copy).then_inc(self.flipped_out, 1)

        with act.Fori(0, BATCHES // 2) as i:
            for k in range(2):
                step(k, 2 * i + k)
        step(0, BATCHES - 1)


class AttentionTable:

    def __init__(self, nc, m, sem, layer):
        self.nc, self.m, self.layer = nc, m, layer
        self.table = m.area(NJ * ROW, NJ, ROW, parts=NP)
        self.project = Projection(nc, m, sem, f"att{layer}", m.w_ext[layer][:, :], PROJ)
        self.ready = sem(f"att{layer}_table_ready")
        self.out = sem(f"att{layer}_table_out")
        self.starts_out = sem(f"att{layer}_starts_out")
        self.first_in = sem(f"att{layer}_first_in")
        self.first_out = sem(f"att{layer}_first_out")
        self.first = m.cols[:, 7, 0:H]

    def vector(self, dve, source):
        nc, m, project = self.nc, self.m, self.project

        def bring(k, b):
            return nc.vector.tensor_copy(project.rows[k], source[:, bass.ds(b * NB, NB), :])

        def take(k, b):
            nc.vector.tensor_copy(self.table[:, bass.ds(b * NB, NB), :], project.product[k][:, :, 0:ROW])
            nc.vector.tensor_copy(m.aside[:, bass.ds(b * NB, NB), :], project.product[k][:, :, ROW:PROJ])

        project.vector(dve, bring, take)
        heads = self.table[:, :, 0:ACC].rearrange("p j (h c) -> p j h c", h=H)
        for h in range(H):
            nc.vector.memset(heads[:, :, h, C:HC], 1.0)
        dve.drain()
        dve.sem_inc(self.ready, 1)
        loop = m.cols[0:NP, 6, 0:H]
        nc.vector.tensor_scalar(loop, m.c_edge[self.layer][0:NP, :], m.w_mean[0:NP, :], None, ALU.mult)
        nc.vector.tensor_tensor(m.aself[:, :, :], self.table[:, :, ACC:ROW], m.aside[:, :, :], ALU.add)
        dve.drain()
        nc.vector.tensor_tensor(m.aself[:, :, :], m.aself[:, :, :], along(loop, 1, NJ), ALU.add)
        dve.drain()
        flat = m.aself[:, :, :].rearrange("p j h -> p (j h)")
        nc.vector.scalar_tensor_tensor(flat, flat, 0.2, flat, ALU.mult, ALU.max)

    def gpsimd(self, pool):
        m = self.m
        pool.wait_ge(self.ready, 1)
        for j in range(NJ):
            pool.indirect_dma_start(m.adst_edges, bass.IndirectOffsetOnAxis(m.start_row[:, j:j + 1], 0),
                                    m.aside[:, j, :], None, bounds_check=E - 1, oob_is_err=False).then_inc(self.starts_out, 16)
        pool.wait_ge(self.out, 32)
        pool.indirect_dma_start(self.first, None, m.adst_table,
                                bass.IndirectOffsetOnAxis(m.first_dst[:, :], 0)).then_inc(self.first_in, 16)

    def sync(self, sp):
        m = self.m
        sp.wait_ge(self.ready, 1)
        sp.dma_start(m.att_table.rearrange("(p j) c -> p j c", p=NP), self.table).then_inc(self.out, 16)
        sp.dma_start(m.adst_table.rearrange("(p j) c -> p j c", p=NP), m.aside[:, :, :]).then_inc(self.out, 16)
        sp.wait_ge(self.starts_out, 16 * NJ)
        sp.wait_ge(self.first_in, 16)
        sp.dma_start(m.adst_edges.rearrange("(p f) h -> p f h", p=P)[:, 0, :], self.first).then_inc(self.first_out, 16)
        sp.wait_ge(self.out, 32)
        sp.wait_ge(self.first_out, 16)


def message_nodes(nc, m, ctx):

    def sem(name):
        return ctx.enter_context(nc.semaphore(name))

    fix_in = sem("l0_fix_in")
    fix_ready = sem("l0_fix_ready")
    fix_out = sem("l0_fix_out")
    tail_ready = sem("l0_tail_ready")
    tail_flipped = sem("l0_tail_flipped")
    carry_ready = sem("l0_carry_ready")
    carry_flipped = sem("l0_carry_flipped")
    node_in = sem("l0_node_in")
    std_wanted = sem("l1_std_wanted")
    std_ready = sem("l1_std_ready")
    project = Projection(nc, m, sem, "l0_node", m.w_node[:, :], D)
    table = AttentionTable(nc, m, sem, 0)

    W = G + 1
    last_sums = m.area(3 * G * D + 2 * D * W, D, W)
    agg = m.area(0, NJ, D, parts=NP)
    sq = m.area(0, NJ, D, parts=NP, of=m.stream)
    tail, tail_t, run_t, carry_t = (m.chunk_tmp[:, i, :] for i in range(4))
    fix = m.cols[:, 0, :]
    ps_tail = m.psum[0:D, 2048:2048 + P]
    ps_carry = m.psum[:, 2560:2560 + D]

    with nc.Block() as blk:

        @blk.gpsimd
        def _(pool):
            pool.indirect_dma_start(fix, None, m.edge_sums,
                                    bass.IndirectOffsetOnAxis(m.fix_from[:, :], 0)).then_inc(fix_in, 16)
            pool.wait_ge(fix_ready, 1)
            pool.indirect_dma_start(m.edge_sums, bass.IndirectOffsetOnAxis(m.fix_to[:, :], 0), fix, None,
                                    bounds_check=E - 1, oob_is_err=False).then_inc(fix_out, 16)
            pool.wait_ge(fix_out, 16)
            for j in range(NJ):
                pool.indirect_dma_start(agg[:, j, :], None, m.edge_sums,
                                        bass.IndirectOffsetOnAxis(m.last_row[:, j:j + 1], 0)).then_inc(node_in, 16)
            table.gpsimd(pool)

        @blk.tensor
        def _(pe):
            pe.wait_ge(tail_ready, 1)
            nc.tensor.transpose(ps_tail, tail[:, 0:D], m.ident[:, :]).then_inc(tail_flipped, 1)
            pe.wait_ge(carry_ready, 1)
            nc.tensor.transpose(ps_carry, carry_t[0:D, :], m.ident[0:D, 0:D]).then_inc(carry_flipped, 1)
            project.tensor(pe)
            table.project.tensor(pe)

        @blk.scalar
        def _(act):
            project.scalar(act)
            standard_deviation(nc, act, m.stat, std_wanted, std_ready, 1)
            table.project.scalar(act)

        @blk.sync
        def _(sp):
            table.sync(sp)

        @blk.vector
        def _(dve):
            nc.vector.tensor_copy(tail[:, 0:D], last_sums[:, :, G]).then_inc(tail_ready, 1)
            dve.wait_ge(tail_flipped, 1)
            nc.vector.tensor_copy(tail_t[0:D, :], ps_tail)
            nc.vector.memset(carry_t[0:D, 0:1], 0.0)
            dve.drain()
            nc.vector.tensor_tensor_scan(run_t[0:D, :], m.through[0:D, :], tail_t[0:D, :], 0.0, ALU.mult, ALU.add)
            dve.drain()
            nc.vector.tensor_tensor(carry_t[0:D, 1:P], run_t[0:D, 0:P - 1], m.cont[0:D, 1:P], ALU.mult).then_inc(carry_ready, 1)
            nc.vector.tensor_tensor(m.x_nodes[:, :, :], m.x_nodes[:, :, :], along(m.rows[:, 1, :], 1, NJ), ALU.add)
            dve.wait_ge(carry_flipped, 1)
            dve.wait_ge(fix_in, 16)
            nc.vector.tensor_tensor(fix, fix, ps_carry, ALU.add).then_inc(fix_ready, 1)
            dve.wait_ge(node_in, 16 * NJ)
            nc.vector.tensor_tensor(agg, agg, along(m.full[:, :], 2, D), ALU.mult)
            dve.drain()

            def bring(k, b):
                return nc.vector.tensor_tensor(project.rows[k], agg[:, bass.ds(b * NB, NB), :],
                                               m.h_nodes[:, bass.ds(b * NB, NB), :], ALU.add)

            def take(k, b):
                nc.vector.tensor_tensor(m.x_nodes[:, bass.ds(b * NB, NB), :], m.x_nodes[:, bass.ds(b * NB, NB), :],
                                        project.product[k], ALU.add)

            project.vector(dve, bring, take)
            layer_norm(nc, dve, m.x_nodes[:, :, :], m.h_nodes[:, :, :], sq, m.stat, std_wanted, std_ready, 1)
            table.vector(dve, m.h_nodes[:, :, :])


def attention_edges(nc, m, ctx, layer):
    ins = m.ins

    def sem(name):
        return ctx.enter_context(nc.semaphore(f"edges{layer}_{name}"))

    idx_in = [sem(f"idx_in{k}") for k in range(2)]
    inputs_in = [sem(f"inputs_in{k}") for k in range(2)]
    gathered = [sem(f"gathered{k}") for k in range(2)]
    used = [sem(f"used{k}") for k in range(2)]
    scores_ready = sem("scores_ready")
    exps_ready = sem("exps_ready")
    scanned = sem("scanned")
    rows_ready = sem("rows_ready")
    stored = [sem(f"stored{k}") for k in range(2)]
    turn = sem("turn")

    W = G + 1
    at = 0

    def take(*shape):
        nonlocal at
        v = m.area(at, *shape)
        for s in shape[1:]:
            shape = (shape[0] * s,)
        at += shape[0]
        return v

    sums = [take(ACC, W) for _ in range(2)]
    maxima = [take(H, W) for _ in range(2)]
    rows_g = [take(G, ROW) for _ in range(2)]
    rows_out = [take(G, ROW) for _ in range(2)]
    factors = take(ACC, W)
    terms = take(ACC, W)
    adst_in = [take(G, H) for _ in range(2)]
    weight_in = [take(G) for _ in range(2)]
    adst_s = take(H, W)
    adst = [take(H, W) for _ in range(2)]
    keep = take(H, W)
    reset = take(H, W)
    score = take(H, W)
    raw = take(H, G)
    edge_term = take(H, G)
    args = take(2, H, W)
    weights = take(H, W)
    src_v = ins["src"].bitcast(U32).rearrange("(p f) -> p f", p=P)
    w_v = ins["edge_weight1"].rearrange("(p f) o -> p (f o)", p=P)
    adst_v = m.adst_edges.rearrange("(p f) h -> p f h", p=P)
    out_v = m.edge_rows.rearrange("(p f) c -> p f c", p=P)

    def by_head(v):
        return v.rearrange("p (h c) g -> p h c g", h=H)

    with nc.Block() as blk:

        @blk.sync
        def _(sp):
            def body(k, g, n):
                sp.wait_ge(used[k], n + 1)
                sp.sem_inc(turn, 1)
                sp.dma_start(m.idx[:, k, :], src_v[:, bass.ds(g * G, G)]).then_inc(idx_in[k], 16)
                sp.dma_start(adst_in[k], adst_v[:, bass.ds(g * G, G), :]).then_inc(inputs_in[k], 16)
                sp.dma_start(weight_in[k], w_v[:, bass.ds(g * G, G)]).then_inc(inputs_in[k], 16)

            run(sp, body)

        @blk.gpsimd
        def _(pool):
            def body(k, g, n):
                pool.wait_ge(idx_in[k], 16 * (n + 1))
                pool.sem_inc(turn, 1)
                for t in range(G):
                    pool.indirect_dma_start(rows_g[k][:, t, :], None, m.att_table,
                                            bass.IndirectOffsetOnAxis(m.idx[:, k, t:t + 1], 0)).then_inc(gathered[k], 16)

            run(pool, body)

        @blk.scalar
        def _(act):
            def body(k, g, n):
                act.wait_ge(scores_ready, g + 1)
                act.wait_ge(scanned, g + 1)
                nc.scalar.activation(weights[:, :, 1:W], args[:, 1, :, 1:W], ACT.Exp)
                nc.scalar.activation(by_head(factors), along(args[:, 0, :, :], 2, HC), ACT.Exp).then_inc(exps_ready, 1)
                act.wait_ge(scanned, g + 2)
                nc.scalar.activation(rows_out[k][:, :, ACC:ROW], maxima[k][:, :, 1:W].rearrange("p h g -> p g h"), ACT.Copy)
                nc.scalar.activation(rows_out[k][:, :, 0:ACC], sums[k][:, :, 1:W].rearrange("p c g -> p g c"),
                                     ACT.Copy).then_inc(rows_ready, 1)
                act.wait_ge(rows_ready, g + 1)
                act.dma_start(out_v[:, bass.ds(g * G, G), :], rows_out[k]).then_inc(stored[k], 16)

            with act.Fori(0, PAIRS) as i:
                for k in range(2):
                    body(k, 2 * i + k, i)
                for k in range(2):
                    act.wait_ge(stored[k], 16 * (i + 1))
            body(0, 2 * PAIRS, PAIRS)
            act.wait_ge(stored[0], 16 * (PAIRS + 1))

        @blk.vector
        def _(dve):
            nc.vector.memset(keep[:, :, 0:1], 0.0)
            nc.vector.memset(reset[:, :, 0:1], NEG)
            nc.vector.memset(args[:, 0, :, 0:1], NEG)
            nc.vector.memset(adst[1][:, :, G:W], 0.0)
            nc.vector.memset(maxima[1][:, :, G:W], NEG)
            nc.vector.memset(sums[1][:, :, G:W], 0.0)
            dve.drain()
            for k in range(2):
                dve.sem_inc(used[k], 1)
            dve.sem_inc(scanned, 1)

            def flat(v):
                return v.rearrange("p a g -> p (a g)")

            def body(k, g, n):
                keep_g = m.keep[:, bass.ds(g * G, G)]
                nc.vector.tensor_copy(keep[:, :, 1:W], along(keep_g, 1, H))
                nc.vector.tensor_scalar(reset[:, :, 1:W], along(keep_g, 1, H), -NEG, NEG, ALU.mult, ALU.add)
                nc.vector.tensor_copy(adst_s[:, :, 0:1], adst[1 - k][:, :, G:W])
                nc.vector.tensor_copy(score[:, :, 0:1], maxima[1 - k][:, :, G:W])
                dve.wait_ge(inputs_in[k], 32 * (n + 1))
                nc.vector.tensor_copy(adst_s[:, :, 1:W], adst_in[k].rearrange("p g h -> p h g"))
                nc.vector.tensor_tensor(edge_term, along(weight_in[k], 1, H), along(m.c_edge[layer][:, :], 2, G), ALU.mult)
                dve.drain()
                nc.vector.tensor_tensor_scan(flat(adst[k]), flat(keep), flat(adst_s), 0.0, ALU.mult, ALU.add)
                dve.drain()
                nc.vector.tensor_tensor(edge_term, edge_term, adst[k][:, :, 1:W], ALU.add)
                dve.drain()
                dve.wait_ge(gathered[k], 16 * G * (n + 1))
                nc.vector.tensor_tensor(raw, rows_g[k][:, :, ACC:ROW].rearrange("p g h -> p h g"), edge_term, ALU.add)
                dve.drain()
                nc.vector.scalar_tensor_tensor(score[:, :, 1:W], raw, 0.2, raw, ALU.mult, ALU.max)
                dve.drain()
                nc.vector.tensor_tensor_scan(flat(maxima[k]), flat(reset), flat(score), 0.0, ALU.add, ALU.max)
                dve.drain()
                nc.vector.tensor_tensor(args[:, 0, :, 1:W], maxima[k][:, :, 0:G], reset[:, :, 1:W], ALU.add)
                nc.vector.tensor_tensor(args[:, 1, :, 1:W], score[:, :, 1:W], maxima[k][:, :, 1:W], ALU.subtract)
                dve.drain()
                nc.vector.tensor_tensor(args[:, 0, :, 1:W], args[:, 0, :, 1:W], maxima[k][:, :, 1:W], ALU.subtract).then_inc(scores_ready, 1)
                nc.vector.tensor_copy(terms[:, :, 0:1], sums[1 - k][:, :, G:W])
                dve.wait_ge(exps_ready, g + 1)
                nc.vector.tensor_tensor(by_head(terms)[:, :, :, 1:W], by_head(rows_g[k][:, :, 0:ACC].rearrange("p g c -> p c g")),
                                        along(weights[:, :, 1:W], 2, HC), ALU.mult).then_inc(used[k], 1)
                dve.drain()
                nc.vector.tensor_tensor_scan(flat(sums[k]), flat(factors), flat(terms), 0.0, ALU.mult, ALU.add).then_inc(scanned, 1)
                dve.drain()

            run(dve, body)


def attention_nodes(nc, m, ctx, layer, out):
    final = layer == 1

    def sem(name):
        return ctx.enter_context(nc.semaphore(f"nodes{layer}_{name}"))

    fix_in = sem("fix_in")
    fix_ready = sem("fix_ready")
    fix_out = sem("fix_out")
    tail_ready = sem("tail_ready")
    tail_flipped = sem("tail_flipped")
    args_ready = sem("args_ready")
    exps_ready = sem("exps_ready")
    carry_ready = sem("carry_ready")
    carry_flipped = sem("carry_flipped")
    node_in = sem("node_in")
    self_in = sem("self_in")
    sums_ready = sem("sums_ready")
    sums_spread = sem("sums_spread")
    std_wanted = sem("std_wanted")
    std_ready = sem("std_ready")
    out_ready = sem("out_ready")
    out_stored = sem("out_stored")
    table = None if final else AttentionTable(nc, m, sem, layer + 1)

    W = G + 1
    last_sums = m.area(0, ACC, W)
    last_max = m.area(2 * ACC * W, H, W)
    rows_n = m.area(0, NJ, ROW, parts=NP)
    rows_s = m.area(NJ * ROW, NJ, ROW, parts=NP)
    sq = m.area(NJ * ROW, NJ, D, parts=NP)
    feats = m.area(0, NJ, D, parts=NP, of=m.stream)
    scal = m.area(2 * NJ * ROW, 4, NJ, H, parts=NP)
    tail, t_sum, t_max, t_run, t_args, t_args2 = (m.chunk_tmp[:, i, :] for i in range(6))
    fix = m.area(15872, ROW)
    fixw = m.cols[:, 0:4, :].rearrange("p a b -> p (a b)")[:, 0:3 * ACC].rearrange("p (a b) -> p a b", a=3)
    ps_tail = m.psum[0:ACC, 2048:2048 + 2 * P].rearrange("p (a b) -> p a b", a=2)
    ps_carry = m.psum[:, 2560:2560 + 2 * ACC].rearrange("p (a b) -> p a b", a=2)
    ps_sum = m.psum[0:NP, 3072:3072 + D]

    def heads(v, width=HC):
        return v.rearrange("p (h c) -> p h c", h=H) if len(v.shape) == 2 else v.rearrange("p j (h c) -> p j h c", h=H)

    with nc.Block() as blk:

        @blk.gpsimd
        def _(pool):
            pool.indirect_dma_start(fix, None, m.edge_rows,
                                    bass.IndirectOffsetOnAxis(m.fix_from[:, :], 0)).then_inc(fix_in, 16)
            pool.wait_ge(fix_ready, 1)
            pool.indirect_dma_start(m.edge_rows, bass.IndirectOffsetOnAxis(m.fix_to[:, :], 0), fix, None,
                                    bounds_check=E - 1, oob_is_err=False).then_inc(fix_out, 16)
            pool.wait_ge(fix_out, 16)
            for j in range(NJ):
                pool.indirect_dma_start(rows_n[:, j, :], None, m.edge_rows,
                                        bass.IndirectOffsetOnAxis(m.last_row[:, j:j + 1], 0)).then_inc(node_in, 16)
            if not final:
                table.gpsimd(pool)

        @blk.tensor
        def _(pe):
            pe.wait_ge(tail_ready, 1)
            nc.tensor.transpose(ps_tail[:, 0, :], tail[:, 0:ACC], m.ident[:, :])
            nc.tensor.transpose(ps_tail[:, 1, :], t_args[:, 0:ACC], m.ident[:, :]).then_inc(tail_flipped, 1)
            pe.wait_ge(carry_ready, 1)
            nc.tensor.transpose(ps_carry[:, 0, :], t_sum[0:ACC, :], m.ident[0:ACC, 0:ACC])
            nc.tensor.transpose(ps_carry[:, 1, :], t_max[0:ACC, :], m.ident[0:ACC, 0:ACC]).then_inc(carry_flipped, 1)
            for k in range(2):
                pe.wait_ge(sums_ready, k + 1)
                nc.tensor.matmul(ps_sum, m.ones[0:NP, 0:NP], m.cols[0:NP, 4, :], start=True, stop=True).then_inc(sums_spread, 1)
            if not final:
                table.project.tensor(pe)

        @blk.scalar
        def _(act):
            act.wait_ge(args_ready, 1)
            pair = m.chunk_tmp[0:ACC, 4:6, :]
            nc.scalar.activation(pair, pair, ACT.Exp).then_inc(exps_ready, 1)
            act.wait_ge(args_ready, 2)
            nc.scalar.activation(fixw[:, 0:2, :], fixw[:, 0:2, :], ACT.Exp).then_inc(exps_ready, 1)
            act.wait_ge(args_ready, 3)
            nc.scalar.activation(scal[:, 0:2, :, :], scal[:, 0:2, :, :], ACT.Exp).then_inc(exps_ready, 1)
            act.wait_ge(std_wanted, 1)
            nc.scalar.activation(m.cols[0:NP, 5, :], m.cols[0:NP, 5, :], ACT.Sqrt).then_inc(std_ready, 1)
            if not final:
                table.project.scalar(act)

        @blk.sync
        def _(sp):
            sp.wait_ge(tail_ready, 1)
            sp.dma_start(rows_s, m.att_table.rearrange("(p j) c -> p j c", p=NP)).then_inc(self_in, 16)
            if final:
                sp.wait_ge(out_ready, 1)
                sp.dma_start(out.rearrange("(p j) c -> p j c", p=NP), feats).then_inc(out_stored, 16)
                sp.wait_ge(out_stored, 16)
            else:
                table.sync(sp)

        @blk.vector
        def _(dve):
            nc.vector.tensor_copy(tail[:, 0:ACC], last_sums[:, :, G])
            nc.vector.tensor_copy(heads(t_args[:, 0:ACC]), along(last_max[:, :, G], 2, HC))
            dve.drain()
            dve.sem_inc(tail_ready, 1)
            dve.wait_ge(tail_flipped, 1)
            up = slice(1, P)
            down = slice(0, P - 1)
            A = slice(0, ACC)
            nc.vector.tensor_copy(t_sum[A, :], ps_tail[:, 0, :])
            nc.vector.tensor_copy(t_max[A, :], ps_tail[:, 1, :])
            nc.vector.tensor_scalar(tail[A, :], m.through[:, :], -NEG, NEG, ALU.mult, ALU.add)
            dve.drain()
            nc.vector.tensor_tensor_scan(t_run[A, :], tail[A, :], t_max[A, :], NEG, ALU.add, ALU.max)
            dve.drain()
            nc.vector.memset(t_args[A, 0:1], NEG)
            nc.vector.tensor_tensor(t_args[A, up], t_run[A, down], tail[A, up], ALU.add)
            nc.vector.tensor_tensor(t_args2[A, :], t_max[A, :], t_run[A, :], ALU.subtract)
            dve.drain()
            nc.vector.tensor_tensor(t_args[A, :], t_args[A, :], t_run[A, :], ALU.subtract)
            dve.drain()
            dve.sem_inc(args_ready, 1)
            dve.wait_ge(exps_ready, 1)
            nc.vector.tensor_tensor(t_sum[A, :], t_sum[A, :], t_args2[A, :], ALU.mult)
            nc.vector.tensor_scalar(tail[A, :], m.cont[:, :], -NEG, NEG, ALU.mult, ALU.add)
            nc.vector.memset(t_max[A, 0:1], NEG)
            dve.drain()
            nc.vector.tensor_tensor(t_max[A, up], t_run[A, down], tail[A, up], ALU.add)
            dve.drain()
            nc.vector.tensor_tensor_scan(t_run[A, :], t_args[A, :], t_sum[A, :], 0.0, ALU.mult, ALU.add)
            dve.drain()
            nc.vector.memset(t_sum[A, 0:1], 0.0)
            nc.vector.tensor_copy(t_sum[A, up], t_run[A, down])
            dve.drain()
            dve.sem_inc(carry_ready, 1)
            dve.wait_ge(carry_flipped, 1)
            dve.wait_ge(fix_in, 16)
            nc.vector.tensor_tensor(heads(fixw[:, 2, :]), along(fix[:, ACC:ROW], 2, HC), heads(ps_carry[:, 1, :]), ALU.max)
            dve.drain()
            nc.vector.tensor_tensor(heads(fixw[:, 0, :]), along(fix[:, ACC:ROW], 2, HC), heads(fixw[:, 2, :]), ALU.subtract)
            nc.vector.tensor_tensor(fixw[:, 1, :], ps_carry[:, 1, :], fixw[:, 2, :], ALU.subtract)
            dve.drain()
            dve.sem_inc(args_ready, 1)
            dve.wait_ge(exps_ready, 2)
            nc.vector.tensor_tensor(fix[:, 0:ACC], fix[:, 0:ACC], fixw[:, 0, :], ALU.mult)
            nc.vector.tensor_tensor(fixw[:, 1, :], ps_carry[:, 0, :], fixw[:, 1, :], ALU.mult)
            dve.drain()
            nc.vector.tensor_tensor(fix[:, 0:ACC], fix[:, 0:ACC], fixw[:, 1, :], ALU.add)
            nc.vector.tensor_copy(fix[:, ACC:ROW], heads(fixw[:, 2, :])[:, :, 0])
            dve.drain()
            dve.sem_inc(fix_ready, 1)
            dve.wait_ge(node_in, 16 * NJ)
            nc.vector.tensor_scalar(m.stat[0:NP, 0, :], m.full[:, :], -NEG, NEG, ALU.mult, ALU.add)
            dve.drain()
            nc.vector.tensor_tensor(scal[:, 0, :, :], rows_n[:, :, ACC:ROW], along(m.stat[0:NP, 0, :], 2, H), ALU.add)
            dve.drain()
            nc.vector.tensor_tensor(scal[:, 2, :, :], scal[:, 0, :, :], m.aself[:, :, :], ALU.max)
            dve.drain()
            nc.vector.tensor_tensor(scal[:, 0, :, :], scal[:, 0, :, :], scal[:, 2, :, :], ALU.subtract)
            nc.vector.tensor_tensor(scal[:, 1, :, :], m.aself[:, :, :], scal[:, 2, :, :], ALU.subtract)
            dve.drain()
            dve.sem_inc(args_ready, 1)
            dve.wait_ge(exps_ready, 3)
            sums_n, sums_s = rows_n[:, :, 0:ACC], rows_s[:, :, 0:ACC]
            nc.vector.tensor_tensor(heads(sums_n), heads(sums_n), along(scal[:, 0, :, :], 3, HC), ALU.mult)
            dve.wait_ge(self_in, 16)
            nc.vector.tensor_tensor(heads(sums_s), heads(sums_s), along(scal[:, 1, :, :], 3, HC), ALU.mult)
            dve.drain()
            nc.vector.tensor_tensor(sums_n, sums_n, sums_s, ALU.add)
            dve.drain()
            nc.vector.reciprocal(scal[:, 3, :, :], heads(sums_n)[:, :, :, C])
            dve.drain()
            nc.vector.tensor_tensor(heads(feats), heads(sums_n)[:, :, :, 0:C], along(scal[:, 3, :, :], 3, C), ALU.mult)
            dve.drain()
            nc.vector.tensor_tensor(feats, feats, along(m.rows[:, 2 + layer, :], 1, NJ), ALU.add)
            dve.drain()
            sums, mean, scale = m.cols[0:NP, 4, :], m.cols[0:NP, 6, :], m.cols[0:NP, 5, :]
            nc.vector.tensor_reduce(sums, feats.rearrange("p j c -> p c j"), AX.X, ALU.add).then_inc(sums_ready, 1)
            dve.wait_ge(sums_spread, 1)
            nc.vector.tensor_scalar(mean, ps_sum, 1.0 / N, None, ALU.mult)
            dve.drain()
            nc.vector.tensor_tensor(feats, feats, along(mean, 1, NJ), ALU.subtract)
            dve.drain()
            nc.vector.tensor_tensor(sq, feats, feats, ALU.mult)
            dve.drain()
            nc.vector.tensor_reduce(sums, sq.rearrange("p j c -> p c j"), AX.X, ALU.add).then_inc(sums_ready, 1)
            dve.wait_ge(sums_spread, 2)
            nc.vector.tensor_scalar(scale, ps_sum, 1.0 / N, BN_EPS, ALU.mult, ALU.add).then_inc(std_wanted, 1)
            dve.wait_ge(std_ready, 1)
            nc.vector.reciprocal(scale, scale)
            dve.drain()
            nc.vector.tensor_tensor(scale, scale, m.rows[:, 4, :], ALU.mult)
            dve.drain()
            nc.vector.tensor_tensor(feats, feats, along(scale, 1, NJ), ALU.mult)
            dve.drain()
            nc.vector.tensor_tensor(feats, feats, along(m.rows[:, 5, :], 1, NJ), ALU.add)
            dve.drain()
            if final:
                nc.vector.tensor_tensor(feats, feats, m.h_nodes[:, :, :], ALU.add)
                dve.drain()
                flat = feats.rearrange("p j c -> p (j c)")
                nc.vector.scalar_tensor_tensor(flat, flat, 0.0, m.x_nodes[:, :, :].rearrange("p j c -> p (j c)"),
                                               ALU.max, ALU.add).then_inc(out_ready, 1)
            else:
                nc.vector.tensor_scalar(feats, feats, 0.0, None, ALU.max)
                dve.drain()
                table.vector(dve, feats)


def build(nc, ins, out):
    ctx = ExitStack()
    with ctx:
        m = Memory(nc, ctx, ins)
        setup(nc, m, ctx)
        message_edges(nc, m, ctx)
        message_nodes(nc, m, ctx)
        for layer in range(2):
            attention_edges(nc, m, ctx, layer)
            attention_nodes(nc, m, ctx, layer, out)


def kernel(**inputs):
    import numpy as _np
    import concourse.bacc as _bacc
    from concourse import mybir as _mybir
    from concourse.bass_utils import run_bass_kernel_spmd as _run

    arrays = {name: _np.ascontiguousarray(a) for name, a in inputs.items()}
    dst = arrays["dst"]
    arrays["dst_blocks"] = _np.ascontiguousarray(dst.reshape(SUPER, BLOCKS, BLOCK)[:, :, BLOCK - 1])
    arrays["dst_supers"] = _np.ascontiguousarray(dst.reshape(SUPER, BLOCKS * BLOCK)[:, BLOCKS * BLOCK - 1])
    arrays["edge_attr"] = _np.ascontiguousarray(arrays.pop("edge_attr_64").reshape(P, CHUNK, D).transpose(2, 1, 0))
    arrays["ident"] = _np.eye(P, dtype=_np.float32)
    head = _np.arange(D) // C
    arrays["head_mask"] = (head[:, None] == _np.arange(H)[None, :]).astype(_np.float32)
    place = _np.zeros((D, ACC), _np.float32)
    place[_np.arange(D), head * HC + _np.arange(D) % C] = 1.0
    arrays["place"] = place
    arrays["chunk_ends"] = (_np.arange(1, P + 1, dtype=_np.float32) * CHUNK)[:, None]

    nc = _bacc.Bacc("TRN2", target_bir_lowering=False, num_devices=1)
    ins = {}
    for name, a in arrays.items():
        ins[name] = nc.dram_tensor(f"in_{name}", a.shape, _mybir.dt.from_np(a.dtype), kind="ExternalInput").ap()
    out = nc.dram_tensor("out", (N, D), _mybir.dt.float32, kind="ExternalOutput").ap()
    build(nc, ins, out)
    r = _run(nc, [{f"in_{name}": a for name, a in arrays.items()}], core_ids=[0])
    return r.results[0]["out"]
```

```python
import concourse.bass as bass
from concourse import mybir
from contextlib import ExitStack

P = 128
N = 12500
E = 400000
D = 64
H, C = 4, 16
CHUNK = E // P
G = 25
GROUPS = CHUNK // G
PAIRS = GROUPS // 2
NP, NJ = 125, 100
HC = C + 1
ACC = H * HC
ROW = ACC + H
PROJ = ROW + H
PARTS = 5
JC = NJ // PARTS
NB = 4
HALF = PAIRS // 2
LO = 128
HI = -(-N // LO)
NEG = -1.0e30
SKIP = float(1 << 20)
LN_EPS = 1e-05
BN_EPS = 1e-05

F32 = mybir.dt.float32
BF16 = mybir.dt.bfloat16
I32 = mybir.dt.int32
U32 = mybir.dt.uint32
ALU = mybir.AluOpType
ACT = mybir.ActivationFunctionType
AX = mybir.AxisListType


def along(ap, axis, count):
    shape = list(ap.shape)
    return ap.unsqueeze(axis).broadcast_to(shape[:axis] + [count] + shape[axis:])


def part(c):
    return slice(c * JC, (c + 1) * JC)


class Memory:

    def __init__(self, nc, ctx, ins):
        def sb(name, shape, dt=F32):
            return ctx.enter_context(nc.sbuf_tensor(name, shape, dt))

        def dram(name, shape, dt=F32):
            return nc.dram_tensor(name, shape, dt).ap()

        self.ins = ins
        self.node_in = [ctx.enter_context(nc.semaphore(f"node_in{c}")) for c in range(PARTS)]
        self.turn = ctx.enter_context(nc.semaphore("turn"))
        self.relu_table = dram("relu_table", (N, D))
        self.edge_sums = dram("edge_sums", (E, D))
        self.att_table = dram("att_table", (N, ROW))
        self.adst_table = dram("adst_table", (N, H))
        self.adst_edges = dram("adst_edges", (E, H))
        self.edge_rows = dram("edge_rows", (E, ROW))
        self.counts = dram("counts", (HI * LO + 1, 1))

        self.ident = sb("ident", [P, P])
        self.ones = sb("ones", [P, P])
        self.head_mask = sb("head_mask", [D, H])
        self.before = sb("before", [HI, HI])
        self.w_edge = sb("w_edge", [D + 1, D])
        self.w_node = sb("w_node", [D, D])
        self.w_att = [sb(f"w_att{i}", [D, D]) for i in range(2)]
        self.heads = [sb(f"heads{i}", [D, 4]) for i in range(2)]
        self.place = [sb(f"place{i}", [D, PROJ]) for i in range(2)]
        self.w_ext = [sb(f"w_ext{i}", [D, PROJ]) for i in range(2)]
        self.we_prod = [sb(f"we_prod{i}", [D, P]) for i in range(2)]
        self.c_edge = [sb(f"c_edge{i}", [P, H]) for i in range(2)]
        self.rows = sb("rows", [NP, 5, D])
        self.w_mean = sb("w_mean", [P, 1])

        self.keep = sb("keep", [P, CHUNK])
        self.ends = sb("ends", [P, 2], I32)
        self.cont = sb("cont", [ACC, P])
        self.through = sb("through", [ACC, P])
        self.chunk_end = sb("chunk_end", [P, 1])
        self.fix_from = sb("fix_from", [P, 1], U32)
        self.fix_to = sb("fix_to", [P, 1], U32)
        self.first_dst = sb("first_dst", [P, 1], U32)
        self.last_row = sb("last_row", [NP, NJ], U32)
        self.start_row = sb("start_row", [NP, NJ], U32)
        self.dst_hi = sb("dst_hi", [P, CHUNK], BF16)
        self.dst_lo = sb("dst_lo", [P, CHUNK], BF16)
        self.lanes = sb("lanes", [P, LO], BF16)
        self.one_hot = sb("one_hot", [P, 2, G, HI + LO], BF16)
        self.stat = sb("stat", [P, 4, NJ])
        self.cols = sb("cols", [P, 8, D])
        self.chunk_tmp = sb("chunk_tmp", [P, 6, P])

        self.x_nodes = sb("x_nodes", [NP, NJ, D])
        self.h_nodes = sb("h_nodes", [NP, NJ, D])
        self.aside = sb("aside", [NP, NJ, H])
        self.aself = sb("aself", [NP, NJ, H])

        self.work = sb("work", [P, 16000])
        self.stream = sb("stream", [P, 2 * G * P])
        self.idx = sb("idx", [P, 2, G], U32)
        self.psum = ctx.enter_context(nc.psum_tensor("psum", [P, 4096], F32))

    def area(self, at, *shape, parts=P, dt=F32, of=None):
        size = 1
        for s in shape:
            size *= s
        v = (self.work if of is None else of)[0:parts, at:at + size]
        if dt is not F32:
            v = v.bitcast(dt)
        names = "abcd"[:len(shape)]
        if len(shape) > 1:
            v = v.rearrange("p (" + " ".join(names) + ") -> p " + " ".join(names),
                            **{n: s for n, s in zip(names, shape)})
        return v


def run(eng, body):
    with eng.Fori(0, PAIRS) as i:
        for k in range(2):
            body(k, 2 * i + k, i)
    body(0, 2 * PAIRS, PAIRS)


def run_halves(eng, first, between, second, close=None):
    for start, end, body in ((0, HALF, first), (HALF, PAIRS, second)):
        with eng.Fori(start, end) as i:
            for k in range(2):
                body(k, 2 * i + k, i)
            if close is not None:
                close(i)
        if start == 0:
            between()
    second(0, 2 * PAIRS, PAIRS)


def layer_norm(nc, dve, x, y, sq, stat, cols, std_wanted, std_ready, nth):
    total, mean, var, rstd = (stat[0:NP, i, cols] for i in range(4))
    nc.vector.tensor_reduce(total, x, AX.X, ALU.add)
    dve.drain()
    nc.vector.tensor_scalar(mean, total, 1.0 / D, None, ALU.mult)
    dve.drain()
    nc.vector.tensor_tensor(y, x, along(mean, 2, D), ALU.subtract)
    dve.drain()
    nc.vector.tensor_tensor(sq, y, y, ALU.mult)
    dve.drain()
    nc.vector.tensor_reduce(total, sq, AX.X, ALU.add)
    dve.drain()
    nc.vector.tensor_scalar(var, total, 1.0 / D, LN_EPS, ALU.mult, ALU.add).then_inc(std_wanted, 1)
    dve.wait_ge(std_ready, nth)
    nc.vector.reciprocal(rstd, var)
    dve.drain()
    nc.vector.scalar_tensor_tensor(y, y, 0.0, along(rstd, 2, D), ALU.max, ALU.mult)
    dve.drain()


def standard_deviation(nc, act, stat, cols, std_wanted, std_ready, nth):
    act.wait_ge(std_wanted, nth)
    nc.scalar.activation(stat[0:NP, 2, cols], stat[0:NP, 2, cols], ACT.Sqrt).then_inc(std_ready, 1)


def setup(nc, m, ctx):
    ins = m.ins

    def sem(name):
        return ctx.enter_context(nc.semaphore(name))

    weights_in = sem("weights_in")
    x_in = [sem(f"x_in{c}") for c in range(PARTS)]
    centred = sem("centred")
    squared = sem("squared")
    std_wanted = sem("std_wanted")
    std_ready = sem("std_ready")
    table_ready = sem("table_ready")
    table_out = sem("table_out")
    sq = m.area(0, NJ, D, parts=NP, of=m.stream)

    with nc.Block() as blk:

        @blk.sync
        def _(sp):
            x_v = ins["x"].rearrange("(p j) c -> p j c", p=NP)
            for c in range(PARTS):
                sp.dma_start(m.x_nodes[:, part(c), :], x_v[:, part(c), :]).then_inc(x_in[c], 16)
            for c in range(PARTS):
                sp.wait_ge(table_ready, c + 1)
                sp.dma_start(m.relu_table.rearrange("(p j) c -> p j c", p=NP)[:, part(c), :],
                             m.h_nodes[:, part(c), :]).then_inc(table_out, 16)
            sp.wait_ge(table_out, 16 * PARTS)

        @blk.scalar
        def _(act):
            loads = []

            def load(to, what):
                act.dma_start(to, what).then_inc(weights_in, 16)
                loads.append(1)

            load(m.ident[:, :], ins["ident"])
            load(m.head_mask[:, :], ins["head_mask"])
            load(m.before[:, :], ins["before"])
            load(m.chunk_end[:, :], ins["chunk_ends"])
            load(m.w_edge[0:D, :], ins["L0_gnn_Wl"])
            load(m.w_edge[D:D + 1, :], ins["L0_gnn_bl"].rearrange("(o a) -> o a", o=1))
            load(m.w_node[:, :], ins["L0_gnn_Wn"])
            for i in range(2):
                load(m.w_att[i][:, :], ins[f"L1_gnn_W{i + 1}"])
                load(m.place[i][:, 0:ACC], ins["place"])
                for k, name in enumerate(("as", "ad", "ae")):
                    load(m.heads[i][:, k:k + 1], ins[f"L1_gnn_{name}{i + 1}"].rearrange("h (c o) -> (h c) o", o=1))
                load(m.heads[i][:, 3:4], ins[f"L1_gnn_We{i + 1}"])
            for k, name in enumerate(("L0_gnn_bn", "L1_gnn_b1", "L1_gnn_b2", "L1_gnn_gamma", "L1_gnn_beta")):
                load(m.rows[:, k, :], ins[name].rearrange("(o a) -> o a", o=1).broadcast_to([NP, D]))
            for c in range(PARTS):
                act.wait_ge(centred, c + 1)
                nc.scalar.activation(sq[:, part(c), :], m.h_nodes[:, part(c), :], ACT.Square).then_inc(squared, 1)
            for c in range(PARTS):
                standard_deviation(nc, act, m.stat, part(c), std_wanted, std_ready, c + 1)
            act.wait_ge(weights_in, 16 * len(loads))

        @blk.vector
        def _(dve):
            total, mean, var, rstd = (m.stat[0:NP, i, :] for i in range(4))
            for c in range(PARTS):
                x, h = m.x_nodes[:, part(c), :], m.h_nodes[:, part(c), :]
                dve.wait_ge(x_in[c], 16)
                nc.vector.tensor_reduce(total[:, part(c)], x, AX.X, ALU.add)
                dve.drain()
                nc.vector.tensor_scalar(mean[:, part(c)], total[:, part(c)], 1.0 / D, None, ALU.mult)
                dve.drain()
                nc.vector.tensor_tensor(h, x, along(mean[:, part(c)], 2, D), ALU.subtract).then_inc(centred, 1)
            for c in range(PARTS):
                dve.wait_ge(squared, c + 1)
                nc.vector.tensor_reduce(total[:, part(c)], sq[:, part(c), :], AX.X, ALU.add)
                dve.drain()
                nc.vector.tensor_scalar(var[:, part(c)], total[:, part(c)], 1.0 / D, LN_EPS, ALU.mult, ALU.add).then_inc(std_wanted, 1)
            for c in range(PARTS):
                h = m.h_nodes[:, part(c), :]
                dve.wait_ge(std_ready, c + 1)
                nc.vector.reciprocal(rstd[:, part(c)], var[:, part(c)])
                dve.drain()
                nc.vector.scalar_tensor_tensor(h, h, 0.0, along(rstd[:, part(c)], 2, D), ALU.max, ALU.mult).then_inc(table_ready, 1)


def message_edges(nc, m, ctx):
    ins = m.ins

    def sem(name):
        return ctx.enter_context(nc.semaphore(f"l0_{name}"))

    idx_in = [sem(f"idx_in{k}") for k in range(2)]
    attr_in = [sem(f"attr_in{k}") for k in range(2)]
    gathered = [sem(f"gathered{k}") for k in range(2)]
    projected = [sem(f"projected{k}") for k in range(2)]
    added = [sem(f"added{k}") for k in range(2)]
    terms_ready = sem("terms_ready")
    scanned = sem("scanned")
    rows_ready = sem("rows_ready")
    stored = [sem(f"stored{k}") for k in range(2)]
    dst_in = sem("dst_in")
    ew_in = sem("ew_in")
    zeros_ready = sem("zeros_ready")
    adst_cleared = sem("adst_cleared")
    lanes_ready = sem("lanes_ready")
    keep_ready = sem("keep_ready")
    bias_ready = sem("bias_ready")
    parts_ready = sem("parts_ready")
    products_ready = sem("products_ready")
    hot = sem("hot")
    counted = sem("counted")
    counts_closed = sem("counts_closed")
    totals_ready = sem("totals_ready")
    before_ready = sem("before_ready")
    counts_ready = sem("counts_ready")
    counts_out = sem("counts_out")
    ranges_in = sem("ranges_in")
    fix_in = sem("fix_in")

    W = G + 1
    attr = [m.area(k * G * P, G, P, parts=D + 1, of=m.stream) for k in range(2)]
    rows_g = [m.area(k * G * D, G, D) for k in range(2)]
    at = 2 * G * D
    total = m.area(at, G, D)
    at += G * D
    keeps = m.area(at, D, W)
    at += D * W
    terms = m.area(at, D, W)
    at += D * W
    sums = [m.area(at + k * D * W, D, W) for k in range(2)]
    dst_all = m.area(at, CHUNK, dt=I32)
    ew_all = m.area(at + CHUNK, CHUNK)
    at += 2 * D * W
    rows_out = [m.area(at + k * G * D, G, D) for k in range(2)]
    at += 2 * G * D
    zeros = m.area(at, 500)
    proj = m.psum[:, 0:G * D]
    ps_count = m.psum[0:HI, 3584:3584 + LO]
    ps_before = m.psum[0:HI, 3584 + LO:3584 + LO + 1]
    src_v = ins["src"].bitcast(U32).rearrange("(p f) -> p f", p=P)
    dst_v = ins["dst"].rearrange("(p f) -> p f", p=P)
    out_v = m.edge_sums.rearrange("(p f) c -> p f c", p=P)
    hi_hot, lo_hot = m.one_hot[:, :, :, 0:HI], m.one_hot[:, :, :, HI:HI + LO]

    ends_f = m.cols[:, 0, 0:2]
    wsum = m.cols[:, 2, 0:1]
    fix = m.cols[:, 1, 0:4]
    ends_b = m.chunk_tmp[:, 0:2, 0:ACC]
    last = m.chunk_tmp[0:ACC, 2, :]
    run_count = m.chunk_tmp[0:HI, 3, :]
    row_ones = m.chunk_tmp[0:HI, 4, :]
    count, start, found, empty = (m.stat[0:NP, i, :] for i in range(4))
    ps_ends = m.psum[0:ACC, 2048:2048 + 2 * P].rearrange("p (a b) -> p a b", a=2)
    ps_ext = m.psum[0:D, 2560:2560 + 2 * PROJ].rearrange("p (a b) -> p a b", a=2)
    ps_c = m.psum[:, 3072:3072 + 2 * H].rearrange("p (a b) -> p a b", a=2)
    ps_w = m.psum[:, 3072 + 2 * H:3072 + 2 * H + 1]

    with nc.Block() as blk:

        @blk.sync
        def _(sp):
            sp.dma_start(dst_all, dst_v).then_inc(dst_in, 16)
            sp.dma_start(ew_all, ins["edge_weight1"].rearrange("(p f) o -> p (f o)", p=P)).then_inc(ew_in, 16)

            def load_idx(k, g):
                sp.dma_start(m.idx[:, k, :], src_v[:, bass.ds(g * G, G)]).then_inc(idx_in[k], 16)

            def load_attr(k, g):
                sp.dma_start(attr[k][0:D], ins["edge_attr"][:, bass.ds(g * G, G), :]).then_inc(attr_in[k], 16)

            def body(k, g, n):
                sp.wait_ge(added[k], n + 1)
                sp.sem_inc(m.turn, 1)
                load_idx(k, g)
                load_attr(k, g)

            for k in range(2):
                load_idx(k, k)
                load_attr(k, k)
            with sp.Fori(1, PAIRS) as i:
                for k in range(2):
                    body(k, 2 * i + k, i)
            body(0, 2 * PAIRS, PAIRS)
            sp.wait_ge(adst_cleared, 16)

        @blk.gpsimd
        def _(pool):
            nc.gpsimd.iota(m.chunk_tmp[:, 5, :].bitcast(I32), pattern=[[1, LO]], base=0, channel_multiplier=0).then_inc(lanes_ready, 1)

            def body(k, g, n):
                pool.wait_ge(idx_in[k], 16 * (n + 1))
                pool.sem_inc(m.turn, 1)
                for t in range(G):
                    pool.indirect_dma_start(rows_g[k][:, t, :], None, m.relu_table,
                                            bass.IndirectOffsetOnAxis(m.idx[:, k, t:t + 1], 0)).then_inc(gathered[k], 16)

            def between():
                pool.wait_ge(counts_out, 32)
                pool.indirect_dma_start(fix[:, 0:1], None, m.counts,
                                        bass.IndirectOffsetOnAxis(m.first_dst[:, :], 0)).then_inc(fix_in, 16)

            with pool.Fori(0, PAIRS) as i:
                for k in range(2):
                    body(k, 2 * i + k, i)
            between()
            body(0, 2 * PAIRS, PAIRS)

        @blk.tensor
        def _(pe):
            pe.wait_ge(parts_ready, 1)
            nc.tensor.matmul(ps_ends[:, 0, :], ends_b[:, 0, :], m.ident[:, :], start=True, stop=True)
            nc.tensor.matmul(ps_ends[:, 1, :], ends_b[:, 1, :], m.ident[:, :], start=True, stop=True)
            for i in range(2):
                nc.tensor.matmul(ps_ext[:, i, :], m.w_att[i][:, :], m.place[i][:, :], start=True, stop=True)
                nc.tensor.matmul(ps_c[:, i, :], m.we_prod[i][:, :], m.head_mask[:, :], start=True, stop=True)
            nc.tensor.matmul(ps_w, m.ones[:, :], wsum, start=True, stop=True).then_inc(products_ready, 1)
            for slot in range(2):
                zero = m.one_hot[:, slot, 0, :]
                nc.tensor.matmul(ps_count, zero[:, 0:HI], zero[:, HI:HI + LO], start=(slot == 0), stop=False).then_inc(counted, 1)

            def project(k, g, n):
                pe.wait_ge(added[1 - k], n + 1 + k)
                pe.wait_ge(attr_in[k], 16 * (n + 1))
                for t in range(G):
                    last_one = nc.tensor.matmul(proj[:, t * D:(t + 1) * D], attr[k][:, t, :], m.w_edge[:, :],
                                                start=True, stop=True)
                last_one.then_inc(projected[k], 1)

            def count_up(slot, nth, close=False):
                pe.wait_ge(hot, nth)
                for t in range(G):
                    done = nc.tensor.matmul(ps_count, hi_hot[:, slot, t, :], lo_hot[:, slot, t, :],
                                            start=False, stop=close and t == G - 1)
                done.then_inc(counts_closed if close else counted, 1)

            def first(k, g, n):
                project(k, g, n)
                for slot in range(2):
                    count_up(slot, 2 * g + slot + 1)

            def between():
                count_up(0, GROUPS, close=True)
                pe.wait_ge(totals_ready, 1)
                nc.tensor.matmul(ps_before, m.before[:, :], run_count[:, LO - 1:LO], start=True, stop=True).then_inc(before_ready, 1)

            run_halves(pe, first, between, project)

        @blk.scalar
        def _(act):
            def body(k, g, n):
                act.wait_ge(scanned, g + 1)
                nc.scalar.activation(keeps[:, :, 1:W], along(m.keep[:, bass.ds(g * G, G)], 1, D), ACT.Copy)
                act.wait_ge(added[k], n + 2)
                nc.scalar.activation(terms[:, :, 1:W], total.rearrange("p g c -> p c g"), ACT.Relu).then_inc(terms_ready, 1)
                act.wait_ge(scanned, g + 2)
                nc.scalar.activation(rows_out[k], sums[k][:, :, 1:W].rearrange("p c g -> p g c"), ACT.Copy).then_inc(rows_ready, 1)
                act.wait_ge(rows_ready, g + 1)
                act.dma_start(out_v[:, bass.ds(g * G, G), :], rows_out[k]).then_inc(stored[k], 16)

            def close(i):
                for k in range(2):
                    act.wait_ge(stored[k], 16 * (i + 1))

            def between():
                act.wait_ge(counts_ready, 1)
                act.dma_start(m.counts[1:HI * LO + 1, :].rearrange("(p j) o -> p (j o)", p=HI), run_count).then_inc(counts_out, 16)
                act.dma_start(m.counts[0:1, :], zeros[0:1, 0:1]).then_inc(counts_out, 16)
                act.wait_ge(counts_out, 32)
                act.dma_start(count, m.counts[1:N + 1, :].rearrange("(p j) o -> p (j o)", p=NP)).then_inc(ranges_in, 16)
                act.dma_start(start, m.counts[0:N, :].rearrange("(p j) o -> p (j o)", p=NP)).then_inc(ranges_in, 16)

            act.wait_ge(zeros_ready, 1)
            act.dma_start(m.adst_edges.rearrange("(p k f) h -> p k (f h)", p=P, k=25),
                          along(zeros, 1, 25)).then_inc(adst_cleared, 16)
            act.wait_ge(keep_ready, 1)
            run_halves(act, body, between, body, close)
            act.wait_ge(stored[0], 16 * (PAIRS + 1))

        @blk.vector
        def _(dve):
            for k in range(2):
                nc.vector.memset(attr[k][D:D + 1], 1.0)
            nc.vector.memset(zeros, 0.0)
            nc.vector.memset(m.ones[:, :], 1.0)
            nc.vector.memset(m.one_hot[:, :, 0:2, :], 0.0)
            nc.vector.memset(keeps[:, :, 0:1], 0.0)
            dve.drain()
            dve.sem_inc(zeros_ready, 1)
            for k in range(2):
                dve.sem_inc(added[k], 1)
            dve.wait_ge(dst_in, 16)
            nc.vector.memset(m.keep[:, 0:1], 0.0)
            nc.vector.tensor_tensor(m.keep[:, 1:CHUNK], dst_all[:, 1:CHUNK], dst_all[:, 0:CHUNK - 1], ALU.is_equal)
            dve.drain()
            dve.sem_inc(keep_ready, 1)
            for k, f in enumerate((0, CHUNK - 1)):
                nc.vector.tensor_copy(m.ends[:, k:k + 1], dst_all[:, f:f + 1])
                nc.vector.tensor_copy(ends_f[:, k:k + 1], dst_all[:, f:f + 1])
            dve.wait_ge(ew_in, 16)
            nc.vector.tensor_reduce(wsum, ew_all, AX.X, ALU.add)
            dve.drain()
            for k in range(2):
                nc.vector.tensor_copy(ends_b[:, k, :], ends_f[:, k:k + 1].broadcast_to([P, ACC]))
            nc.vector.tensor_scalar(m.first_dst[:, :], ends_f[:, 0:1], 1.0, None, ALU.add)
            for i in range(2):
                for k in range(2):
                    nc.vector.tensor_scalar(m.place[i][:, ACC + k * H:ACC + (k + 1) * H], m.head_mask[:, :],
                                            m.heads[i][:, k:k + 1], None, ALU.mult)
                nc.vector.tensor_tensor(m.we_prod[i][:, :], m.heads[i][:, 2:3].broadcast_to([D, P]),
                                        m.heads[i][:, 3:4].broadcast_to([D, P]), ALU.mult)
            dve.drain()
            dve.sem_inc(parts_ready, 1)
            dve.wait_ge(lanes_ready, 1)
            nc.vector.tensor_copy(m.lanes[:, :], m.chunk_tmp[:, 5, :].bitcast(I32))
            nc.vector.tensor_single_scalar(ew_all.bitcast(I32), dst_all, LO.bit_length() - 1, ALU.logical_shift_right)
            dve.drain()
            nc.vector.tensor_copy(m.dst_hi[:, :], ew_all.bitcast(I32))
            dve.drain()
            nc.vector.tensor_single_scalar(ew_all.bitcast(I32), dst_all, LO - 1, ALU.bitwise_and)
            dve.drain()
            nc.vector.tensor_copy(m.dst_lo[:, :], ew_all.bitcast(I32))
            dve.wait_ge(products_ready, 1)
            for i in range(2):
                nc.vector.tensor_copy(m.w_ext[i][:, :], ps_ext[:, i, :])
                nc.vector.tensor_copy(m.c_edge[i][:, :], ps_c[:, i, :])
            nc.vector.tensor_scalar(m.w_mean[:, :], ps_w, 1.0 / E, None, ALU.mult)
            nc.vector.tensor_copy(last, ps_ends[:, 1, :])
            nc.vector.memset(m.cont[:, 0:1], 0.0)
            nc.vector.memset(row_ones, 1.0)
            dve.drain()
            nc.vector.tensor_tensor(m.cont[:, 1:P], ps_ends[:, 0, 1:P], last[:, 0:P - 1], ALU.is_equal)
            nc.vector.tensor_tensor(m.through[:, :], ps_ends[:, 0, :], last, ALU.is_equal)
            dve.drain()
            nc.vector.tensor_tensor(m.through[:, :], m.through[:, :], m.cont[:, :], ALU.mult)
            nc.vector.memset(sums[1][:, :, G:W], 0.0)
            dve.drain()
            dve.sem_inc(scanned, 1)

            def scan(k, g, n):
                dve.wait_ge(gathered[k], 16 * G * (n + 1))
                dve.wait_ge(projected[k], n + 1)
                nc.vector.tensor_tensor(total.rearrange("p g c -> p (g c)"), rows_g[k].rearrange("p g c -> p (g c)"),
                                        proj, ALU.add).then_inc(added[k], 1)
                dve.drain()
                nc.vector.tensor_copy(terms[:, :, 0:1], sums[1 - k][:, :, G:W])
                dve.drain()
                dve.wait_ge(terms_ready, g + 1)
                nc.vector.tensor_tensor_scan(sums[k].rearrange("p c g -> p (c g)"), keeps.rearrange("p c g -> p (c g)"),
                                             terms.rearrange("p c g -> p (c g)"), 0.0, ALU.mult, ALU.add).then_inc(scanned, 1)

            def make_hot(slot, group, nth):
                dve.wait_ge(counted, nth)
                nc.vector.tensor_tensor(hi_hot[:, slot], along(m.dst_hi[:, bass.ds(group * G, G)], 2, HI),
                                        along(m.lanes[:, 0:HI], 1, G), ALU.is_equal)
                nc.vector.tensor_tensor(lo_hot[:, slot], along(m.dst_lo[:, bass.ds(group * G, G)], 2, LO),
                                        along(m.lanes[:, :], 1, G), ALU.is_equal).then_inc(hot, 1)

            def first(k, g, n):
                for slot in range(2):
                    make_hot(slot, 2 * g + slot, 2 * g + slot + 1)
                scan(k, g, n)

            def between():
                make_hot(0, GROUPS - 1, GROUPS)
                dve.wait_ge(counts_closed, 1)
                nc.vector.tensor_tensor_scan(run_count, row_ones, ps_count, 0.0, ALU.mult, ALU.add).then_inc(totals_ready, 1)
                dve.wait_ge(before_ready, 1)
                nc.vector.tensor_scalar(run_count, run_count, ps_before, None, ALU.add).then_inc(counts_ready, 1)
                dve.wait_ge(ranges_in, 32)
                nc.vector.tensor_tensor(empty, count, start, ALU.is_equal)
                dve.drain()
                nc.vector.scalar_tensor_tensor(found, empty, SKIP, start, ALU.mult, ALU.add)
                dve.drain()
                nc.vector.tensor_copy(m.start_row[:, :], found)
                dve.drain()
                nc.vector.tensor_scalar(found, count, -1.0, 0.0, ALU.add, ALU.max)
                dve.drain()
                nc.vector.scalar_tensor_tensor(found, empty, SKIP, found, ALU.mult, ALU.add)
                dve.drain()
                nc.vector.tensor_copy(m.last_row[:, :], found)

            run_halves(dve, first, between, scan)
            dve.wait_ge(fix_in, 16)
            nc.vector.tensor_scalar(fix[:, 1:2], fix[:, 0:1], m.chunk_end[:, :], None, ALU.is_gt)
            nc.vector.tensor_scalar(fix[:, 2:3], fix[:, 0:1], m.chunk_end[:, :], -1.0, ALU.min, ALU.add)
            dve.drain()
            nc.vector.tensor_copy(m.fix_from[:, :], fix[:, 2:3])
            nc.vector.scalar_tensor_tensor(fix[:, 3:4], fix[:, 1:2], SKIP, fix[:, 2:3], ALU.mult, ALU.add)
            dve.drain()
            nc.vector.tensor_copy(m.fix_to[:, :], fix[:, 3:4])
            nc.vector.tensor_copy(m.first_dst[:, :], m.ends[:, 0:1])


class Projection:

    def __init__(self, nc, m, sem):
        at = 2 * NJ * ROW
        self.nc, self.m = nc, m
        self.flipped = [m.area(at + k * NB * NP, NB, NP, parts=D) for k in range(2)]
        self.flipped_ps = [m.psum[0:D, k * 512:k * 512 + NB * NP].rearrange("p (a b) -> p a b", a=NB) for k in range(2)]
        self.rows_ready = sem("rows_ready")
        self.flipped_ready = sem("flipped_ready")
        self.flipped_out = sem("flipped_out")
        self.product_ready = sem("product_ready")
        self.product_taken = sem("product_taken")
        self.parts = {"pe": 0, "act": 0, "dve": 0}

    def product(self, cols):
        v = self.m.psum[0:NP, 1024:3072].rearrange("p (a b) -> p a b", a=JC // 5)
        return v[:, :, 0:5 * cols].rearrange("p a (j c) -> p a j c", j=5)

    def tensor(self, pe, rows, weight, cols):
        before = self.parts["pe"] * (JC // NB)
        self.parts["pe"] += 1
        product = self.product(cols)

        def flip(b):
            for q in range(NB):
                last = self.nc.tensor.transpose(self.flipped_ps[b % 2][:, q, :], rows[:, b * NB + q, :], self.m.ident[0:NP, 0:NP])
            last.then_inc(self.flipped_ready, 1)

        def multiply(b):
            pe.wait_ge(self.flipped_out, before + b + 1)
            for q in range(NB):
                j = b * NB + q
                last = self.nc.tensor.matmul(product[:, j // 5, j % 5, :], self.flipped[b % 2][:, q, :], weight,
                                             start=True, stop=True)
            return last

        pe.wait_ge(self.rows_ready, self.parts["pe"])
        flip(0)
        if self.parts["pe"] > 1:
            pe.wait_ge(self.product_taken, self.parts["pe"] - 1)
        for b in range(1, JC // NB):
            flip(b)
            multiply(b - 1)
        multiply(JC // NB - 1).then_inc(self.product_ready, 1)

    def scalar(self, act, func):
        before = self.parts["act"] * (JC // NB)
        self.parts["act"] += 1
        for b in range(JC // NB):
            act.wait_ge(self.flipped_ready, before + b + 1)
            self.nc.scalar.activation(self.flipped[b % 2], self.flipped_ps[b % 2], func).then_inc(self.flipped_out, 1)

    def wait_product(self, eng, who):
        self.parts[who] += 1
        eng.wait_ge(self.product_ready, self.parts[who])


class AttentionTable:

    def __init__(self, nc, m, sem, layer, projection):
        self.nc, self.m, self.layer, self.projection = nc, m, layer, projection
        self.table = m.area(NJ * ROW, NJ, ROW, parts=NP)
        self.part_ready = sem("table_part_ready")
        self.out = sem("table_out")
        self.starts_out = sem("table_starts_out")
        self.first_in = sem("table_first_in")
        self.first_out = sem("table_first_out")
        self.first = m.cols[:, 7, 0:H]

    def vector(self, dve, c):
        nc, m = self.nc, self.m
        self.projection.wait_product(dve, "dve")
        product = self.projection.product(PROJ)
        table, aside, aself = self.table[:, part(c), :], m.aside[:, part(c), :], m.aself[:, part(c), :]
        nc.vector.tensor_copy(table.rearrange("p (a j) c -> p a j c", j=5), product[:, :, :, 0:ROW])
        nc.vector.tensor_copy(aside.rearrange("p (a j) c -> p a j c", j=5), product[:, :, :, ROW:PROJ]).then_inc(self.projection.product_taken, 1)
        if c == 0:
            nc.vector.tensor_scalar(m.cols[0:NP, 6, 0:H], m.c_edge[self.layer][0:NP, :], m.w_mean[0:NP, :], None, ALU.mult)
        dve.drain()
        nc.vector.memset(table[:, :, 0:ACC].rearrange("p j (h c) -> p j h c", h=H)[:, :, :, C], 1.0)
        nc.vector.tensor_tensor(aself, table[:, :, ACC:ROW], aside, ALU.add)
        dve.drain()
        dve.sem_inc(self.part_ready, 1)
        nc.vector.tensor_tensor(aself, aself, along(m.cols[0:NP, 6, 0:H], 1, JC), ALU.add)
        dve.drain()
        flat = aself.rearrange("p j h -> p (j h)")
        nc.vector.scalar_tensor_tensor(flat, flat, 0.2, flat, ALU.mult, ALU.max)

    def gpsimd(self, pool):
        m = self.m
        for j in range(NJ):
            if j % JC == 0:
                pool.wait_ge(self.part_ready, j // JC + 1)
            pool.indirect_dma_start(m.adst_edges, bass.IndirectOffsetOnAxis(m.start_row[:, j:j + 1], 0),
                                    m.aside[:, j, :], None, bounds_check=E - 1, oob_is_err=False).then_inc(self.starts_out, 16)
        pool.wait_ge(self.out, 16 * (PARTS + 1))
        pool.indirect_dma_start(self.first, None, m.adst_table,
                                bass.IndirectOffsetOnAxis(m.first_dst[:, :], 0)).then_inc(self.first_in, 16)

    def sync(self, sp):
        m = self.m
        for c in range(PARTS):
            sp.wait_ge(self.part_ready, c + 1)
            sp.dma_start(m.att_table.rearrange("(p j) c -> p j c", p=NP)[:, part(c), :], self.table[:, part(c), :]).then_inc(self.out, 16)
        sp.dma_start(m.adst_table.rearrange("(p j) c -> p j c", p=NP), m.aside[:, :, :]).then_inc(self.out, 16)
        sp.wait_ge(self.starts_out, 16 * NJ)
        sp.wait_ge(self.first_in, 16)
        sp.dma_start(m.adst_edges.rearrange("(p f) h -> p f h", p=P)[:, 0, :], self.first).then_inc(self.first_out, 16)
        sp.wait_ge(self.out, 16 * (PARTS + 1))
        sp.wait_ge(self.first_out, 16)


def message_nodes(nc, m, ctx):

    def sem(name):
        return ctx.enter_context(nc.semaphore(f"nodes_{name}"))

    fix_in = sem("fix_in")
    fix_ready = sem("fix_ready")
    fix_out = sem("fix_out")
    tail_ready = sem("tail_ready")
    tail_flipped = sem("tail_flipped")
    carry_ready = sem("carry_ready")
    carry_flipped = sem("carry_flipped")
    agg_cleared = sem("agg_cleared")
    std_wanted = sem("std_wanted")
    std_ready = sem("std_ready")
    projection = Projection(nc, m, sem)
    table = AttentionTable(nc, m, sem, 0, projection)

    W = G + 1
    last_sums = m.area(3 * G * D + 2 * D * W, D, W)
    agg = m.area(0, NJ, D, parts=NP)
    sq = m.area(0, NJ, D, parts=NP, of=m.stream)
    tail, tail_t, run_t, carry_t = (m.chunk_tmp[:, i, :] for i in range(4))
    fix = m.cols[:, 0, :]
    ps_tail = m.psum[0:D, 3072:3072 + P]
    ps_carry = m.psum[:, 3584:3584 + D]

    with nc.Block() as blk:

        @blk.gpsimd
        def _(pool):
            pool.indirect_dma_start(fix, None, m.edge_sums,
                                    bass.IndirectOffsetOnAxis(m.fix_from[:, :], 0)).then_inc(fix_in, 16)
            pool.wait_ge(fix_ready, 1)
            pool.indirect_dma_start(m.edge_sums, bass.IndirectOffsetOnAxis(m.fix_to[:, :], 0), fix, None,
                                    bounds_check=E - 1, oob_is_err=False).then_inc(fix_out, 16)
            pool.wait_ge(agg_cleared, 1)
            pool.wait_ge(fix_out, 16)
            for j in range(NJ):
                pool.indirect_dma_start(agg[:, j, :], None, m.edge_sums, bass.IndirectOffsetOnAxis(m.last_row[:, j:j + 1], 0),
                                        bounds_check=E - 1, oob_is_err=False).then_inc(m.node_in[j // JC], 16)
            table.gpsimd(pool)

        @blk.tensor
        def _(pe):
            pe.wait_ge(tail_ready, 1)
            nc.tensor.transpose(ps_tail, tail[:, 0:D], m.ident[:, :]).then_inc(tail_flipped, 1)
            pe.wait_ge(carry_ready, 1)
            nc.tensor.transpose(ps_carry, carry_t[0:D, :], m.ident[0:D, 0:D]).then_inc(carry_flipped, 1)
            for c in range(PARTS):
                projection.tensor(pe, agg[:, part(c), :], m.w_node[:, :], D)
                projection.tensor(pe, m.h_nodes[:, part(c), :], m.w_ext[0][:, :], PROJ)

        @blk.scalar
        def _(act):
            for c in range(PARTS):
                projection.scalar(act, ACT.Copy)
                standard_deviation(nc, act, m.stat, part(c), std_wanted, std_ready, c + 1)
                projection.scalar(act, ACT.Copy)

        @blk.sync
        def _(sp):
            table.sync(sp)

        @blk.vector
        def _(dve):
            nc.vector.tensor_copy(tail[:, 0:D], last_sums[:, :, G]).then_inc(tail_ready, 1)
            nc.vector.memset(agg, 0.0).then_inc(agg_cleared, 1)
            dve.wait_ge(tail_flipped, 1)
            nc.vector.tensor_copy(tail_t[0:D, :], ps_tail)
            nc.vector.memset(carry_t[0:D, 0:1], 0.0)
            dve.drain()
            nc.vector.tensor_tensor_scan(run_t[0:D, :], m.through[0:D, :], tail_t[0:D, :], 0.0, ALU.mult, ALU.add)
            dve.drain()
            nc.vector.tensor_tensor(carry_t[0:D, 1:P], run_t[0:D, 0:P - 1], m.cont[0:D, 1:P], ALU.mult)
            dve.drain()
            dve.sem_inc(carry_ready, 1)
            dve.wait_ge(carry_flipped, 1)
            dve.wait_ge(fix_in, 16)
            nc.vector.tensor_tensor(fix, fix, ps_carry, ALU.add).then_inc(fix_ready, 1)
            nc.vector.tensor_tensor(m.x_nodes[:, :, :], m.x_nodes[:, :, :], along(m.rows[:, 0, :], 1, NJ), ALU.add)
            dve.drain()
            for c in range(PARTS):
                x, h = m.x_nodes[:, part(c), :], m.h_nodes[:, part(c), :]
                dve.wait_ge(m.node_in[c], 16 * JC)
                nc.vector.tensor_tensor(agg[:, part(c), :], agg[:, part(c), :], h, ALU.add).then_inc(projection.rows_ready, 1)
                projection.wait_product(dve, "dve")
                x4 = x.rearrange("p (a j) c -> p a (j c)", j=5)
                nc.vector.tensor_tensor(x4, x4, projection.product(D).rearrange("p a j c -> p a (j c)"),
                                        ALU.add).then_inc(projection.product_taken, 1)
                dve.drain()
                layer_norm(nc, dve, x, h, sq[:, part(c), :], m.stat, part(c), std_wanted, std_ready, c + 1)
                dve.sem_inc(projection.rows_ready, 1)
                table.vector(dve, c)


def attention_edges(nc, m, ctx, layer):
    ins = m.ins

    def sem(name):
        return ctx.enter_context(nc.semaphore(f"edges{layer}_{name}"))

    idx_in = [sem(f"idx_in{k}") for k in range(2)]
    inputs_in = [sem(f"inputs_in{k}") for k in range(2)]
    gathered = [sem(f"gathered{k}") for k in range(2)]
    used = [sem(f"used{k}") for k in range(2)]
    carries_ready = sem("carries_ready")
    laid_out = sem("laid_out")
    scores_ready = sem("scores_ready")
    exps_ready = sem("exps_ready")
    scanned = sem("scanned")
    rows_ready = sem("rows_ready")
    stored = [sem(f"stored{k}") for k in range(2)]

    W = G + 1
    at = 0

    def take(*shape):
        nonlocal at
        v = m.area(at, *shape)
        for s in shape[1:]:
            shape = (shape[0] * s,)
        at += shape[0]
        return v

    sums = [take(ACC, W) for _ in range(2)]
    maxima = [take(H, W) for _ in range(2)]
    rows_g = [take(G, ROW) for _ in range(2)]
    rows_out = [take(G, ROW) for _ in range(2)]
    factors = take(ACC, W)
    terms = take(ACC, W)
    adst_in = [take(G, H) for _ in range(2)]
    weight_in = [take(G) for _ in range(2)]
    adst_s = take(H, W)
    adst = [take(H, W) for _ in range(2)]
    keep = take(H, W)
    reset = take(H, W)
    score = take(H, W)
    raw = take(H, G)
    edge_term = take(H, G)
    args = take(2, H, W)
    weights = take(H, W)
    src_v = ins["src"].bitcast(U32).rearrange("(p f) -> p f", p=P)
    w_v = ins["edge_weight1"].rearrange("(p f) o -> p (f o)", p=P)
    adst_v = m.adst_edges.rearrange("(p f) h -> p f h", p=P)
    out_v = m.edge_rows.rearrange("(p f) c -> p f c", p=P)

    def by_head(v):
        return v.rearrange("p (h c) g -> p h c g", h=H)

    with nc.Block() as blk:

        @blk.sync
        def _(sp):
            def body(k, g, n):
                sp.wait_ge(used[k], n + 1)
                sp.sem_inc(m.turn, 1)
                sp.dma_start(m.idx[:, k, :], src_v[:, bass.ds(g * G, G)]).then_inc(idx_in[k], 16)
                sp.dma_start(adst_in[k], adst_v[:, bass.ds(g * G, G), :]).then_inc(inputs_in[k], 16)
                sp.dma_start(weight_in[k], w_v[:, bass.ds(g * G, G)]).then_inc(inputs_in[k], 16)

            run(sp, body)

        @blk.gpsimd
        def _(pool):
            def body(k, g, n):
                pool.wait_ge(idx_in[k], 16 * (n + 1))
                pool.sem_inc(m.turn, 1)
                for t in range(G):
                    pool.indirect_dma_start(rows_g[k][:, t, :], None, m.att_table,
                                            bass.IndirectOffsetOnAxis(m.idx[:, k, t:t + 1], 0)).then_inc(gathered[k], 16)

            run(pool, body)

        @blk.scalar
        def _(act):
            def lay_out(k, g, n):
                keep_g = along(m.keep[:, bass.ds(g * G, G)], 1, H)
                nc.scalar.activation(keep[:, :, 1:W], keep_g, ACT.Copy)
                nc.scalar.activation(reset[:, :, 1:W], keep_g, ACT.Copy, bias=NEG, scale=-NEG)
                act.wait_ge(inputs_in[k], 32 * (n + 1))
                nc.scalar.activation(adst_s[:, :, 1:W], adst_in[k].rearrange("p g h -> p h g"), ACT.Copy).then_inc(laid_out, 1)

            def body(k, g, n, more=True):
                act.wait_ge(scores_ready, g + 1)
                act.wait_ge(scanned, g + 1)
                nc.scalar.activation(weights[:, :, 1:W], args[:, 1, :, 1:W], ACT.Exp)
                nc.scalar.activation(by_head(factors), along(args[:, 0, :, :], 2, HC), ACT.Exp).then_inc(exps_ready, 1)
                if more:
                    lay_out(1 - k, g + 1, n + k)
                act.wait_ge(scanned, g + 2)
                nc.scalar.activation(rows_out[k][:, :, ACC:ROW], maxima[k][:, :, 1:W].rearrange("p h g -> p g h"), ACT.Copy)
                nc.scalar.activation(rows_out[k][:, :, 0:ACC], sums[k][:, :, 1:W].rearrange("p c g -> p g c"),
                                     ACT.Copy).then_inc(rows_ready, 1)
                act.wait_ge(rows_ready, g + 1)
                act.dma_start(out_v[:, bass.ds(g * G, G), :], rows_out[k]).then_inc(stored[k], 16)

            act.wait_ge(carries_ready, 1)
            lay_out(0, 0, 0)
            with act.Fori(0, PAIRS) as i:
                for k in range(2):
                    body(k, 2 * i + k, i)
                for k in range(2):
                    act.wait_ge(stored[k], 16 * (i + 1))
            body(0, 2 * PAIRS, PAIRS, more=False)
            act.wait_ge(stored[0], 16 * (PAIRS + 1))

        @blk.vector
        def _(dve):
            nc.vector.memset(keep[:, :, 0:1], 0.0)
            nc.vector.memset(reset[:, :, 0:1], NEG)
            nc.vector.memset(args[:, 0, :, 0:1], NEG)
            nc.vector.memset(adst[1][:, :, G:W], 0.0)
            nc.vector.memset(maxima[1][:, :, G:W], NEG)
            nc.vector.memset(sums[1][:, :, G:W], 0.0)
            dve.drain()
            for k in range(2):
                dve.sem_inc(used[k], 1)
            dve.sem_inc(scanned, 1)
            dve.sem_inc(carries_ready, 1)

            def flat(v):
                return v.rearrange("p a g -> p (a g)")

            def body(k, g, n):
                nc.vector.tensor_copy(adst_s[:, :, 0:1], adst[1 - k][:, :, G:W])
                nc.vector.tensor_copy(score[:, :, 0:1], maxima[1 - k][:, :, G:W])
                dve.wait_ge(inputs_in[k], 32 * (n + 1))
                nc.vector.tensor_tensor(edge_term, along(weight_in[k], 1, H), along(m.c_edge[layer][:, :], 2, G), ALU.mult)
                dve.drain()
                dve.wait_ge(laid_out, g + 1)
                nc.vector.tensor_tensor_scan(flat(adst[k]), flat(keep), flat(adst_s), 0.0, ALU.mult, ALU.add)
                dve.drain()
                nc.vector.tensor_tensor(edge_term, edge_term, adst[k][:, :, 1:W], ALU.add)
                dve.drain()
                dve.wait_ge(gathered[k], 16 * G * (n + 1))
                nc.vector.tensor_tensor(raw, rows_g[k][:, :, ACC:ROW].rearrange("p g h -> p h g"), edge_term, ALU.add)
                dve.drain()
                nc.vector.scalar_tensor_tensor(score[:, :, 1:W], raw, 0.2, raw, ALU.mult, ALU.max)
                dve.drain()
                nc.vector.tensor_tensor_scan(flat(maxima[k]), flat(reset), flat(score), 0.0, ALU.add, ALU.max)
                dve.drain()
                nc.vector.tensor_tensor(args[:, 0, :, 1:W], maxima[k][:, :, 0:G], reset[:, :, 1:W], ALU.add)
                nc.vector.tensor_tensor(args[:, 1, :, 1:W], score[:, :, 1:W], maxima[k][:, :, 1:W], ALU.subtract)
                dve.drain()
                nc.vector.tensor_tensor(args[:, 0, :, 1:W], args[:, 0, :, 1:W], maxima[k][:, :, 1:W], ALU.subtract).then_inc(scores_ready, 1)
                nc.vector.tensor_copy(terms[:, :, 0:1], sums[1 - k][:, :, G:W])
                dve.wait_ge(exps_ready, g + 1)
                nc.vector.tensor_tensor(by_head(terms)[:, :, :, 1:W], by_head(rows_g[k][:, :, 0:ACC].rearrange("p g c -> p c g")),
                                        along(weights[:, :, 1:W], 2, HC), ALU.mult).then_inc(used[k], 1)
                dve.drain()
                nc.vector.tensor_tensor_scan(flat(sums[k]), flat(factors), flat(terms), 0.0, ALU.mult, ALU.add).then_inc(scanned, 1)
                dve.drain()

            run(dve, body)


def attention_nodes(nc, m, ctx, layer, out):
    final = layer == 1

    def sem(name):
        return ctx.enter_context(nc.semaphore(f"nodes{layer}_{name}"))

    fix_in = sem("fix_in")
    fix_ready = sem("fix_ready")
    fix_out = sem("fix_out")
    tail_ready = sem("tail_ready")
    tail_flipped = sem("tail_flipped")
    args_ready = sem("args_ready")
    exps_ready = sem("exps_ready")
    carry_ready = sem("carry_ready")
    carry_flipped = sem("carry_flipped")
    cleared = sem("cleared")
    self_in = sem("self_in")
    feats_ready = sem("feats_ready")
    centred = sem("centred")
    squared = sem("squared")
    sums_spread = sem("sums_spread")
    std_wanted = sem("std_wanted")
    std_ready = sem("std_ready")
    out_ready = sem("out_ready")
    out_stored = sem("out_stored")
    projection = None if final else Projection(nc, m, sem)
    table = None if final else AttentionTable(nc, m, sem, layer + 1, projection)

    W = G + 1
    last_sums = m.area(0, ACC, W)
    last_max = m.area(2 * ACC * W, H, W)
    rows_n = m.area(0, NJ, ROW, parts=NP)
    rows_s = m.area(NJ * ROW, NJ, ROW, parts=NP)
    sq = m.area(NJ * ROW, NJ, D, parts=NP)
    feats = m.area(0, NJ, D, parts=NP, of=m.stream)
    scal = m.area(2 * NJ * ROW, 4, NJ, H, parts=NP)
    tail, t_sum, t_max, t_run, t_args, t_args2 = (m.chunk_tmp[:, i, :] for i in range(6))
    fix = m.area(15872, ROW)
    fixw = m.cols[:, 0:4, :].rearrange("p a b -> p (a b)")[:, 0:3 * ACC].rearrange("p (a b) -> p a b", a=3)
    ps_tail = m.psum[0:ACC, 0:2 * P].rearrange("p (a b) -> p a b", a=2)
    ps_carry = m.psum[:, 512:512 + 2 * ACC].rearrange("p (a b) -> p a b", a=2)
    ps_sum = [m.psum[0:NP, 3072 + k * 512:3072 + k * 512 + NB * D] for k in range(2)]

    def heads(v, width=HC):
        return v.rearrange("p (h c) -> p h c", h=H) if len(v.shape) == 2 else v.rearrange("p j (h c) -> p j h c", h=H)

    with nc.Block() as blk:

        @blk.gpsimd
        def _(pool):
            pool.indirect_dma_start(fix, None, m.edge_rows,
                                    bass.IndirectOffsetOnAxis(m.fix_from[:, :], 0)).then_inc(fix_in, 16)
            pool.wait_ge(fix_ready, 1)
            pool.indirect_dma_start(m.edge_rows, bass.IndirectOffsetOnAxis(m.fix_to[:, :], 0), fix, None,
                                    bounds_check=E - 1, oob_is_err=False).then_inc(fix_out, 16)
            pool.wait_ge(cleared, 1)
            pool.wait_ge(fix_out, 16)
            for j in range(NJ):
                pool.indirect_dma_start(rows_n[:, j, :], None, m.edge_rows, bass.IndirectOffsetOnAxis(m.last_row[:, j:j + 1], 0),
                                        bounds_check=E - 1, oob_is_err=False).then_inc(m.node_in[j // JC], 16)
            if not final:
                table.gpsimd(pool)

        @blk.tensor
        def _(pe):
            pe.wait_ge(tail_ready, 1)
            nc.tensor.transpose(ps_tail[:, 0, :], tail[:, 0:ACC], m.ident[:, :])
            nc.tensor.transpose(ps_tail[:, 1, :], t_args[:, 0:ACC], m.ident[:, :]).then_inc(tail_flipped, 1)
            pe.wait_ge(carry_ready, 1)
            nc.tensor.transpose(ps_carry[:, 0, :], t_sum[0:ACC, :], m.ident[0:ACC, 0:ACC])
            nc.tensor.transpose(ps_carry[:, 1, :], t_max[0:ACC, :], m.ident[0:ACC, 0:ACC]).then_inc(carry_flipped, 1)

            def add_up(k, source, ready):
                for c in range(PARTS):
                    pe.wait_ge(ready, c + 1)
                    for q in range(JC // NB):
                        j = c * JC + q * NB
                        last = nc.tensor.matmul(ps_sum[k], m.ones[0:NP, 0:NP], source[:, j:j + NB, :].rearrange("p j c -> p (j c)"),
                                                start=(j == 0), stop=(j == NJ - NB))
                last.then_inc(sums_spread, 1)

            add_up(0, feats, feats_ready)
            add_up(1, sq, squared)
            if not final:
                for c in range(PARTS):
                    projection.tensor(pe, feats[:, part(c), :], m.w_ext[layer + 1][:, :], PROJ)

        @blk.scalar
        def _(act):
            act.wait_ge(args_ready, 1)
            pair = m.chunk_tmp[0:ACC, 4:6, :]
            nc.scalar.activation(pair, pair, ACT.Exp).then_inc(exps_ready, 1)
            act.wait_ge(args_ready, 2)
            nc.scalar.activation(fixw[:, 0:2, :], fixw[:, 0:2, :], ACT.Exp).then_inc(exps_ready, 1)
            for c in range(PARTS):
                act.wait_ge(args_ready, 3 + c)
                nc.scalar.activation(scal[:, 0:2, part(c), :], scal[:, 0:2, part(c), :], ACT.Exp).then_inc(exps_ready, 1)
            for c in range(PARTS):
                act.wait_ge(centred, c + 1)
                nc.scalar.activation(sq[:, part(c), :], feats[:, part(c), :], ACT.Square).then_inc(squared, 1)
            act.wait_ge(std_wanted, 1)
            nc.scalar.activation(m.cols[0:NP, 5, :], m.cols[0:NP, 5, :], ACT.Sqrt).then_inc(std_ready, 1)
            if not final:
                for c in range(PARTS):
                    projection.scalar(act, ACT.Relu)

        @blk.sync
        def _(sp):
            sp.wait_ge(tail_ready, 1)
            sp.dma_start(rows_s, m.att_table.rearrange("(p j) c -> p j c", p=NP)).then_inc(self_in, 16)
            if final:
                for c in range(PARTS):
                    sp.wait_ge(out_ready, c + 1)
                    sp.dma_start(out.rearrange("(p j) c -> p j c", p=NP)[:, part(c), :], feats[:, part(c), :]).then_inc(out_stored, 16)
                sp.wait_ge(out_stored, 16 * PARTS)
            else:
                table.sync(sp)

        @blk.vector
        def _(dve):
            nc.vector.tensor_copy(tail[:, 0:ACC], last_sums[:, :, G])
            nc.vector.tensor_copy(heads(t_args[:, 0:ACC]), along(last_max[:, :, G], 2, HC))
            dve.drain()
            dve.sem_inc(tail_ready, 1)
            dve.wait_ge(tail_flipped, 1)
            up = slice(1, P)
            down = slice(0, P - 1)
            A = slice(0, ACC)
            nc.vector.tensor_copy(t_sum[A, :], ps_tail[:, 0, :])
            nc.vector.tensor_copy(t_max[A, :], ps_tail[:, 1, :])
            nc.vector.tensor_scalar(tail[A, :], m.through[:, :], -NEG, NEG, ALU.mult, ALU.add)
            dve.drain()
            nc.vector.tensor_tensor_scan(t_run[A, :], tail[A, :], t_max[A, :], NEG, ALU.add, ALU.max)
            dve.drain()
            nc.vector.memset(t_args[A, 0:1], NEG)
            nc.vector.tensor_tensor(t_args[A, up], t_run[A, down], tail[A, up], ALU.add)
            nc.vector.tensor_tensor(t_args2[A, :], t_max[A, :], t_run[A, :], ALU.subtract)
            dve.drain()
            nc.vector.tensor_tensor(t_args[A, :], t_args[A, :], t_run[A, :], ALU.subtract)
            dve.drain()
            dve.sem_inc(args_ready, 1)
            dve.wait_ge(exps_ready, 1)
            nc.vector.tensor_tensor(t_sum[A, :], t_sum[A, :], t_args2[A, :], ALU.mult)
            nc.vector.tensor_scalar(tail[A, :], m.cont[:, :], -NEG, NEG, ALU.mult, ALU.add)
            nc.vector.memset(t_max[A, 0:1], NEG)
            dve.drain()
            nc.vector.tensor_tensor(t_max[A, up], t_run[A, down], tail[A, up], ALU.add)
            dve.drain()
            nc.vector.tensor_tensor_scan(t_run[A, :], t_args[A, :], t_sum[A, :], 0.0, ALU.mult, ALU.add)
            dve.drain()
            nc.vector.memset(t_sum[A, 0:1], 0.0)
            nc.vector.tensor_copy(t_sum[A, up], t_run[A, down])
            dve.drain()
            dve.sem_inc(carry_ready, 1)
            nc.vector.memset(rows_n[:, :, 0:ACC], 0.0)
            nc.vector.memset(rows_n[:, :, ACC:ROW], NEG).then_inc(cleared, 1)
            dve.wait_ge(carry_flipped, 1)
            dve.wait_ge(fix_in, 16)
            nc.vector.tensor_tensor(heads(fixw[:, 2, :]), along(fix[:, ACC:ROW], 2, HC), heads(ps_carry[:, 1, :]), ALU.max)
            dve.drain()
            nc.vector.tensor_tensor(heads(fixw[:, 0, :]), along(fix[:, ACC:ROW], 2, HC), heads(fixw[:, 2, :]), ALU.subtract)
            nc.vector.tensor_tensor(fixw[:, 1, :], ps_carry[:, 1, :], fixw[:, 2, :], ALU.subtract)
            dve.drain()
            dve.sem_inc(args_ready, 1)
            dve.wait_ge(exps_ready, 2)
            nc.vector.tensor_tensor(fix[:, 0:ACC], fix[:, 0:ACC], fixw[:, 0, :], ALU.mult)
            nc.vector.tensor_tensor(fixw[:, 1, :], ps_carry[:, 0, :], fixw[:, 1, :], ALU.mult)
            dve.drain()
            nc.vector.tensor_tensor(fix[:, 0:ACC], fix[:, 0:ACC], fixw[:, 1, :], ALU.add)
            nc.vector.tensor_copy(fix[:, ACC:ROW], heads(fixw[:, 2, :])[:, :, 0])
            dve.drain()
            dve.sem_inc(fix_ready, 1)
            if final:
                nc.vector.tensor_tensor(m.h_nodes[:, :, :], m.h_nodes[:, :, :], along(m.rows[:, 4, :], 1, NJ), ALU.add)
            for c in range(PARTS):
                J = part(c)
                dve.wait_ge(m.node_in[c], 16 * JC * (layer + 2))
                nc.vector.tensor_tensor(scal[:, 2, J, :], rows_n[:, J, ACC:ROW], m.aself[:, J, :], ALU.max)
                dve.drain()
                nc.vector.tensor_tensor(scal[:, 0, J, :], rows_n[:, J, ACC:ROW], scal[:, 2, J, :], ALU.subtract)
                nc.vector.tensor_tensor(scal[:, 1, J, :], m.aself[:, J, :], scal[:, 2, J, :], ALU.subtract)
                dve.drain()
                dve.sem_inc(args_ready, 1)
                dve.wait_ge(exps_ready, 3 + c)
                sums_n, sums_s = rows_n[:, J, 0:ACC], rows_s[:, J, 0:ACC]
                nc.vector.tensor_tensor(heads(sums_n), heads(sums_n), along(scal[:, 0, J, :], 3, HC), ALU.mult)
                dve.wait_ge(self_in, 16)
                nc.vector.tensor_tensor(heads(sums_s), heads(sums_s), along(scal[:, 1, J, :], 3, HC), ALU.mult)
                dve.drain()
                nc.vector.tensor_tensor(sums_n, sums_n, sums_s, ALU.add)
                dve.drain()
                nc.vector.reciprocal(scal[:, 3, J, :], heads(sums_n)[:, :, :, C])
                dve.drain()
                nc.vector.tensor_tensor(heads(feats[:, J, :]), heads(sums_n)[:, :, :, 0:C], along(scal[:, 3, J, :], 3, C), ALU.mult)
                dve.drain()
                nc.vector.tensor_tensor(feats[:, J, :], feats[:, J, :], along(m.rows[:, 1 + layer, :], 1, JC), ALU.add).then_inc(feats_ready, 1)
            mean, scale = m.cols[0:NP, 4, :], m.cols[0:NP, 5, :]

            def moment(to, k):
                nc.vector.tensor_reduce(to, ps_sum[k].rearrange("p (j c) -> p c j", j=NB), AX.X, ALU.add)
                dve.drain()

            dve.wait_ge(sums_spread, 1)
            moment(mean, 0)
            nc.vector.tensor_scalar(mean, mean, 1.0 / N, None, ALU.mult)
            dve.drain()
            for c in range(PARTS):
                nc.vector.tensor_tensor(feats[:, part(c), :], feats[:, part(c), :], along(mean, 1, JC), ALU.subtract).then_inc(centred, 1)
            dve.wait_ge(sums_spread, 2)
            moment(scale, 1)
            nc.vector.tensor_scalar(scale, scale, 1.0 / N, BN_EPS, ALU.mult, ALU.add).then_inc(std_wanted, 1)
            dve.wait_ge(std_ready, 1)
            nc.vector.reciprocal(scale, scale)
            dve.drain()
            nc.vector.tensor_tensor(scale, scale, m.rows[:, 3, :], ALU.mult)
            dve.drain()
            for c in range(PARTS):
                f = feats[:, part(c), :]
                nc.vector.tensor_tensor(f, f, along(scale, 1, JC), ALU.mult)
                dve.drain()
                if final:
                    nc.vector.tensor_tensor(f, f, m.h_nodes[:, part(c), :], ALU.add)
                    dve.drain()
                    flat = f.rearrange("p j c -> p (j c)")
                    nc.vector.scalar_tensor_tensor(flat, flat, 0.0, m.x_nodes[:, part(c), :].rearrange("p j c -> p (j c)"),
                                                   ALU.max, ALU.add).then_inc(out_ready, 1)
                else:
                    nc.vector.tensor_tensor(f, f, along(m.rows[:, 4, :], 1, JC), ALU.add).then_inc(projection.rows_ready, 1)
                    if c:
                        table.vector(dve, c - 1)
            if not final:
                table.vector(dve, PARTS - 1)


def build(nc, ins, out):
    ctx = ExitStack()
    with ctx:
        m = Memory(nc, ctx, ins)
        setup(nc, m, ctx)
        message_edges(nc, m, ctx)
        message_nodes(nc, m, ctx)
        for layer in range(2):
            attention_edges(nc, m, ctx, layer)
            attention_nodes(nc, m, ctx, layer, out)


def kernel(**inputs):
    import numpy as _np
    import concourse.bacc as _bacc
    from concourse import mybir as _mybir
    from concourse.bass_utils import run_bass_kernel_spmd as _run

    arrays = {name: _np.ascontiguousarray(a) for name, a in inputs.items()}
    arrays["edge_attr"] = _np.ascontiguousarray(arrays.pop("edge_attr_64").reshape(P, CHUNK, D).transpose(2, 1, 0))
    arrays["ident"] = _np.eye(P, dtype=_np.float32)
    head = _np.arange(D) // C
    arrays["head_mask"] = (head[:, None] == _np.arange(H)[None, :]).astype(_np.float32)
    place = _np.zeros((D, ACC), _np.float32)
    place[_np.arange(D), head * HC + _np.arange(D) % C] = 1.0
    arrays["place"] = place
    arrays["before"] = _np.triu(_np.ones((HI, HI), _np.float32), 1)
    arrays["chunk_ends"] = (_np.arange(1, P + 1, dtype=_np.float32) * CHUNK)[:, None]

    nc = _bacc.Bacc("TRN2", target_bir_lowering=False, num_devices=1)
    ins = {}
    for name, a in arrays.items():
        ins[name] = nc.dram_tensor(f"in_{name}", a.shape, _mybir.dt.from_np(a.dtype), kind="ExternalInput").ap()
    out = nc.dram_tensor("out", (N, D), _mybir.dt.float32, kind="ExternalOutput").ap()
    build(nc, ins, out)
    r = _run(nc, [{f"in_{name}": a for name, a in arrays.items()}], core_ids=[0])
    return r.results[0]["out"]
```

```python
import concourse.bass as bass
from concourse import mybir
from contextlib import ExitStack

P = 128
N = 12500
E = 400000
D = 64
H, C = 4, 16
CHUNK = E // P
G = 25
GROUPS = CHUNK // G
PAIRS = GROUPS // 2
NP, NJ = 125, 100
HC = C + 1
ACC = H * HC
ROW = ACC + H
PROJ = ROW + H
PARTS = 5
JC = NJ // PARTS
NB = 4
HALF = PAIRS // 2
LO = 128
HI = -(-N // LO)
NEG = -1.0e30
SKIP = float(1 << 20)
LN_EPS = 1e-05
BN_EPS = 1e-05

F32 = mybir.dt.float32
BF16 = mybir.dt.bfloat16
I32 = mybir.dt.int32
U32 = mybir.dt.uint32
ALU = mybir.AluOpType
ACT = mybir.ActivationFunctionType
AX = mybir.AxisListType


def along(ap, axis, count):
    shape = list(ap.shape)
    return ap.unsqueeze(axis).broadcast_to(shape[:axis] + [count] + shape[axis:])


def part(c):
    return slice(c * JC, (c + 1) * JC)


class Memory:

    def __init__(self, nc, ctx, ins):
        def sb(name, shape, dt=F32):
            return ctx.enter_context(nc.sbuf_tensor(name, shape, dt))

        def dram(name, shape, dt=F32):
            return nc.dram_tensor(name, shape, dt).ap()

        self.ins = ins
        self.node_in = [ctx.enter_context(nc.semaphore(f"node_in{c}")) for c in range(PARTS)]
        self.turn = ctx.enter_context(nc.semaphore("turn"))
        self.src = dram("src_ordered", (E,), I32)
        self.dst = dram("dst_ordered", (E,), I32)
        self.edge_w = dram("edge_w_ordered", (E,))
        self.edge_attr = dram("edge_attr_ordered", (D, CHUNK, P))
        self.relu_table = dram("relu_table", (N, D))
        self.edge_sums = dram("edge_sums", (E, D))
        self.att_table = dram("att_table", (N, ROW))
        self.adst_table = dram("adst_table", (N, H))
        self.adst_edges = dram("adst_edges", (E, H))
        self.edge_rows = dram("edge_rows", (E, ROW))
        self.counts = dram("counts", (HI * LO + 1, 1))

        self.ident = sb("ident", [P, P])
        self.ones = sb("ones", [P, P])
        self.head_mask = sb("head_mask", [D, H])
        self.before = sb("before", [P, P])
        self.unordered = sb("unordered", [1, 1], I32)
        self.w_edge = sb("w_edge", [D + 1, D])
        self.w_node = sb("w_node", [D, D])
        self.w_att = [sb(f"w_att{i}", [D, D]) for i in range(2)]
        self.heads = [sb(f"heads{i}", [D, 4]) for i in range(2)]
        self.place = [sb(f"place{i}", [D, PROJ]) for i in range(2)]
        self.w_ext = [sb(f"w_ext{i}", [D, PROJ]) for i in range(2)]
        self.we_prod = [sb(f"we_prod{i}", [D, P]) for i in range(2)]
        self.c_edge = [sb(f"c_edge{i}", [P, H]) for i in range(2)]
        self.rows = sb("rows", [NP, 5, D])
        self.w_mean = sb("w_mean", [P, 1])

        self.keep = sb("keep", [P, CHUNK])
        self.ends = sb("ends", [P, 2], I32)
        self.cont = sb("cont", [ACC, P])
        self.through = sb("through", [ACC, P])
        self.chunk_end = sb("chunk_end", [P, 1])
        self.fix_from = sb("fix_from", [P, 1], U32)
        self.fix_to = sb("fix_to", [P, 1], U32)
        self.first_dst = sb("first_dst", [P, 1], U32)
        self.last_row = sb("last_row", [NP, NJ], U32)
        self.start_row = sb("start_row", [NP, NJ], U32)
        self.dst_hi = sb("dst_hi", [P, CHUNK], BF16)
        self.dst_lo = sb("dst_lo", [P, CHUNK], BF16)
        self.lanes = sb("lanes", [P, LO], BF16)
        self.one_hot = sb("one_hot", [P, 2, G, HI + LO], BF16)
        self.stat = sb("stat", [P, 4, NJ])
        self.cols = sb("cols", [P, 8, D])
        self.chunk_tmp = sb("chunk_tmp", [P, 6, P])

        self.x_nodes = sb("x_nodes", [NP, NJ, D])
        self.h_nodes = sb("h_nodes", [NP, NJ, D])
        self.aside = sb("aside", [NP, NJ, H])
        self.aself = sb("aself", [NP, NJ, H])

        self.work = sb("work", [P, 16000])
        self.stream = sb("stream", [P, 2 * G * P])
        self.idx = sb("idx", [P, 2, G], U32)
        self.psum = ctx.enter_context(nc.psum_tensor("psum", [P, 4096], F32))

    def area(self, at, *shape, parts=P, dt=F32, of=None):
        size = 1
        for s in shape:
            size *= s
        v = (self.work if of is None else of)[0:parts, at:at + size]
        if dt is not F32:
            v = v.bitcast(dt)
        names = "abcd"[:len(shape)]
        if len(shape) > 1:
            v = v.rearrange("p (" + " ".join(names) + ") -> p " + " ".join(names),
                            **{n: s for n, s in zip(names, shape)})
        return v


def run(eng, body):
    with eng.Fori(0, PAIRS) as i:
        for k in range(2):
            body(k, 2 * i + k, i)
    body(0, 2 * PAIRS, PAIRS)


def run_halves(eng, first, between, second, close=None):
    for start, end, body in ((0, HALF, first), (HALF, PAIRS, second)):
        with eng.Fori(start, end) as i:
            for k in range(2):
                body(k, 2 * i + k, i)
            if close is not None:
                close(i)
        if start == 0:
            between()
    second(0, 2 * PAIRS, PAIRS)


def layer_norm(nc, dve, x, y, sq, stat, cols, std_wanted, std_ready, nth):
    total, mean, var, rstd = (stat[0:NP, i, cols] for i in range(4))
    nc.vector.tensor_reduce(total, x, AX.X, ALU.add)
    dve.drain()
    nc.vector.tensor_scalar(mean, total, 1.0 / D, None, ALU.mult)
    dve.drain()
    nc.vector.tensor_tensor(y, x, along(mean, 2, D), ALU.subtract)
    dve.drain()
    nc.vector.tensor_tensor(sq, y, y, ALU.mult)
    dve.drain()
    nc.vector.tensor_reduce(total, sq, AX.X, ALU.add)
    dve.drain()
    nc.vector.tensor_scalar(var, total, 1.0 / D, LN_EPS, ALU.mult, ALU.add).then_inc(std_wanted, 1)
    dve.wait_ge(std_ready, nth)
    nc.vector.reciprocal(rstd, var)
    dve.drain()
    nc.vector.scalar_tensor_tensor(y, y, 0.0, along(rstd, 2, D), ALU.max, ALU.mult)
    dve.drain()


def standard_deviation(nc, act, stat, cols, std_wanted, std_ready, nth):
    act.wait_ge(std_wanted, nth)
    nc.scalar.activation(stat[0:NP, 2, cols], stat[0:NP, 2, cols], ACT.Sqrt).then_inc(std_ready, 1)


def setup(nc, m, ctx):
    ins = m.ins

    def sem(name):
        return ctx.enter_context(nc.semaphore(name))

    weights_in = sem("weights_in")
    x_in = [sem(f"x_in{c}") for c in range(PARTS)]
    mean_ready = sem("mean_ready")
    centred = sem("centred")
    centred_by_pool = sem("centred_by_pool")
    ON_POOL = (1, 3)
    squared = sem("squared")
    std_wanted = sem("std_wanted")
    std_ready = sem("std_ready")
    table_ready = sem("table_ready")
    table_out = sem("table_out")
    dst_in = sem("setup_dst_in")
    copied = sem("copied")
    falls_ready = sem("falls_ready")
    falls_summed = sem("falls_summed")
    sq = m.area(0, NJ, D, parts=NP, of=m.stream)
    dst_all = m.area(0, CHUNK, dt=I32)
    falls = m.area(CHUNK, CHUNK)
    seam = m.area(2 * CHUNK, 2, dt=I32)
    fall = m.cols[:, 0, 0:1]
    ps_falls = m.psum[:, 0:1]

    with nc.Block() as blk:

        @blk.sync
        def _(sp):
            x_v = ins["x"].rearrange("(p j) c -> p j c", p=NP)
            for c in range(PARTS):
                sp.dma_start(m.x_nodes[:, part(c), :], x_v[:, part(c), :]).then_inc(x_in[c], 16)
            sp.dma_start(dst_all, ins["dst"].rearrange("(p f) -> p f", p=P)).then_inc(dst_in, 16)
            seams = ins["dst"][CHUNK - 1:CHUNK - 1 + (P - 1) * CHUNK].rearrange("(p f) -> p f", p=P - 1)
            sp.dma_start(seam[0:P - 1], seams[:, 0:2]).then_inc(dst_in, 16)
            for to, what in ((m.src, ins["src"]), (m.dst, ins["dst"]), (m.edge_w, ins["edge_weight1"].rearrange("e o -> (e o)"))):
                sp.dma_start(to.rearrange("(p f) -> p f", p=P), what.rearrange("(p f) -> p f", p=P)).then_inc(copied, 16)
            for c in range(PARTS):
                sp.wait_ge(table_ready, c + 1)
                sp.dma_start(m.relu_table.rearrange("(p j) c -> p j c", p=NP)[:, part(c), :],
                             m.h_nodes[:, part(c), :]).then_inc(table_out, 16)
            sp.wait_ge(table_out, 16 * PARTS)
            sp.wait_ge(copied, 48)

        @blk.tensor
        def _(pe):
            pe.wait_ge(falls_ready, 1)
            nc.tensor.matmul(ps_falls, m.ones[:, :], fall, start=True, stop=True).then_inc(falls_summed, 1)

        @blk.gpsimd
        def _(pool):
            mean = m.stat[0:NP, 1, :]
            for c in ON_POOL:
                pool.wait_ge(mean_ready, c + 1)
                nc.gpsimd.tensor_tensor(m.h_nodes[:, part(c), :], m.x_nodes[:, part(c), :], along(mean[:, part(c)], 2, D),
                                        ALU.subtract).then_inc(centred_by_pool, 1)

        @blk.scalar
        def _(act):
            loads = []

            def load(to, what):
                act.dma_start(to, what).then_inc(weights_in, 16)
                loads.append(1)

            load(m.ident[:, :], ins["ident"])
            load(m.head_mask[:, :], ins["head_mask"])
            load(m.before[:, :], ins["before"])
            load(m.chunk_end[:, :], ins["chunk_ends"])
            load(m.w_edge[0:D, :], ins["L0_gnn_Wl"])
            load(m.w_edge[D:D + 1, :], ins["L0_gnn_bl"].rearrange("(o a) -> o a", o=1))
            load(m.w_node[:, :], ins["L0_gnn_Wn"])
            for i in range(2):
                load(m.w_att[i][:, :], ins[f"L1_gnn_W{i + 1}"])
                load(m.place[i][:, 0:ACC], ins["place"])
                for k, name in enumerate(("as", "ad", "ae")):
                    load(m.heads[i][:, k:k + 1], ins[f"L1_gnn_{name}{i + 1}"].rearrange("h (c o) -> (h c) o", o=1))
                load(m.heads[i][:, 3:4], ins[f"L1_gnn_We{i + 1}"])
            for k, name in enumerate(("L0_gnn_bn", "L1_gnn_b1", "L1_gnn_b2", "L1_gnn_gamma", "L1_gnn_beta")):
                load(m.rows[:, k, :], ins[name].rearrange("(o a) -> o a", o=1).broadcast_to([NP, D]))
            for c in range(PARTS):
                if c in ON_POOL:
                    act.wait_ge(centred_by_pool, ON_POOL.index(c) + 1)
                else:
                    act.wait_ge(centred, c + 1 - sum(k < c for k in ON_POOL))
                nc.scalar.activation(sq[:, part(c), :], m.h_nodes[:, part(c), :], ACT.Square).then_inc(squared, 1)
            for c in range(PARTS):
                standard_deviation(nc, act, m.stat, part(c), std_wanted, std_ready, c + 1)
            act.wait_ge(weights_in, 16 * len(loads))

        @blk.vector
        def _(dve):
            total, mean, var, rstd = (m.stat[0:NP, i, :] for i in range(4))
            nc.vector.memset(m.ones[:, :], 1.0)
            nc.vector.memset(falls[:, 0:1], 0.0)
            for c in range(PARTS):
                x, h = m.x_nodes[:, part(c), :], m.h_nodes[:, part(c), :]
                dve.wait_ge(x_in[c], 16)
                nc.vector.tensor_reduce(total[:, part(c)], x, AX.X, ALU.add)
                dve.drain()
                nc.vector.tensor_scalar(mean[:, part(c)], total[:, part(c)], 1.0 / D, None, ALU.mult).then_inc(mean_ready, 1)
                if c not in ON_POOL:
                    dve.drain()
                    nc.vector.tensor_tensor(h, x, along(mean[:, part(c)], 2, D), ALU.subtract).then_inc(centred, 1)
            dve.wait_ge(dst_in, 32)
            nc.vector.tensor_tensor(falls[:, 1:CHUNK], dst_all[:, 0:CHUNK - 1], dst_all[:, 1:CHUNK], ALU.is_gt)
            nc.vector.tensor_tensor(falls[0:P - 1, 0:1], seam[0:P - 1, 0:1], seam[0:P - 1, 1:2], ALU.is_gt)
            for c in range(PARTS):
                dve.wait_ge(squared, c + 1)
                nc.vector.tensor_reduce(total[:, part(c)], sq[:, part(c), :], AX.X, ALU.add)
                dve.drain()
                nc.vector.tensor_scalar(var[:, part(c)], total[:, part(c)], 1.0 / D, LN_EPS, ALU.mult, ALU.add).then_inc(std_wanted, 1)
            nc.vector.tensor_reduce(fall, falls, AX.X, ALU.max).then_inc(falls_ready, 1)
            for c in range(PARTS):
                h = m.h_nodes[:, part(c), :]
                dve.wait_ge(std_ready, c + 1)
                nc.vector.reciprocal(rstd[:, part(c)], var[:, part(c)])
                dve.drain()
                nc.vector.scalar_tensor_tensor(h, h, 0.0, along(rstd[:, part(c)], 2, D), ALU.max, ALU.mult).then_inc(table_ready, 1)
            dve.wait_ge(falls_summed, 1)
            nc.vector.tensor_copy(m.unordered[:, :], ps_falls[0:1, :])
            dve.drain()


def order_edges(nc, m):
    ins = m.ins
    names = ["loaded", "cursor_cleared", "tile_ready", "spread", "cursor_in", "cursor_ready", "cursor_out", "counts_in",
             "totals_ready", "before_ready", "bases_ready", "bases_out", "base_in", "attr_in", "flipped", "record_ready",
             "record_out", "record_in", "unflipped", "attr_ready", "attr_out", "record_used", "stored"]
    sems = {n: nc.alloc_semaphore(name=f"order_{n}") for n in names}
    (loaded, cursor_cleared, tile_ready, spread, cursor_in, cursor_ready, cursor_out, counts_in, totals_ready,
     before_ready, bases_ready, bases_out, base_in, attr_in, flipped, record_ready, record_out, record_in, unflipped,
     attr_ready, attr_out, record_used, stored) = (sems[n] for n in names)

    dst, src = (m.area(k * CHUNK, CHUNK, dt=I32) for k in range(2))
    weight, rank = (m.area(k * CHUNK, CHUNK) for k in (2, 3))
    at = 4 * CHUNK
    lanes, same, later = (m.area(at + k * P, P) for k in range(3))
    at += 3 * P
    record = m.area(at, ROW)
    at += ROW
    index, place = (m.area(at + k, 1, dt=U32) for k in range(2))
    dst_col, cursor, total, after, new = (m.area(at + 2 + k, 1) for k in range(5))
    at += 8
    counts, bases, node_ones = (m.area(at + k * NJ, NJ, parts=NP) for k in range(3))
    at += 3 * NJ
    attr = m.area(at, P, parts=D)
    at += P
    zeros = m.area(at, NJ, parts=NP)
    ps_spread = m.psum[:, 0:P]
    ps_before = m.psum[0:NP, 512:513]
    ps_rows = m.psum[:, 1024:1024 + D]
    ps_attr = m.psum[0:D, 1536:1536 + P]
    cursors = m.counts[0:N, :]
    cursors_v = cursors.rearrange("(p j) o -> p (j o)", p=NP)
    records = m.edge_rows.rearrange("(p f) c -> p f c", p=P)
    inputs = ((dst, ins["dst"]), (src, ins["src"]), (weight, ins["edge_weight1"].rearrange("e o -> (e o)")))
    outputs = ((m.dst, dst), (m.src, src), (m.edge_w, weight))

    with nc.Block() as blk:

        @blk.sync
        def _(sp):
            for to, what in inputs:
                sp.dma_start(to, what.rearrange("(p f) -> p f", p=P)).then_inc(loaded, 16)
            sp.wait_ge(bases_ready, 1)
            sp.dma_start(cursors_v, zeros).then_inc(cursor_cleared, 16)
            sp.wait_ge(cursor_out, 16 * CHUNK)
            sp.dma_start(counts, cursors_v).then_inc(counts_in, 16)
            sp.wait_ge(bases_ready, 2)
            sp.dma_start(cursors_v, bases).then_inc(bases_out, 16)
            sp.dma_start(attr, ins["edge_attr"][:, 0, :]).then_inc(attr_in, 16)
            with sp.Fori(1, CHUNK) as f:
                sp.wait_ge(flipped, f)
                sp.sem_inc(m.turn, 1)
                sp.dma_start(attr, ins["edge_attr"][:, bass.ds(f, 1), :].rearrange("k f p -> k (f p)")).then_inc(attr_in, 16)
            sp.wait_ge(record_out, 16 * CHUNK)
            with sp.Fori(0, CHUNK) as f:
                sp.dma_start(record, records[:, bass.ds(f, 1), :].rearrange("p f c -> p (f c)")).then_inc(record_in, 16)
                sp.wait_ge(attr_ready, f + 1)
                sp.sem_inc(m.turn, 1)
                sp.dma_start(m.edge_attr[:, bass.ds(f, 1), :].rearrange("k f p -> k (f p)"), attr).then_inc(attr_out, 16)
                sp.wait_ge(attr_out, 16 * (f + 1))
                sp.wait_ge(record_used, f + 1)
                sp.sem_inc(m.turn, 1)
            for to, what in outputs:
                sp.dma_start(to.rearrange("(p f) -> p f", p=P), what).then_inc(stored, 16)
            sp.wait_ge(stored, 48)

        @blk.gpsimd
        def _(pool):
            rows = bass.IndirectOffsetOnAxis(index, 0)
            pool.wait_ge(cursor_cleared, 16)
            with pool.Fori(0, CHUNK) as f:
                pool.wait_ge(tile_ready, f + 1)
                pool.sem_inc(m.turn, 1)
                pool.indirect_dma_start(cursor, None, cursors, rows).then_inc(cursor_in, 16)
                pool.wait_ge(cursor_ready, f + 1)
                pool.sem_inc(m.turn, 1)
                pool.indirect_dma_start(cursors, bass.IndirectOffsetOnAxis(place, 0), new, None,
                                        bounds_check=N - 1, oob_is_err=False).then_inc(cursor_out, 16)
                pool.wait_ge(cursor_out, 16 * (f + 1))
                pool.sem_inc(m.turn, 1)
            pool.wait_ge(bases_out, 16)
            with pool.Fori(0, CHUNK) as f:
                pool.wait_ge(tile_ready, f + CHUNK + 1)
                pool.sem_inc(m.turn, 1)
                pool.indirect_dma_start(cursor, None, cursors, rows).then_inc(base_in, 16)
                pool.wait_ge(record_ready, f + 1)
                pool.sem_inc(m.turn, 1)
                pool.indirect_dma_start(m.edge_rows, bass.IndirectOffsetOnAxis(place, 0), record, None).then_inc(record_out, 16)

        @blk.tensor
        def _(pe):
            with pe.Fori(0, CHUNK) as f:
                pe.wait_ge(tile_ready, f + 1)
                nc.tensor.matmul(ps_spread, lanes, m.ident[:, :], start=True, stop=True).then_inc(spread, 1)
            pe.wait_ge(totals_ready, 1)
            nc.tensor.matmul(ps_before, m.before[0:NP, 0:NP], counts[:, NJ - 1:NJ], start=True, stop=True).then_inc(before_ready, 1)
            with pe.Fori(0, CHUNK) as f:
                pe.wait_ge(tile_ready, f + CHUNK + 1)
                pe.wait_ge(attr_in, 16 * (f + 1))
                pe.sem_inc(m.turn, 1)
                nc.tensor.transpose(ps_rows, attr, m.ident[0:D, 0:D]).then_inc(flipped, 1)
            with pe.Fori(0, CHUNK) as f:
                pe.wait_ge(record_in, 16 * (f + 1))
                pe.sem_inc(m.turn, 1)
                nc.tensor.transpose(ps_attr, record[:, 0:D], m.ident[:, :]).then_inc(unflipped, 1)

        @blk.vector
        def _(dve):
            nc.vector.memset(zeros, 0.0)
            nc.vector.memset(node_ones, 1.0)
            dve.drain()
            dve.sem_inc(bases_ready, 1)
            dve.wait_ge(loaded, 48)
            with dve.Fori(0, CHUNK) as f:
                col = dst[:, bass.ds(f, 1)]
                nc.vector.tensor_copy(index, col)
                nc.vector.tensor_copy(dst_col, col)
                nc.vector.tensor_copy(lanes, col.broadcast_to([P, P]))
                dve.drain()
                dve.sem_inc(tile_ready, 1)
                dve.wait_ge(spread, f + 1)
                nc.vector.tensor_scalar(same, ps_spread, dst_col, None, ALU.is_equal)
                dve.drain()
                nc.vector.tensor_tensor(later, same, m.before[:, :], ALU.mult)
                nc.vector.tensor_reduce(total, same, AX.X, ALU.add)
                dve.drain()
                nc.vector.tensor_reduce(after, later, AX.X, ALU.add)
                dve.wait_ge(cursor_in, 16 * (f + 1))
                nc.vector.tensor_tensor(new, cursor, total, ALU.add)
                dve.drain()
                nc.vector.scalar_tensor_tensor(rank[:, bass.ds(f, 1)], new, -1.0, after, ALU.add, ALU.subtract)
                nc.vector.tensor_scalar(after, after, 0.5, SKIP, ALU.is_gt, ALU.mult)
                dve.drain()
                nc.vector.tensor_tensor(place, after, dst_col, ALU.add)
                dve.drain()
                dve.sem_inc(cursor_ready, 1)
                dve.wait_ge(cursor_out, 16 * (f + 1))
                dve.sem_inc(m.turn, 1)
            dve.wait_ge(counts_in, 16)
            nc.vector.tensor_copy(bases, counts)
            dve.drain()
            nc.vector.tensor_tensor_scan(counts, node_ones, bases, 0.0, ALU.mult, ALU.add).then_inc(totals_ready, 1)
            dve.wait_ge(before_ready, 1)
            nc.vector.tensor_tensor(bases, counts, bases, ALU.subtract)
            dve.drain()
            nc.vector.tensor_scalar(bases, bases, ps_before, None, ALU.add).then_inc(bases_ready, 1)
            nc.vector.memset(record, 0.0)
            dve.drain()
            with dve.Fori(0, CHUNK) as f:
                nc.vector.tensor_copy(index, dst[:, bass.ds(f, 1)])
                dve.drain()
                dve.sem_inc(tile_ready, 1)
                nc.vector.tensor_copy(record[:, D:D + 1], dst[:, bass.ds(f, 1)])
                nc.vector.tensor_copy(record[:, D + 1:D + 2], src[:, bass.ds(f, 1)])
                nc.vector.tensor_copy(record[:, D + 2:D + 3], weight[:, bass.ds(f, 1)])
                nc.vector.tensor_copy(new, rank[:, bass.ds(f, 1)])
                dve.drain()
                dve.wait_ge(flipped, f + 1)
                nc.vector.tensor_copy(record[:, 0:D], ps_rows)
                dve.wait_ge(base_in, 16 * (f + 1))
                nc.vector.tensor_tensor(place, cursor, new, ALU.add)
                dve.drain()
                dve.sem_inc(record_ready, 1)
                dve.wait_ge(record_out, 16 * (f + 1))
                dve.sem_inc(m.turn, 1)
            with dve.Fori(0, CHUNK) as f:
                dve.wait_ge(record_in, 16 * (f + 1))
                nc.vector.tensor_copy(dst[:, bass.ds(f, 1)], record[:, D:D + 1])
                nc.vector.tensor_copy(src[:, bass.ds(f, 1)], record[:, D + 1:D + 2])
                nc.vector.tensor_copy(weight[:, bass.ds(f, 1)], record[:, D + 2:D + 3])
                dve.drain()
                dve.sem_inc(record_used, 1)

        @blk.scalar
        def _(act):
            with act.Fori(0, CHUNK) as f:
                act.wait_ge(unflipped, f + 1)
                act.sem_inc(m.turn, 1)
                nc.scalar.copy(attr, ps_attr).then_inc(attr_ready, 1)

    nc.clear_and_free_semaphores([sems[n] for n in names])
    nc.all_engine_barrier()


def message_edges(nc, m, ctx, unordered):
    ins = m.ins

    def sem(name):
        return ctx.enter_context(nc.semaphore(f"l0_{name}"))

    idx_in = [sem(f"idx_in{k}") for k in range(2)]
    attr_in = [sem(f"attr_in{k}") for k in range(2)]
    gathered = [sem(f"gathered{k}") for k in range(2)]
    projected = [sem(f"projected{k}") for k in range(2)]
    added = [sem(f"added{k}") for k in range(2)]
    terms_ready = sem("terms_ready")
    scanned = sem("scanned")
    rows_ready = sem("rows_ready")
    stored = [sem(f"stored{k}") for k in range(2)]
    dst_in = sem("dst_in")
    ew_in = sem("ew_in")
    zeros_ready = sem("zeros_ready")
    adst_cleared = sem("adst_cleared")
    lanes_ready = sem("lanes_ready")
    keep_ready = sem("keep_ready")
    bias_ready = sem("bias_ready")
    parts_ready = sem("parts_ready")
    products_ready = sem("products_ready")
    hot = sem("hot")
    counted = sem("counted")
    counts_closed = sem("counts_closed")
    totals_ready = sem("totals_ready")
    before_ready = sem("before_ready")
    counts_ready = sem("counts_ready")
    counts_out = sem("counts_out")
    ranges_in = sem("ranges_in")
    fix_in = sem("fix_in")

    W = G + 1
    attr = [m.area(k * G * P, G, P, parts=D + 1, of=m.stream) for k in range(2)]
    rows_g = [m.area(k * G * D, G, D) for k in range(2)]
    at = 2 * G * D
    total = m.area(at, G, D)
    at += G * D
    keeps = m.area(at, D, W)
    at += D * W
    terms = m.area(at, D, W)
    at += D * W
    sums = [m.area(at + k * D * W, D, W) for k in range(2)]
    dst_all = m.area(at, CHUNK, dt=I32)
    ew_all = m.area(at + CHUNK, CHUNK)
    at += 2 * D * W
    rows_out = [m.area(at + k * G * D, G, D) for k in range(2)]
    at += 2 * G * D
    zeros = m.area(at, 500)
    proj = m.psum[:, 0:G * D]
    ps_count = m.psum[0:HI, 3584:3584 + LO]
    ps_before = m.psum[0:HI, 3584 + LO:3584 + LO + 1]
    src_v = m.src.bitcast(U32).rearrange("(p f) -> p f", p=P)
    dst_v = m.dst.rearrange("(p f) -> p f", p=P)
    out_v = m.edge_sums.rearrange("(p f) c -> p f c", p=P)
    hi_hot, lo_hot = m.one_hot[:, :, :, 0:HI], m.one_hot[:, :, :, HI:HI + LO]

    ends_f = m.cols[:, 0, 0:2]
    wsum = m.cols[:, 2, 0:1]
    fix = m.cols[:, 1, 0:4]
    ends_b = m.chunk_tmp[:, 0:2, 0:ACC]
    last = m.chunk_tmp[0:ACC, 2, :]
    run_count = m.chunk_tmp[0:HI, 3, :]
    row_ones = m.chunk_tmp[0:HI, 4, :]
    count, start, found, empty = (m.stat[0:NP, i, :] for i in range(4))
    ps_ends = m.psum[0:ACC, 2048:2048 + 2 * P].rearrange("p (a b) -> p a b", a=2)
    ps_ext = m.psum[0:D, 2560:2560 + 2 * PROJ].rearrange("p (a b) -> p a b", a=2)
    ps_c = m.psum[:, 3072:3072 + 2 * H].rearrange("p (a b) -> p a b", a=2)
    ps_w = m.psum[:, 3072 + 2 * H:3072 + 2 * H + 1]

    with nc.Block() as blk:

        @blk.sync
        def _(sp):
            def load_idx(k, g):
                sp.dma_start(m.idx[:, k, :], src_v[:, bass.ds(g * G, G)]).then_inc(idx_in[k], 16)

            for k in range(2):
                load_idx(k, k)
            sp.dma_start(dst_all, dst_v).then_inc(dst_in, 16)
            sp.dma_start(ew_all, m.edge_w.rearrange("(p f) -> p f", p=P)).then_inc(ew_in, 16)

            def stream(edge_attr):
                def load_attr(k, g):
                    sp.dma_start(attr[k][0:D], edge_attr[:, bass.ds(g * G, G), :]).then_inc(attr_in[k], 16)

                def body(k, g, n):
                    sp.wait_ge(added[k], n + 1)
                    sp.sem_inc(m.turn, 1)
                    load_idx(k, g)
                    load_attr(k, g)

                for k in range(2):
                    load_attr(k, k)
                with sp.Fori(1, PAIRS) as i:
                    for k in range(2):
                        body(k, 2 * i + k, i)
                body(0, 2 * PAIRS, PAIRS)

            with sp.If(unordered < 1):
                stream(ins["edge_attr"])
            with sp.If(unordered > 0):
                stream(m.edge_attr)
            sp.wait_ge(adst_cleared, 16)

        @blk.gpsimd
        def _(pool):
            nc.gpsimd.iota(m.chunk_tmp[:, 5, :].bitcast(I32), pattern=[[1, LO]], base=0, channel_multiplier=0).then_inc(lanes_ready, 1)

            def body(k, g, n):
                pool.wait_ge(idx_in[k], 16 * (n + 1))
                pool.sem_inc(m.turn, 1)
                for t in range(G):
                    pool.indirect_dma_start(rows_g[k][:, t, :], None, m.relu_table,
                                            bass.IndirectOffsetOnAxis(m.idx[:, k, t:t + 1], 0)).then_inc(gathered[k], 16)

            def between():
                pool.wait_ge(counts_out, 32)
                pool.indirect_dma_start(fix[:, 0:1], None, m.counts,
                                        bass.IndirectOffsetOnAxis(m.first_dst[:, :], 0)).then_inc(fix_in, 16)

            with pool.Fori(0, PAIRS) as i:
                for k in range(2):
                    body(k, 2 * i + k, i)
            between()
            body(0, 2 * PAIRS, PAIRS)

        @blk.tensor
        def _(pe):
            pe.wait_ge(parts_ready, 1)
            nc.tensor.matmul(ps_ends[:, 0, :], ends_b[:, 0, :], m.ident[:, :], start=True, stop=True)
            nc.tensor.matmul(ps_ends[:, 1, :], ends_b[:, 1, :], m.ident[:, :], start=True, stop=True)
            for i in range(2):
                nc.tensor.matmul(ps_ext[:, i, :], m.w_att[i][:, :], m.place[i][:, :], start=True, stop=True)
                nc.tensor.matmul(ps_c[:, i, :], m.we_prod[i][:, :], m.head_mask[:, :], start=True, stop=True)
            nc.tensor.matmul(ps_w, m.ones[:, :], wsum, start=True, stop=True).then_inc(products_ready, 1)
            for slot in range(2):
                zero = m.one_hot[:, slot, 0, :]
                nc.tensor.matmul(ps_count, zero[:, 0:HI], zero[:, HI:HI + LO], start=(slot == 0), stop=False).then_inc(counted, 1)

            def project(k, g, n):
                pe.wait_ge(added[1 - k], n + 1 + k)
                pe.wait_ge(attr_in[k], 16 * (n + 1))
                for t in range(G):
                    last_one = nc.tensor.matmul(proj[:, t * D:(t + 1) * D], attr[k][:, t, :], m.w_edge[:, :],
                                                start=True, stop=True)
                last_one.then_inc(projected[k], 1)

            def count_up(slot, nth, close=False):
                pe.wait_ge(hot, nth)
                for t in range(G):
                    done = nc.tensor.matmul(ps_count, hi_hot[:, slot, t, :], lo_hot[:, slot, t, :],
                                            start=False, stop=close and t == G - 1)
                done.then_inc(counts_closed if close else counted, 1)

            def first(k, g, n):
                project(k, g, n)
                for slot in range(2):
                    count_up(slot, 2 * g + slot + 1)

            def between():
                count_up(0, GROUPS, close=True)
                pe.wait_ge(totals_ready, 1)
                nc.tensor.matmul(ps_before, m.before[0:HI, 0:HI], run_count[:, LO - 1:LO], start=True, stop=True).then_inc(before_ready, 1)

            run_halves(pe, first, between, project)

        @blk.scalar
        def _(act):
            def body(k, g, n):
                act.wait_ge(scanned, g + 1)
                nc.scalar.activation(keeps[:, :, 1:W], along(m.keep[:, bass.ds(g * G, G)], 1, D), ACT.Copy)
                act.wait_ge(added[k], n + 2)
                nc.scalar.activation(terms[:, :, 1:W], total.rearrange("p g c -> p c g"), ACT.Relu).then_inc(terms_ready, 1)
                act.wait_ge(scanned, g + 2)
                nc.scalar.activation(rows_out[k], sums[k][:, :, 1:W].rearrange("p c g -> p g c"), ACT.Copy).then_inc(rows_ready, 1)
                act.wait_ge(rows_ready, g + 1)
                act.dma_start(out_v[:, bass.ds(g * G, G), :], rows_out[k]).then_inc(stored[k], 16)

            def close(i):
                for k in range(2):
                    act.wait_ge(stored[k], 16 * (i + 1))

            def between():
                act.wait_ge(counts_ready, 1)
                act.dma_start(m.counts[1:HI * LO + 1, :].rearrange("(p j) o -> p (j o)", p=HI), run_count).then_inc(counts_out, 16)
                act.dma_start(m.counts[0:1, :], zeros[0:1, 0:1]).then_inc(counts_out, 16)
                act.wait_ge(counts_out, 32)
                act.dma_start(count, m.counts[1:N + 1, :].rearrange("(p j) o -> p (j o)", p=NP)).then_inc(ranges_in, 16)
                act.dma_start(start, m.counts[0:N, :].rearrange("(p j) o -> p (j o)", p=NP)).then_inc(ranges_in, 16)

            act.wait_ge(zeros_ready, 1)
            act.dma_start(m.adst_edges.rearrange("(p k f) h -> p k (f h)", p=P, k=25),
                          along(zeros, 1, 25)).then_inc(adst_cleared, 16)
            act.wait_ge(keep_ready, 1)
            run_halves(act, body, between, body, close)
            act.wait_ge(stored[0], 16 * (PAIRS + 1))

        @blk.vector
        def _(dve):
            for k in range(2):
                nc.vector.memset(attr[k][D:D + 1], 1.0)
            nc.vector.memset(zeros, 0.0)
            nc.vector.memset(m.one_hot[:, :, 0:2, :], 0.0)
            nc.vector.memset(keeps[:, :, 0:1], 0.0)
            dve.drain()
            dve.sem_inc(zeros_ready, 1)
            for k in range(2):
                dve.sem_inc(added[k], 1)
            dve.wait_ge(dst_in, 16)
            nc.vector.memset(m.keep[:, 0:1], 0.0)
            nc.vector.tensor_tensor(m.keep[:, 1:CHUNK], dst_all[:, 1:CHUNK], dst_all[:, 0:CHUNK - 1], ALU.is_equal)
            dve.drain()
            dve.sem_inc(keep_ready, 1)
            for k, f in enumerate((0, CHUNK - 1)):
                nc.vector.tensor_copy(m.ends[:, k:k + 1], dst_all[:, f:f + 1])
                nc.vector.tensor_copy(ends_f[:, k:k + 1], dst_all[:, f:f + 1])
            dve.wait_ge(ew_in, 16)
            nc.vector.tensor_reduce(wsum, ew_all, AX.X, ALU.add)
            dve.drain()
            for k in range(2):
                nc.vector.tensor_copy(ends_b[:, k, :], ends_f[:, k:k + 1].broadcast_to([P, ACC]))
            nc.vector.tensor_scalar(m.first_dst[:, :], ends_f[:, 0:1], 1.0, None, ALU.add)
            for i in range(2):
                for k in range(2):
                    nc.vector.tensor_scalar(m.place[i][:, ACC + k * H:ACC + (k + 1) * H], m.head_mask[:, :],
                                            m.heads[i][:, k:k + 1], None, ALU.mult)
                nc.vector.tensor_tensor(m.we_prod[i][:, :], m.heads[i][:, 2:3].broadcast_to([D, P]),
                                        m.heads[i][:, 3:4].broadcast_to([D, P]), ALU.mult)
            dve.drain()
            dve.sem_inc(parts_ready, 1)
            dve.wait_ge(lanes_ready, 1)
            nc.vector.tensor_copy(m.lanes[:, :], m.chunk_tmp[:, 5, :].bitcast(I32))
            nc.vector.tensor_single_scalar(ew_all.bitcast(I32), dst_all, LO.bit_length() - 1, ALU.logical_shift_right)
            dve.drain()
            nc.vector.tensor_copy(m.dst_hi[:, :], ew_all.bitcast(I32))
            dve.drain()
            nc.vector.tensor_single_scalar(ew_all.bitcast(I32), dst_all, LO - 1, ALU.bitwise_and)
            dve.drain()
            nc.vector.tensor_copy(m.dst_lo[:, :], ew_all.bitcast(I32))
            dve.wait_ge(products_ready, 1)
            for i in range(2):
                nc.vector.tensor_copy(m.w_ext[i][:, :], ps_ext[:, i, :])
                nc.vector.tensor_copy(m.c_edge[i][:, :], ps_c[:, i, :])
            nc.vector.tensor_scalar(m.w_mean[:, :], ps_w, 1.0 / E, None, ALU.mult)
            nc.vector.tensor_copy(last, ps_ends[:, 1, :])
            nc.vector.memset(m.cont[:, 0:1], 0.0)
            nc.vector.memset(row_ones, 1.0)
            dve.drain()
            nc.vector.tensor_tensor(m.cont[:, 1:P], ps_ends[:, 0, 1:P], last[:, 0:P - 1], ALU.is_equal)
            nc.vector.tensor_tensor(m.through[:, :], ps_ends[:, 0, :], last, ALU.is_equal)
            dve.drain()
            nc.vector.tensor_tensor(m.through[:, :], m.through[:, :], m.cont[:, :], ALU.mult)
            nc.vector.memset(sums[1][:, :, G:W], 0.0)
            dve.drain()
            dve.sem_inc(scanned, 1)

            def scan(k, g, n):
                dve.wait_ge(gathered[k], 16 * G * (n + 1))
                dve.wait_ge(projected[k], n + 1)
                nc.vector.tensor_tensor(total.rearrange("p g c -> p (g c)"), rows_g[k].rearrange("p g c -> p (g c)"),
                                        proj, ALU.add).then_inc(added[k], 1)
                dve.drain()
                nc.vector.tensor_copy(terms[:, :, 0:1], sums[1 - k][:, :, G:W])
                dve.drain()
                dve.wait_ge(terms_ready, g + 1)
                nc.vector.tensor_tensor_scan(sums[k].rearrange("p c g -> p (c g)"), keeps.rearrange("p c g -> p (c g)"),
                                             terms.rearrange("p c g -> p (c g)"), 0.0, ALU.mult, ALU.add).then_inc(scanned, 1)

            def make_hot(slot, group, nth):
                dve.wait_ge(counted, nth)
                nc.vector.tensor_tensor(hi_hot[:, slot], along(m.dst_hi[:, bass.ds(group * G, G)], 2, HI),
                                        along(m.lanes[:, 0:HI], 1, G), ALU.is_equal)
                nc.vector.tensor_tensor(lo_hot[:, slot], along(m.dst_lo[:, bass.ds(group * G, G)], 2, LO),
                                        along(m.lanes[:, :], 1, G), ALU.is_equal).then_inc(hot, 1)

            def first(k, g, n):
                for slot in range(2):
                    make_hot(slot, 2 * g + slot, 2 * g + slot + 1)
                scan(k, g, n)

            def between():
                make_hot(0, GROUPS - 1, GROUPS)
                dve.wait_ge(counts_closed, 1)
                nc.vector.tensor_tensor_scan(run_count, row_ones, ps_count, 0.0, ALU.mult, ALU.add).then_inc(totals_ready, 1)
                dve.wait_ge(before_ready, 1)
                nc.vector.tensor_scalar(run_count, run_count, ps_before, None, ALU.add).then_inc(counts_ready, 1)
                dve.wait_ge(ranges_in, 32)
                nc.vector.tensor_tensor(empty, count, start, ALU.is_equal)
                dve.drain()
                nc.vector.scalar_tensor_tensor(found, empty, SKIP, start, ALU.mult, ALU.add)
                dve.drain()
                nc.vector.tensor_copy(m.start_row[:, :], found)
                dve.drain()
                nc.vector.tensor_scalar(found, count, -1.0, 0.0, ALU.add, ALU.max)
                dve.drain()
                nc.vector.scalar_tensor_tensor(found, empty, SKIP, found, ALU.mult, ALU.add)
                dve.drain()
                nc.vector.tensor_copy(m.last_row[:, :], found)

            run_halves(dve, first, between, scan)
            dve.wait_ge(fix_in, 16)
            nc.vector.tensor_scalar(fix[:, 1:2], fix[:, 0:1], m.chunk_end[:, :], None, ALU.is_gt)
            nc.vector.tensor_scalar(fix[:, 2:3], fix[:, 0:1], m.chunk_end[:, :], -1.0, ALU.min, ALU.add)
            dve.drain()
            nc.vector.tensor_copy(m.fix_from[:, :], fix[:, 2:3])
            nc.vector.scalar_tensor_tensor(fix[:, 3:4], fix[:, 1:2], SKIP, fix[:, 2:3], ALU.mult, ALU.add)
            dve.drain()
            nc.vector.tensor_copy(m.fix_to[:, :], fix[:, 3:4])
            nc.vector.tensor_copy(m.first_dst[:, :], m.ends[:, 0:1])


class Projection:

    def __init__(self, nc, m, sem):
        at = 2 * NJ * ROW
        self.nc, self.m = nc, m
        self.flipped = [m.area(at + k * NB * NP, NB, NP, parts=D) for k in range(2)]
        self.flipped_ps = [m.psum[0:D, k * 512:k * 512 + NB * NP].rearrange("p (a b) -> p a b", a=NB) for k in range(2)]
        self.rows_ready = sem("rows_ready")
        self.flipped_ready = sem("flipped_ready")
        self.flipped_out = sem("flipped_out")
        self.product_ready = sem("product_ready")
        self.product_taken = sem("product_taken")
        self.parts = {"pe": 0, "act": 0, "dve": 0}

    def product(self, cols):
        v = self.m.psum[0:NP, 1024:3072].rearrange("p (a b) -> p a b", a=JC // 5)
        return v[:, :, 0:5 * cols].rearrange("p a (j c) -> p a j c", j=5)

    def tensor(self, pe, rows, weight, cols):
        before = self.parts["pe"] * (JC // NB)
        self.parts["pe"] += 1
        product = self.product(cols)

        def flip(b):
            for q in range(NB):
                last = self.nc.tensor.transpose(self.flipped_ps[b % 2][:, q, :], rows[:, b * NB + q, :], self.m.ident[0:NP, 0:NP])
            last.then_inc(self.flipped_ready, 1)

        def multiply(b):
            pe.wait_ge(self.flipped_out, before + b + 1)
            for q in range(NB):
                j = b * NB + q
                last = self.nc.tensor.matmul(product[:, j // 5, j % 5, :], self.flipped[b % 2][:, q, :], weight,
                                             start=True, stop=True)
            return last

        pe.wait_ge(self.rows_ready, self.parts["pe"])
        flip(0)
        if self.parts["pe"] > 1:
            pe.wait_ge(self.product_taken, self.parts["pe"] - 1)
        for b in range(1, JC // NB):
            flip(b)
            multiply(b - 1)
        multiply(JC // NB - 1).then_inc(self.product_ready, 1)

    def scalar(self, act, func):
        before = self.parts["act"] * (JC // NB)
        self.parts["act"] += 1
        for b in range(JC // NB):
            act.wait_ge(self.flipped_ready, before + b + 1)
            self.nc.scalar.activation(self.flipped[b % 2], self.flipped_ps[b % 2], func).then_inc(self.flipped_out, 1)

    def wait_product(self, eng, who):
        self.parts[who] += 1
        eng.wait_ge(self.product_ready, self.parts[who])


class AttentionTable:

    def __init__(self, nc, m, sem, layer, projection):
        self.nc, self.m, self.layer, self.projection = nc, m, layer, projection
        self.table = m.area(NJ * ROW, NJ, ROW, parts=NP)
        self.part_ready = sem("table_part_ready")
        self.out = sem("table_out")
        self.starts_out = sem("table_starts_out")
        self.first_in = sem("table_first_in")
        self.first_out = sem("table_first_out")
        self.first = m.cols[:, 7, 0:H]

    def vector(self, dve, c):
        nc, m = self.nc, self.m
        self.projection.wait_product(dve, "dve")
        product = self.projection.product(PROJ)
        table, aside, aself = self.table[:, part(c), :], m.aside[:, part(c), :], m.aself[:, part(c), :]
        nc.vector.tensor_copy(table.rearrange("p (a j) c -> p a j c", j=5), product[:, :, :, 0:ROW])
        nc.vector.tensor_copy(aside.rearrange("p (a j) c -> p a j c", j=5), product[:, :, :, ROW:PROJ]).then_inc(self.projection.product_taken, 1)
        if c == 0:
            nc.vector.tensor_scalar(m.cols[0:NP, 6, 0:H], m.c_edge[self.layer][0:NP, :], m.w_mean[0:NP, :], None, ALU.mult)
        dve.drain()
        nc.vector.memset(table[:, :, 0:ACC].rearrange("p j (h c) -> p j h c", h=H)[:, :, :, C], 1.0)
        nc.vector.tensor_tensor(aself, table[:, :, ACC:ROW], aside, ALU.add)
        dve.drain()
        dve.sem_inc(self.part_ready, 1)
        nc.vector.tensor_tensor(aself, aself, along(m.cols[0:NP, 6, 0:H], 1, JC), ALU.add)
        dve.drain()
        flat = aself.rearrange("p j h -> p (j h)")
        nc.vector.scalar_tensor_tensor(flat, flat, 0.2, flat, ALU.mult, ALU.max)

    def gpsimd(self, pool):
        m = self.m
        for j in range(NJ):
            if j % JC == 0:
                pool.wait_ge(self.part_ready, j // JC + 1)
            pool.indirect_dma_start(m.adst_edges, bass.IndirectOffsetOnAxis(m.start_row[:, j:j + 1], 0),
                                    m.aside[:, j, :], None, bounds_check=E - 1, oob_is_err=False).then_inc(self.starts_out, 16)
        pool.wait_ge(self.out, 16 * (PARTS + 1))
        pool.indirect_dma_start(self.first, None, m.adst_table,
                                bass.IndirectOffsetOnAxis(m.first_dst[:, :], 0)).then_inc(self.first_in, 16)

    def sync(self, sp):
        m = self.m
        for c in range(PARTS):
            sp.wait_ge(self.part_ready, c + 1)
            sp.dma_start(m.att_table.rearrange("(p j) c -> p j c", p=NP)[:, part(c), :], self.table[:, part(c), :]).then_inc(self.out, 16)
        sp.dma_start(m.adst_table.rearrange("(p j) c -> p j c", p=NP), m.aside[:, :, :]).then_inc(self.out, 16)
        sp.wait_ge(self.starts_out, 16 * NJ)
        sp.wait_ge(self.first_in, 16)
        sp.dma_start(m.adst_edges.rearrange("(p f) h -> p f h", p=P)[:, 0, :], self.first).then_inc(self.first_out, 16)
        sp.wait_ge(self.out, 16 * (PARTS + 1))
        sp.wait_ge(self.first_out, 16)


def message_nodes(nc, m, ctx):

    def sem(name):
        return ctx.enter_context(nc.semaphore(f"nodes_{name}"))

    fix_in = sem("fix_in")
    fix_ready = sem("fix_ready")
    fix_out = sem("fix_out")
    tail_ready = sem("tail_ready")
    tail_flipped = sem("tail_flipped")
    carry_ready = sem("carry_ready")
    carry_flipped = sem("carry_flipped")
    agg_cleared = sem("agg_cleared")
    std_wanted = sem("std_wanted")
    std_ready = sem("std_ready")
    projection = Projection(nc, m, sem)
    table = AttentionTable(nc, m, sem, 0, projection)

    W = G + 1
    last_sums = m.area(3 * G * D + 2 * D * W, D, W)
    agg = m.area(0, NJ, D, parts=NP)
    sq = m.area(0, NJ, D, parts=NP, of=m.stream)
    tail, tail_t, run_t, carry_t = (m.chunk_tmp[:, i, :] for i in range(4))
    fix = m.cols[:, 0, :]
    ps_tail = m.psum[0:D, 3072:3072 + P]
    ps_carry = m.psum[:, 3584:3584 + D]

    with nc.Block() as blk:

        @blk.gpsimd
        def _(pool):
            pool.indirect_dma_start(fix, None, m.edge_sums,
                                    bass.IndirectOffsetOnAxis(m.fix_from[:, :], 0)).then_inc(fix_in, 16)
            pool.wait_ge(fix_ready, 1)
            pool.indirect_dma_start(m.edge_sums, bass.IndirectOffsetOnAxis(m.fix_to[:, :], 0), fix, None,
                                    bounds_check=E - 1, oob_is_err=False).then_inc(fix_out, 16)
            pool.wait_ge(agg_cleared, 1)
            pool.wait_ge(fix_out, 16)
            for j in range(NJ):
                pool.indirect_dma_start(agg[:, j, :], None, m.edge_sums, bass.IndirectOffsetOnAxis(m.last_row[:, j:j + 1], 0),
                                        bounds_check=E - 1, oob_is_err=False).then_inc(m.node_in[j // JC], 16)
            table.gpsimd(pool)

        @blk.tensor
        def _(pe):
            pe.wait_ge(tail_ready, 1)
            nc.tensor.transpose(ps_tail, tail[:, 0:D], m.ident[:, :]).then_inc(tail_flipped, 1)
            pe.wait_ge(carry_ready, 1)
            nc.tensor.transpose(ps_carry, carry_t[0:D, :], m.ident[0:D, 0:D]).then_inc(carry_flipped, 1)
            for c in range(PARTS):
                projection.tensor(pe, agg[:, part(c), :], m.w_node[:, :], D)
                projection.tensor(pe, m.h_nodes[:, part(c), :], m.w_ext[0][:, :], PROJ)

        @blk.scalar
        def _(act):
            for c in range(PARTS):
                projection.scalar(act, ACT.Copy)
                standard_deviation(nc, act, m.stat, part(c), std_wanted, std_ready, c + 1)
                projection.scalar(act, ACT.Copy)

        @blk.sync
        def _(sp):
            table.sync(sp)

        @blk.vector
        def _(dve):
            nc.vector.tensor_copy(tail[:, 0:D], last_sums[:, :, G]).then_inc(tail_ready, 1)
            nc.vector.memset(agg, 0.0).then_inc(agg_cleared, 1)
            dve.wait_ge(tail_flipped, 1)
            nc.vector.tensor_copy(tail_t[0:D, :], ps_tail)
            nc.vector.memset(carry_t[0:D, 0:1], 0.0)
            dve.drain()
            nc.vector.tensor_tensor_scan(run_t[0:D, :], m.through[0:D, :], tail_t[0:D, :], 0.0, ALU.mult, ALU.add)
            dve.drain()
            nc.vector.tensor_tensor(carry_t[0:D, 1:P], run_t[0:D, 0:P - 1], m.cont[0:D, 1:P], ALU.mult)
            dve.drain()
            dve.sem_inc(carry_ready, 1)
            dve.wait_ge(carry_flipped, 1)
            dve.wait_ge(fix_in, 16)
            nc.vector.tensor_tensor(fix, fix, ps_carry, ALU.add).then_inc(fix_ready, 1)
            nc.vector.tensor_tensor(m.x_nodes[:, :, :], m.x_nodes[:, :, :], along(m.rows[:, 0, :], 1, NJ), ALU.add)
            dve.drain()
            for c in range(PARTS):
                x, h = m.x_nodes[:, part(c), :], m.h_nodes[:, part(c), :]
                dve.wait_ge(m.node_in[c], 16 * JC)
                nc.vector.tensor_tensor(agg[:, part(c), :], agg[:, part(c), :], h, ALU.add).then_inc(projection.rows_ready, 1)
                projection.wait_product(dve, "dve")
                x4 = x.rearrange("p (a j) c -> p a (j c)", j=5)
                nc.vector.tensor_tensor(x4, x4, projection.product(D).rearrange("p a j c -> p a (j c)"),
                                        ALU.add).then_inc(projection.product_taken, 1)
                dve.drain()
                layer_norm(nc, dve, x, h, sq[:, part(c), :], m.stat, part(c), std_wanted, std_ready, c + 1)
                dve.sem_inc(projection.rows_ready, 1)
                table.vector(dve, c)


def attention_edges(nc, m, ctx, layer):
    ins = m.ins

    def sem(name):
        return ctx.enter_context(nc.semaphore(f"edges{layer}_{name}"))

    idx_in = [sem(f"idx_in{k}") for k in range(2)]
    inputs_in = [sem(f"inputs_in{k}") for k in range(2)]
    gathered = [sem(f"gathered{k}") for k in range(2)]
    used = [sem(f"used{k}") for k in range(2)]
    carries_ready = sem("carries_ready")
    laid_out = sem("laid_out")
    scores_ready = sem("scores_ready")
    exps_ready = sem("exps_ready")
    scanned = sem("scanned")
    rows_ready = sem("rows_ready")
    stored = [sem(f"stored{k}") for k in range(2)]

    W = G + 1
    at = 0

    def take(*shape):
        nonlocal at
        v = m.area(at, *shape)
        for s in shape[1:]:
            shape = (shape[0] * s,)
        at += shape[0]
        return v

    sums = [take(ACC, W) for _ in range(2)]
    maxima = [take(H, W) for _ in range(2)]
    rows_g = [take(G, ROW) for _ in range(2)]
    rows_out = [take(G, ROW) for _ in range(2)]
    factors = take(ACC, W)
    terms = take(ACC, W)
    adst_in = [take(G, H) for _ in range(2)]
    weight_in = [take(G) for _ in range(2)]
    adst_s = take(H, W)
    adst = [take(H, W) for _ in range(2)]
    keep = take(H, W)
    reset = take(H, W)
    score = take(H, W)
    raw = take(H, G)
    edge_term = take(H, G)
    args = take(2, H, W)
    weights = take(H, W)
    src_v = m.src.bitcast(U32).rearrange("(p f) -> p f", p=P)
    w_v = m.edge_w.rearrange("(p f) -> p f", p=P)
    adst_v = m.adst_edges.rearrange("(p f) h -> p f h", p=P)
    out_v = m.edge_rows.rearrange("(p f) c -> p f c", p=P)

    def by_head(v):
        return v.rearrange("p (h c) g -> p h c g", h=H)

    with nc.Block() as blk:

        @blk.sync
        def _(sp):
            def body(k, g, n):
                sp.wait_ge(used[k], n + 1)
                sp.sem_inc(m.turn, 1)
                sp.dma_start(m.idx[:, k, :], src_v[:, bass.ds(g * G, G)]).then_inc(idx_in[k], 16)
                sp.dma_start(adst_in[k], adst_v[:, bass.ds(g * G, G), :]).then_inc(inputs_in[k], 16)
                sp.dma_start(weight_in[k], w_v[:, bass.ds(g * G, G)]).then_inc(inputs_in[k], 16)

            run(sp, body)

        @blk.gpsimd
        def _(pool):
            def body(k, g, n):
                pool.wait_ge(idx_in[k], 16 * (n + 1))
                pool.sem_inc(m.turn, 1)
                for t in range(G):
                    pool.indirect_dma_start(rows_g[k][:, t, :], None, m.att_table,
                                            bass.IndirectOffsetOnAxis(m.idx[:, k, t:t + 1], 0)).then_inc(gathered[k], 16)

            run(pool, body)

        @blk.scalar
        def _(act):
            def lay_out(k, g, n):
                keep_g = along(m.keep[:, bass.ds(g * G, G)], 1, H)
                nc.scalar.activation(keep[:, :, 1:W], keep_g, ACT.Copy)
                nc.scalar.activation(reset[:, :, 1:W], keep_g, ACT.Copy, bias=NEG, scale=-NEG)
                act.wait_ge(inputs_in[k], 32 * (n + 1))
                nc.scalar.activation(adst_s[:, :, 1:W], adst_in[k].rearrange("p g h -> p h g"), ACT.Copy).then_inc(laid_out, 1)

            def body(k, g, n, more=True):
                act.wait_ge(scores_ready, g + 1)
                act.wait_ge(scanned, g + 1)
                nc.scalar.activation(weights[:, :, 1:W], args[:, 1, :, 1:W], ACT.Exp)
                nc.scalar.activation(by_head(factors), along(args[:, 0, :, :], 2, HC), ACT.Exp).then_inc(exps_ready, 1)
                if more:
                    lay_out(1 - k, g + 1, n + k)
                act.wait_ge(scanned, g + 2)
                nc.scalar.activation(rows_out[k][:, :, ACC:ROW], maxima[k][:, :, 1:W].rearrange("p h g -> p g h"), ACT.Copy)
                nc.scalar.activation(rows_out[k][:, :, 0:ACC], sums[k][:, :, 1:W].rearrange("p c g -> p g c"),
                                     ACT.Copy).then_inc(rows_ready, 1)
                act.wait_ge(rows_ready, g + 1)
                act.dma_start(out_v[:, bass.ds(g * G, G), :], rows_out[k]).then_inc(stored[k], 16)

            act.wait_ge(carries_ready, 1)
            lay_out(0, 0, 0)
            with act.Fori(0, PAIRS) as i:
                for k in range(2):
                    body(k, 2 * i + k, i)
                for k in range(2):
                    act.wait_ge(stored[k], 16 * (i + 1))
            body(0, 2 * PAIRS, PAIRS, more=False)
            act.wait_ge(stored[0], 16 * (PAIRS + 1))

        @blk.vector
        def _(dve):
            nc.vector.memset(keep[:, :, 0:1], 0.0)
            nc.vector.memset(reset[:, :, 0:1], NEG)
            nc.vector.memset(args[:, 0, :, 0:1], NEG)
            nc.vector.memset(adst[1][:, :, G:W], 0.0)
            nc.vector.memset(maxima[1][:, :, G:W], NEG)
            nc.vector.memset(sums[1][:, :, G:W], 0.0)
            dve.drain()
            for k in range(2):
                dve.sem_inc(used[k], 1)
            dve.sem_inc(scanned, 1)
            dve.sem_inc(carries_ready, 1)

            def flat(v):
                return v.rearrange("p a g -> p (a g)")

            def body(k, g, n):
                nc.vector.tensor_copy(adst_s[:, :, 0:1], adst[1 - k][:, :, G:W])
                nc.vector.tensor_copy(score[:, :, 0:1], maxima[1 - k][:, :, G:W])
                dve.wait_ge(inputs_in[k], 32 * (n + 1))
                nc.vector.tensor_tensor(edge_term, along(weight_in[k], 1, H), along(m.c_edge[layer][:, :], 2, G), ALU.mult)
                dve.drain()
                dve.wait_ge(laid_out, g + 1)
                nc.vector.tensor_tensor_scan(flat(adst[k]), flat(keep), flat(adst_s), 0.0, ALU.mult, ALU.add)
                dve.drain()
                nc.vector.tensor_tensor(edge_term, edge_term, adst[k][:, :, 1:W], ALU.add)
                dve.drain()
                dve.wait_ge(gathered[k], 16 * G * (n + 1))
                nc.vector.tensor_tensor(raw, rows_g[k][:, :, ACC:ROW].rearrange("p g h -> p h g"), edge_term, ALU.add)
                dve.drain()
                nc.vector.scalar_tensor_tensor(score[:, :, 1:W], raw, 0.2, raw, ALU.mult, ALU.max)
                dve.drain()
                nc.vector.tensor_tensor_scan(flat(maxima[k]), flat(reset), flat(score), 0.0, ALU.add, ALU.max)
                dve.drain()
                nc.vector.tensor_tensor(args[:, 0, :, 1:W], maxima[k][:, :, 0:G], reset[:, :, 1:W], ALU.add)
                nc.vector.tensor_tensor(args[:, 1, :, 1:W], score[:, :, 1:W], maxima[k][:, :, 1:W], ALU.subtract)
                dve.drain()
                nc.vector.tensor_tensor(args[:, 0, :, 1:W], args[:, 0, :, 1:W], maxima[k][:, :, 1:W], ALU.subtract).then_inc(scores_ready, 1)
                nc.vector.tensor_copy(terms[:, :, 0:1], sums[1 - k][:, :, G:W])
                dve.wait_ge(exps_ready, g + 1)
                nc.vector.tensor_tensor(by_head(terms)[:, :, :, 1:W], by_head(rows_g[k][:, :, 0:ACC].rearrange("p g c -> p c g")),
                                        along(weights[:, :, 1:W], 2, HC), ALU.mult).then_inc(used[k], 1)
                dve.drain()
                nc.vector.tensor_tensor_scan(flat(sums[k]), flat(factors), flat(terms), 0.0, ALU.mult, ALU.add).then_inc(scanned, 1)
                dve.drain()

            run(dve, body)


def attention_nodes(nc, m, ctx, layer, out):
    final = layer == 1

    def sem(name):
        return ctx.enter_context(nc.semaphore(f"nodes{layer}_{name}"))

    fix_in = sem("fix_in")
    fix_ready = sem("fix_ready")
    fix_out = sem("fix_out")
    tail_ready = sem("tail_ready")
    tail_flipped = sem("tail_flipped")
    args_ready = sem("args_ready")
    exps_ready = sem("exps_ready")
    carry_ready = sem("carry_ready")
    carry_flipped = sem("carry_flipped")
    cleared = sem("cleared")
    self_in = sem("self_in")
    feats_ready = sem("feats_ready")
    centred = sem("centred")
    squared = sem("squared")
    sums_spread = sem("sums_spread")
    std_wanted = sem("std_wanted")
    std_ready = sem("std_ready")
    out_ready = sem("out_ready")
    out_stored = sem("out_stored")
    projection = None if final else Projection(nc, m, sem)
    table = None if final else AttentionTable(nc, m, sem, layer + 1, projection)

    W = G + 1
    last_sums = m.area(0, ACC, W)
    last_max = m.area(2 * ACC * W, H, W)
    rows_n = m.area(0, NJ, ROW, parts=NP)
    rows_s = m.area(NJ * ROW, NJ, ROW, parts=NP)
    sq = m.area(NJ * ROW, NJ, D, parts=NP)
    feats = m.area(0, NJ, D, parts=NP, of=m.stream)
    scal = m.area(2 * NJ * ROW, 4, NJ, H, parts=NP)
    tail, t_sum, t_max, t_run, t_args, t_args2 = (m.chunk_tmp[:, i, :] for i in range(6))
    fix = m.area(15872, ROW)
    fixw = m.cols[:, 0:4, :].rearrange("p a b -> p (a b)")[:, 0:3 * ACC].rearrange("p (a b) -> p a b", a=3)
    ps_tail = m.psum[0:ACC, 0:2 * P].rearrange("p (a b) -> p a b", a=2)
    ps_carry = m.psum[:, 512:512 + 2 * ACC].rearrange("p (a b) -> p a b", a=2)
    ps_sum = [m.psum[0:NP, 3072 + k * 512:3072 + k * 512 + NB * D] for k in range(2)]

    def heads(v, width=HC):
        return v.rearrange("p (h c) -> p h c", h=H) if len(v.shape) == 2 else v.rearrange("p j (h c) -> p j h c", h=H)

    with nc.Block() as blk:

        @blk.gpsimd
        def _(pool):
            pool.indirect_dma_start(fix, None, m.edge_rows,
                                    bass.IndirectOffsetOnAxis(m.fix_from[:, :], 0)).then_inc(fix_in, 16)
            pool.wait_ge(fix_ready, 1)
            pool.indirect_dma_start(m.edge_rows, bass.IndirectOffsetOnAxis(m.fix_to[:, :], 0), fix, None,
                                    bounds_check=E - 1, oob_is_err=False).then_inc(fix_out, 16)
            pool.wait_ge(cleared, 1)
            pool.wait_ge(fix_out, 16)
            for j in range(NJ):
                pool.indirect_dma_start(rows_n[:, j, :], None, m.edge_rows, bass.IndirectOffsetOnAxis(m.last_row[:, j:j + 1], 0),
                                        bounds_check=E - 1, oob_is_err=False).then_inc(m.node_in[j // JC], 16)
            if not final:
                table.gpsimd(pool)

        @blk.tensor
        def _(pe):
            pe.wait_ge(tail_ready, 1)
            nc.tensor.transpose(ps_tail[:, 0, :], tail[:, 0:ACC], m.ident[:, :])
            nc.tensor.transpose(ps_tail[:, 1, :], t_args[:, 0:ACC], m.ident[:, :]).then_inc(tail_flipped, 1)
            pe.wait_ge(carry_ready, 1)
            nc.tensor.transpose(ps_carry[:, 0, :], t_sum[0:ACC, :], m.ident[0:ACC, 0:ACC])
            nc.tensor.transpose(ps_carry[:, 1, :], t_max[0:ACC, :], m.ident[0:ACC, 0:ACC]).then_inc(carry_flipped, 1)

            def add_up(k, source, ready):
                for c in range(PARTS):
                    pe.wait_ge(ready, c + 1)
                    for q in range(JC // NB):
                        j = c * JC + q * NB
                        last = nc.tensor.matmul(ps_sum[k], m.ones[0:NP, 0:NP], source[:, j:j + NB, :].rearrange("p j c -> p (j c)"),
                                                start=(j == 0), stop=(j == NJ - NB))
                last.then_inc(sums_spread, 1)

            add_up(0, feats, feats_ready)
            add_up(1, sq, squared)
            if not final:
                for c in range(PARTS):
                    projection.tensor(pe, feats[:, part(c), :], m.w_ext[layer + 1][:, :], PROJ)

        @blk.scalar
        def _(act):
            act.wait_ge(args_ready, 1)
            pair = m.chunk_tmp[0:ACC, 4:6, :]
            nc.scalar.activation(pair, pair, ACT.Exp).then_inc(exps_ready, 1)
            act.wait_ge(args_ready, 2)
            nc.scalar.activation(fixw[:, 0:2, :], fixw[:, 0:2, :], ACT.Exp).then_inc(exps_ready, 1)
            for c in range(PARTS):
                act.wait_ge(args_ready, 3 + c)
                nc.scalar.activation(scal[:, 0:2, part(c), :], scal[:, 0:2, part(c), :], ACT.Exp).then_inc(exps_ready, 1)
            for c in range(PARTS):
                act.wait_ge(centred, c + 1)
                nc.scalar.activation(sq[:, part(c), :], feats[:, part(c), :], ACT.Square).then_inc(squared, 1)
            act.wait_ge(std_wanted, 1)
            nc.scalar.activation(m.cols[0:NP, 5, :], m.cols[0:NP, 5, :], ACT.Sqrt).then_inc(std_ready, 1)
            if not final:
                for c in range(PARTS):
                    projection.scalar(act, ACT.Relu)

        @blk.sync
        def _(sp):
            sp.wait_ge(tail_ready, 1)
            sp.dma_start(rows_s, m.att_table.rearrange("(p j) c -> p j c", p=NP)).then_inc(self_in, 16)
            if final:
                for c in range(PARTS):
                    sp.wait_ge(out_ready, c + 1)
                    sp.dma_start(out.rearrange("(p j) c -> p j c", p=NP)[:, part(c), :], feats[:, part(c), :]).then_inc(out_stored, 16)
                sp.wait_ge(out_stored, 16 * PARTS)
            else:
                table.sync(sp)

        @blk.vector
        def _(dve):
            nc.vector.tensor_copy(tail[:, 0:ACC], last_sums[:, :, G])
            nc.vector.tensor_copy(heads(t_args[:, 0:ACC]), along(last_max[:, :, G], 2, HC))
            dve.drain()
            dve.sem_inc(tail_ready, 1)
            dve.wait_ge(tail_flipped, 1)
            up = slice(1, P)
            down = slice(0, P - 1)
            A = slice(0, ACC)
            nc.vector.tensor_copy(t_sum[A, :], ps_tail[:, 0, :])
            nc.vector.tensor_copy(t_max[A, :], ps_tail[:, 1, :])
            nc.vector.tensor_scalar(tail[A, :], m.through[:, :], -NEG, NEG, ALU.mult, ALU.add)
            dve.drain()
            nc.vector.tensor_tensor_scan(t_run[A, :], tail[A, :], t_max[A, :], NEG, ALU.add, ALU.max)
            dve.drain()
            nc.vector.memset(t_args[A, 0:1], NEG)
            nc.vector.tensor_tensor(t_args[A, up], t_run[A, down], tail[A, up], ALU.add)
            nc.vector.tensor_tensor(t_args2[A, :], t_max[A, :], t_run[A, :], ALU.subtract)
            dve.drain()
            nc.vector.tensor_tensor(t_args[A, :], t_args[A, :], t_run[A, :], ALU.subtract)
            dve.drain()
            dve.sem_inc(args_ready, 1)
            dve.wait_ge(exps_ready, 1)
            nc.vector.tensor_tensor(t_sum[A, :], t_sum[A, :], t_args2[A, :], ALU.mult)
            nc.vector.tensor_scalar(tail[A, :], m.cont[:, :], -NEG, NEG, ALU.mult, ALU.add)
            nc.vector.memset(t_max[A, 0:1], NEG)
            dve.drain()
            nc.vector.tensor_tensor(t_max[A, up], t_run[A, down], tail[A, up], ALU.add)
            dve.drain()
            nc.vector.tensor_tensor_scan(t_run[A, :], t_args[A, :], t_sum[A, :], 0.0, ALU.mult, ALU.add)
            dve.drain()
            nc.vector.memset(t_sum[A, 0:1], 0.0)
            nc.vector.tensor_copy(t_sum[A, up], t_run[A, down])
            dve.drain()
            dve.sem_inc(carry_ready, 1)
            nc.vector.memset(rows_n[:, :, 0:ACC], 0.0)
            nc.vector.memset(rows_n[:, :, ACC:ROW], NEG).then_inc(cleared, 1)
            dve.wait_ge(carry_flipped, 1)
            dve.wait_ge(fix_in, 16)
            nc.vector.tensor_tensor(heads(fixw[:, 2, :]), along(fix[:, ACC:ROW], 2, HC), heads(ps_carry[:, 1, :]), ALU.max)
            dve.drain()
            nc.vector.tensor_tensor(heads(fixw[:, 0, :]), along(fix[:, ACC:ROW], 2, HC), heads(fixw[:, 2, :]), ALU.subtract)
            nc.vector.tensor_tensor(fixw[:, 1, :], ps_carry[:, 1, :], fixw[:, 2, :], ALU.subtract)
            dve.drain()
            dve.sem_inc(args_ready, 1)
            dve.wait_ge(exps_ready, 2)
            nc.vector.tensor_tensor(fix[:, 0:ACC], fix[:, 0:ACC], fixw[:, 0, :], ALU.mult)
            nc.vector.tensor_tensor(fixw[:, 1, :], ps_carry[:, 0, :], fixw[:, 1, :], ALU.mult)
            dve.drain()
            nc.vector.tensor_tensor(fix[:, 0:ACC], fix[:, 0:ACC], fixw[:, 1, :], ALU.add)
            nc.vector.tensor_copy(fix[:, ACC:ROW], heads(fixw[:, 2, :])[:, :, 0])
            dve.drain()
            dve.sem_inc(fix_ready, 1)
            if final:
                nc.vector.tensor_tensor(m.h_nodes[:, :, :], m.h_nodes[:, :, :], along(m.rows[:, 4, :], 1, NJ), ALU.add)
            for c in range(PARTS):
                J = part(c)
                dve.wait_ge(m.node_in[c], 16 * JC * (layer + 2))
                nc.vector.tensor_tensor(scal[:, 2, J, :], rows_n[:, J, ACC:ROW], m.aself[:, J, :], ALU.max)
                dve.drain()
                nc.vector.tensor_tensor(scal[:, 0, J, :], rows_n[:, J, ACC:ROW], scal[:, 2, J, :], ALU.subtract)
                nc.vector.tensor_tensor(scal[:, 1, J, :], m.aself[:, J, :], scal[:, 2, J, :], ALU.subtract)
                dve.drain()
                dve.sem_inc(args_ready, 1)
                dve.wait_ge(exps_ready, 3 + c)
                sums_n, sums_s = rows_n[:, J, 0:ACC], rows_s[:, J, 0:ACC]
                nc.vector.tensor_tensor(heads(sums_n), heads(sums_n), along(scal[:, 0, J, :], 3, HC), ALU.mult)
                dve.wait_ge(self_in, 16)
                nc.vector.tensor_tensor(heads(sums_s), heads(sums_s), along(scal[:, 1, J, :], 3, HC), ALU.mult)
                dve.drain()
                nc.vector.tensor_tensor(sums_n, sums_n, sums_s, ALU.add)
                dve.drain()
                nc.vector.reciprocal(scal[:, 3, J, :], heads(sums_n)[:, :, :, C])
                dve.drain()
                nc.vector.tensor_tensor(heads(feats[:, J, :]), heads(sums_n)[:, :, :, 0:C], along(scal[:, 3, J, :], 3, C), ALU.mult)
                dve.drain()
                nc.vector.tensor_tensor(feats[:, J, :], feats[:, J, :], along(m.rows[:, 1 + layer, :], 1, JC), ALU.add).then_inc(feats_ready, 1)
            mean, scale = m.cols[0:NP, 4, :], m.cols[0:NP, 5, :]

            def moment(to, k):
                nc.vector.tensor_reduce(to, ps_sum[k].rearrange("p (j c) -> p c j", j=NB), AX.X, ALU.add)
                dve.drain()

            dve.wait_ge(sums_spread, 1)
            moment(mean, 0)
            nc.vector.tensor_scalar(mean, mean, 1.0 / N, None, ALU.mult)
            dve.drain()
            for c in range(PARTS):
                nc.vector.tensor_tensor(feats[:, part(c), :], feats[:, part(c), :], along(mean, 1, JC), ALU.subtract).then_inc(centred, 1)
            dve.wait_ge(sums_spread, 2)
            moment(scale, 1)
            nc.vector.tensor_scalar(scale, scale, 1.0 / N, BN_EPS, ALU.mult, ALU.add).then_inc(std_wanted, 1)
            dve.wait_ge(std_ready, 1)
            nc.vector.reciprocal(scale, scale)
            dve.drain()
            nc.vector.tensor_tensor(scale, scale, m.rows[:, 3, :], ALU.mult)
            dve.drain()
            for c in range(PARTS):
                f = feats[:, part(c), :]
                nc.vector.tensor_tensor(f, f, along(scale, 1, JC), ALU.mult)
                dve.drain()
                if final:
                    nc.vector.tensor_tensor(f, f, m.h_nodes[:, part(c), :], ALU.add)
                    dve.drain()
                    flat = f.rearrange("p j c -> p (j c)")
                    nc.vector.scalar_tensor_tensor(flat, flat, 0.0, m.x_nodes[:, part(c), :].rearrange("p j c -> p (j c)"),
                                                   ALU.max, ALU.add).then_inc(out_ready, 1)
                else:
                    nc.vector.tensor_tensor(f, f, along(m.rows[:, 4, :], 1, JC), ALU.add).then_inc(projection.rows_ready, 1)
                    if c:
                        table.vector(dve, c - 1)
            if not final:
                table.vector(dve, PARTS - 1)


def build(nc, ins, out):
    ctx = ExitStack()
    with ctx:
        m = Memory(nc, ctx, ins)
        setup(nc, m, ctx)
        unordered = nc.values_load(m.unordered[0:1, 0:1], min_val=0, max_val=2 * P,
                                   skip_runtime_bounds_check_because="it is a sum of 2 * P zeros and ones")
        with nc.If(unordered > 0):
            order_edges(nc, m)
        message_edges(nc, m, ctx, unordered)
        message_nodes(nc, m, ctx)
        for layer in range(2):
            attention_edges(nc, m, ctx, layer)
            attention_nodes(nc, m, ctx, layer, out)


def kernel(**inputs):
    import numpy as _np
    import concourse.bacc as _bacc
    from concourse import mybir as _mybir
    from concourse.bass_utils import run_bass_kernel_spmd as _run

    arrays = {name: _np.ascontiguousarray(a) for name, a in inputs.items()}
    arrays["edge_attr"] = _np.ascontiguousarray(arrays.pop("edge_attr_64").reshape(P, CHUNK, D).transpose(2, 1, 0))
    arrays["ident"] = _np.eye(P, dtype=_np.float32)
    head = _np.arange(D) // C
    arrays["head_mask"] = (head[:, None] == _np.arange(H)[None, :]).astype(_np.float32)
    place = _np.zeros((D, ACC), _np.float32)
    place[_np.arange(D), head * HC + _np.arange(D) % C] = 1.0
    arrays["place"] = place
    arrays["before"] = _np.triu(_np.ones((P, P), _np.float32), 1)
    arrays["chunk_ends"] = (_np.arange(1, P + 1, dtype=_np.float32) * CHUNK)[:, None]

    nc = _bacc.Bacc("TRN2", target_bir_lowering=False, num_devices=1)
    ins = {}
    for name, a in arrays.items():
        ins[name] = nc.dram_tensor(f"in_{name}", a.shape, _mybir.dt.from_np(a.dtype), kind="ExternalInput").ap()
    out = nc.dram_tensor("out", (N, D), _mybir.dt.float32, kind="ExternalOutput").ap()
    build(nc, ins, out)
    r = _run(nc, [{f"in_{name}": a for name, a in arrays.items()}], core_ids=[0])
    return r.results[0]["out"]
```
